# Optimizing a Trainium2 kernel written in Bass

```python
import numpy as np
import jax
import jax.numpy as jnp

def _softmax(x, axis=-1):
    return jax.nn.softmax(x, axis=axis)

def _gelu(x):
    return jax.nn.gelu(x, approximate=True)

def _silu(x):
    return jax.nn.silu(x)

def _sigmoid(x):
    return jax.nn.sigmoid(x)

def _layernorm(x, axis=-1, eps=1e-05):
    m = jnp.mean(x, axis=axis, keepdims=True)
    v = jnp.var(x, axis=axis, keepdims=True)
    return (x - m) / jnp.sqrt(v + eps)

def _scatter_add(tgt, idx, src, axis=0):
    return tgt.at[idx].add(src)

def _segment_sum(src, seg, n):
    return jax.ops.segment_sum(src, seg, n)
kernel_name = 'mk_pixart_seq_d4_seqx_r8_c75a26'

def setup_inputs(seed: int=0):
    np.random.seed(seed)
    _w = jnp.asarray

    def _rec_inputs():
        import jax
        import jax.numpy as jnp
        _rk = jax.random.key(seed)
        x = -0.0003929 + 0.9999 * jax.random.normal(jax.random.fold_in(_rk, 1), (16, 256, 128), jnp.float32)
        _lenS = 256 - jax.random.randint(jax.random.fold_in(_rk, 7), (16,), 0, max(1, 256 // 4) + 1, jnp.int32)
        _lenS2 = 1601 - jax.random.randint(jax.random.fold_in(_rk, 8), (16,), 0, max(1, 1601 // 4) + 1, jnp.int32)
        _ctx_1024P = jax.random.normal(jax.random.fold_in(_rk, 11), (16, 16, 128), jnp.float32)
        _ctx_1024c = jax.random.dirichlet(jax.random.fold_in(_rk, 511), 0.3 * jnp.ones((16,), jnp.float32), (16, 1601))
        _ctx_1024t = jnp.einsum('bsk,bkd->bsd', _ctx_1024c, _ctx_1024P)
        _ctx_1024t = _ctx_1024t * jax.lax.rsqrt(jnp.mean(jnp.square(_ctx_1024t)) + 1e-12) * 0.953939
        ctx_1024 = -1.39393e-06 + 0.999914 * (_ctx_1024t + 0.3 * jax.random.normal(jax.random.fold_in(_rk, 611), (16, 1601, 128), jnp.float32))
        cond_1024 = -0.00920427 + 1.00102 * jax.random.normal(jax.random.fold_in(_rk, 12), (16, 128), jnp.float32)
        return (x, ctx_1024, cond_1024)
    x, ctx_1024, cond_1024 = _rec_inputs()

    def _L0_xcond_setup():
        import jax, jax.numpy as jnp
        import numpy as np
        EPS = 1e-05

        def _ada_ln(x, c, W_ss, b_ss):
            mu = jnp.mean(x, axis=-1, keepdims=True)
            var = jnp.mean((x - mu) ** 2, axis=-1, keepdims=True)
            h = (x - mu) / jnp.sqrt(var + EPS)
            ss = jax.nn.silu(c) @ W_ss + b_ss
            scale, bias = jnp.split(ss, 2, axis=-1)
            return (1.0 + scale)[:, None, :] * h + bias[:, None, :]
        key = jax.random.key(seed)
        ks = jax.random.split(key, 12)
        B, Lq, Lkv, H = (8, 256, 64, 128)
        s = 0.02
        return {'x_q': jax.random.normal(ks[0], (B, Lq, H), jnp.float32), 'x_kv': jax.random.normal(ks[1], (B, Lkv, H), jnp.float32), 't_vec': jax.random.normal(ks[2], (B, H), jnp.float32), 'Wq': jax.random.normal(ks[3], (H, H), jnp.float32) * s, 'bq': jnp.zeros((H,), jnp.float32), 'Wkv': jax.random.normal(ks[4], (H, 2 * H), jnp.float32) * s, 'bkv': jnp.zeros((2 * H,), jnp.float32), 'Wp': jax.random.normal(ks[5], (H, H), jnp.float32) * s, 'bp': jnp.zeros((H,), jnp.float32), 'Wss_q': jax.random.normal(ks[6], (H, 2 * H), jnp.float32) * s, 'bss_q': jnp.zeros((2 * H,), jnp.float32), 'Wss_kv': jax.random.normal(ks[7], (H, 2 * H), jnp.float32) * s, 'bss_kv': jnp.zeros((2 * H,), jnp.float32)}
    _L0_xcond_all = _L0_xcond_setup()
    _L0_xcond_in = {k: v for k, v in _L0_xcond_all.items() if k in ('Wq', 'bq', 'Wkv', 'bkv', 'Wp', 'bp', 'Wss_q', 'bss_q', 'Wss_kv', 'bss_kv')}
    del _L0_xcond_all

    def _L1_xcond_setup():
        import jax, jax.numpy as jnp
        import numpy as np
        D = 128
        H = 16
        HD = D // H
        MLP = 4 * D
        EPS = 1e-06
        SCALE = HD ** (-0.5)

        def _p(key, shape, s=0.02):
            return jax.random.normal(key, shape, dtype=jnp.float32) * s

        def _ln(x):
            mu = jnp.mean(x, axis=-1, keepdims=True)
            var = jnp.var(x, axis=-1, keepdims=True)
            return (x - mu) * jax.lax.rsqrt(var + EPS)

        def _heads(t):
            B, L, _ = t.shape
            return t.reshape(B, L, H, HD).transpose(0, 2, 1, 3)

        def _attend(q, k, v):
            attn = jnp.einsum('bhnd,bhsd->bhns', q, k) * SCALE
            attn = jax.nn.softmax(attn, axis=-1)
            o = jnp.einsum('bhns,bhsd->bhnd', attn, v)
            B, _, N, _ = q.shape
            return o.transpose(0, 2, 1, 3).reshape(B, N, D)
        key = jax.random.key(seed)
        ks = jax.random.split(key, 24)
        B, N, S = (4, 128, 77)
        return {'x': jax.random.normal(ks[0], (B, N, D), dtype=jnp.float32), 't_emb': jax.random.normal(ks[1], (B, D), dtype=jnp.float32), 'context': jax.random.normal(ks[2], (B, S, D), dtype=jnp.float32), 'adaln_w': _p(ks[3], (D, 6 * D)), 'adaln_b': _p(ks[4], (6 * D,)), 'qkv_w': _p(ks[5], (D, 3 * D)), 'qkv_b': _p(ks[6], (3 * D,)), 'sa_proj_w': _p(ks[7], (D, D)), 'sa_proj_b': _p(ks[8], (D,)), 'q_w': _p(ks[9], (D, D)), 'q_b': _p(ks[10], (D,)), 'kv_w': _p(ks[11], (D, 2 * D)), 'kv_b': _p(ks[12], (2 * D,)), 'ca_proj_w': _p(ks[13], (D, D)), 'ca_proj_b': _p(ks[14], (D,)), 'fc1_w': _p(ks[15], (D, MLP)), 'fc1_b': _p(ks[16], (MLP,)), 'fc2_w': _p(ks[17], (MLP, D)), 'fc2_b': _p(ks[18], (D,))}
    _L1_xcond_all = _L1_xcond_setup()
    _L1_xcond_in = {k: v for k, v in _L1_xcond_all.items() if k in ('adaln_w', 'adaln_b', 'qkv_w', 'qkv_b', 'sa_proj_w', 'sa_proj_b', 'q_w', 'q_b', 'kv_w', 'kv_b', 'ca_proj_w', 'ca_proj_b', 'fc1_w', 'fc1_b', 'fc2_w', 'fc2_b')}
    del _L1_xcond_all

    def _L2_xcond_setup():
        import jax, jax.numpy as jnp
        import numpy as np
        LN_EPS = 1e-06

        def _ln(x):
            mu = jnp.mean(x, axis=-1, keepdims=True)
            var = jnp.var(x, axis=-1, keepdims=True)
            return (x - mu) * jax.lax.rsqrt(var + LN_EPS)
        key = jax.random.key(seed)
        H, NH = (128, 16)
        B, N, S = (4, 128, 77)
        MLP = int(H * 4.0)
        ks = jax.random.split(key, 20)
        s = 1.0 / np.sqrt(H)
        return {'x': jax.random.normal(ks[0], (B, N, H), jnp.float32), 'c': jax.random.normal(ks[1], (B, H), jnp.float32), 'context': jax.random.normal(ks[2], (B, S, H), jnp.float32), 'W_mod': jax.random.normal(ks[3], (H, 6 * H), jnp.float32) * s, 'b_mod': jnp.zeros((6 * H,), jnp.float32), 'W_qkv': jax.random.normal(ks[4], (H, 3 * H), jnp.float32) * s, 'b_qkv': jnp.zeros((3 * H,), jnp.float32), 'W_proj': jax.random.normal(ks[5], (H, H), jnp.float32) * s, 'b_proj': jnp.zeros((H,), jnp.float32), 'W_qc': jax.random.normal(ks[6], (H, H), jnp.float32) * s, 'b_qc': jnp.zeros((H,), jnp.float32), 'W_kvc': jax.random.normal(ks[7], (H, 2 * H), jnp.float32) * s, 'b_kvc': jnp.zeros((2 * H,), jnp.float32), 'W_cproj': jax.random.normal(ks[8], (H, H), jnp.float32) * s, 'b_cproj': jnp.zeros((H,), jnp.float32), 'W_mlp1': jax.random.normal(ks[9], (H, MLP), jnp.float32) * s, 'b_mlp1': jnp.zeros((MLP,), jnp.float32), 'W_mlp2': jax.random.normal(ks[10], (MLP, H), jnp.float32) * (1.0 / np.sqrt(MLP)), 'b_mlp2': jnp.zeros((H,), jnp.float32)}
    _L2_xcond_all = _L2_xcond_setup()
    _L2_xcond_in = {k: v for k, v in _L2_xcond_all.items() if k in ('W_mod', 'b_mod', 'W_qkv', 'b_qkv', 'W_proj', 'b_proj', 'W_qc', 'b_qc', 'W_kvc', 'b_kvc', 'W_cproj', 'b_cproj', 'W_mlp1', 'b_mlp1', 'W_mlp2', 'b_mlp2')}
    del _L2_xcond_all

    def _L3_xcond_setup():
        import jax, jax.numpy as jnp
        import numpy as np
        H = 128
        RH = 2 * H
        E = 3
        B, T, P = (8, 256, 64)
        LN_EPS = 1e-05

        def _layer_norm(x, gamma, beta):
            mu = jnp.mean(x, axis=-1, keepdims=True)
            var = jnp.mean(jnp.square(x - mu), axis=-1, keepdims=True)
            return (x - mu) * jax.lax.rsqrt(var + LN_EPS) * gamma + beta
        key = jax.random.key(seed)
        ks = jax.random.split(key, 24)
        s = lambda fan_in: 1.0 / np.sqrt(fan_in)
        inp = {'mix_hidden_states': jax.random.normal(ks[0], (B, T, H), jnp.float32), 'global_anchor': jax.random.normal(ks[1], (B, H), jnp.float32), 'prototype_bank': jax.random.normal(ks[2], (B, P, H), jnp.float32), 'ln_gamma': jnp.ones((H,), jnp.float32), 'ln_beta': jnp.zeros((H,), jnp.float32), 'Wq': jax.random.normal(ks[3], (H, H), jnp.float32) * s(H), 'Wk': jax.random.normal(ks[4], (H, H), jnp.float32) * s(H), 'Wv': jax.random.normal(ks[5], (H, H), jnp.float32) * s(H), 'router_W': jax.random.normal(ks[6], (3 * H, E), jnp.float32) * s(3 * H), 'router_b': jnp.zeros((E,), jnp.float32), 'e_w1': jax.random.normal(ks[7], (E, 3 * H, RH), jnp.float32) * s(3 * H), 'e_b1': jnp.zeros((E, RH), jnp.float32), 'e_w2': jax.random.normal(ks[8], (E, RH, H), jnp.float32) * s(RH), 'e_b2': jnp.zeros((E, H), jnp.float32), 'gate_w1': jax.random.normal(ks[9], (3 * H, H), jnp.float32) * s(3 * H), 'gate_b1': jnp.zeros((H,), jnp.float32), 'gate_w2': jax.random.normal(ks[10], (H, H), jnp.float32) * s(H), 'gate_b2': jnp.zeros((H,), jnp.float32), 'out_w': jax.random.normal(ks[11], (H, H), jnp.float32) * s(H), 'out_b': jnp.zeros((H,), jnp.float32)}
        return inp
    _L3_xcond_all = _L3_xcond_setup()
    _L3_xcond_in = {k: v for k, v in _L3_xcond_all.items() if k in ('ln_gamma', 'ln_beta', 'Wq', 'Wk', 'Wv', 'router_W', 'router_b', 'e_w1', 'e_b1', 'e_w2', 'e_b2', 'gate_w1', 'gate_b1', 'gate_w2', 'gate_b2', 'out_w', 'out_b')}
    del _L3_xcond_all
    return {'x': x, 'ctx_1024': ctx_1024, 'cond_1024': cond_1024, 'L0_xcond_Wq': _L0_xcond_in['Wq'], 'L0_xcond_bq': _L0_xcond_in['bq'], 'L0_xcond_Wkv': _L0_xcond_in['Wkv'], 'L0_xcond_bkv': _L0_xcond_in['bkv'], 'L0_xcond_Wp': _L0_xcond_in['Wp'], 'L0_xcond_bp': _L0_xcond_in['bp'], 'L0_xcond_Wss_q': _L0_xcond_in['Wss_q'], 'L0_xcond_bss_q': _L0_xcond_in['bss_q'], 'L0_xcond_Wss_kv': _L0_xcond_in['Wss_kv'], 'L0_xcond_bss_kv': _L0_xcond_in['bss_kv'], 'L1_xcond_adaln_w': _L1_xcond_in['adaln_w'], 'L1_xcond_adaln_b': _L1_xcond_in['adaln_b'], 'L1_xcond_qkv_w': _L1_xcond_in['qkv_w'], 'L1_xcond_qkv_b': _L1_xcond_in['qkv_b'], 'L1_xcond_sa_proj_w': _L1_xcond_in['sa_proj_w'], 'L1_xcond_sa_proj_b': _L1_xcond_in['sa_proj_b'], 'L1_xcond_q_w': _L1_xcond_in['q_w'], 'L1_xcond_q_b': _L1_xcond_in['q_b'], 'L1_xcond_kv_w': _L1_xcond_in['kv_w'], 'L1_xcond_kv_b': _L1_xcond_in['kv_b'], 'L1_xcond_ca_proj_w': _L1_xcond_in['ca_proj_w'], 'L1_xcond_ca_proj_b': _L1_xcond_in['ca_proj_b'], 'L1_xcond_fc1_w': _L1_xcond_in['fc1_w'], 'L1_xcond_fc1_b': _L1_xcond_in['fc1_b'], 'L1_xcond_fc2_w': _L1_xcond_in['fc2_w'], 'L1_xcond_fc2_b': _L1_xcond_in['fc2_b'], 'L2_xcond_W_mod': _L2_xcond_in['W_mod'], 'L2_xcond_b_mod': _L2_xcond_in['b_mod'], 'L2_xcond_W_qkv': _L2_xcond_in['W_qkv'], 'L2_xcond_b_qkv': _L2_xcond_in['b_qkv'], 'L2_xcond_W_proj': _L2_xcond_in['W_proj'], 'L2_xcond_b_proj': _L2_xcond_in['b_proj'], 'L2_xcond_W_qc': _L2_xcond_in['W_qc'], 'L2_xcond_b_qc': _L2_xcond_in['b_qc'], 'L2_xcond_W_kvc': _L2_xcond_in['W_kvc'], 'L2_xcond_b_kvc': _L2_xcond_in['b_kvc'], 'L2_xcond_W_cproj': _L2_xcond_in['W_cproj'], 'L2_xcond_b_cproj': _L2_xcond_in['b_cproj'], 'L2_xcond_W_mlp1': _L2_xcond_in['W_mlp1'], 'L2_xcond_b_mlp1': _L2_xcond_in['b_mlp1'], 'L2_xcond_W_mlp2': _L2_xcond_in['W_mlp2'], 'L2_xcond_b_mlp2': _L2_xcond_in['b_mlp2'], 'L3_xcond_ln_gamma': _L3_xcond_in['ln_gamma'], 'L3_xcond_ln_beta': _L3_xcond_in['ln_beta'], 'L3_xcond_Wq': _L3_xcond_in['Wq'], 'L3_xcond_Wk': _L3_xcond_in['Wk'], 'L3_xcond_Wv': _L3_xcond_in['Wv'], 'L3_xcond_router_W': _L3_xcond_in['router_W'], 'L3_xcond_router_b': _L3_xcond_in['router_b'], 'L3_xcond_e_w1': _L3_xcond_in['e_w1'], 'L3_xcond_e_b1': _L3_xcond_in['e_b1'], 'L3_xcond_e_w2': _L3_xcond_in['e_w2'], 'L3_xcond_e_b2': _L3_xcond_in['e_b2'], 'L3_xcond_gate_w1': _L3_xcond_in['gate_w1'], 'L3_xcond_gate_b1': _L3_xcond_in['gate_b1'], 'L3_xcond_gate_w2': _L3_xcond_in['gate_w2'], 'L3_xcond_gate_b2': _L3_xcond_in['gate_b2'], 'L3_xcond_out_w': _L3_xcond_in['out_w'], 'L3_xcond_out_b': _L3_xcond_in['out_b']}

def reference(x, ctx_1024, cond_1024, L0_xcond_Wq, L0_xcond_bq, L0_xcond_Wkv, L0_xcond_bkv, L0_xcond_Wp, L0_xcond_bp, L0_xcond_Wss_q, L0_xcond_bss_q, L0_xcond_Wss_kv, L0_xcond_bss_kv, L1_xcond_adaln_w, L1_xcond_adaln_b, L1_xcond_qkv_w, L1_xcond_qkv_b, L1_xcond_sa_proj_w, L1_xcond_sa_proj_b, L1_xcond_q_w, L1_xcond_q_b, L1_xcond_kv_w, L1_xcond_kv_b, L1_xcond_ca_proj_w, L1_xcond_ca_proj_b, L1_xcond_fc1_w, L1_xcond_fc1_b, L1_xcond_fc2_w, L1_xcond_fc2_b, L2_xcond_W_mod, L2_xcond_b_mod, L2_xcond_W_qkv, L2_xcond_b_qkv, L2_xcond_W_proj, L2_xcond_b_proj, L2_xcond_W_qc, L2_xcond_b_qc, L2_xcond_W_kvc, L2_xcond_b_kvc, L2_xcond_W_cproj, L2_xcond_b_cproj, L2_xcond_W_mlp1, L2_xcond_b_mlp1, L2_xcond_W_mlp2, L2_xcond_b_mlp2, L3_xcond_ln_gamma, L3_xcond_ln_beta, L3_xcond_Wq, L3_xcond_Wk, L3_xcond_Wv, L3_xcond_router_W, L3_xcond_router_b, L3_xcond_e_w1, L3_xcond_e_b1, L3_xcond_e_w2, L3_xcond_e_b2, L3_xcond_gate_w1, L3_xcond_gate_b1, L3_xcond_gate_w2, L3_xcond_gate_b2, L3_xcond_out_w, L3_xcond_out_b):
    import jax
    import jax.numpy as jnp

    def _L0_xcond_ref(x_q, x_kv, t_vec, Wq, bq, Wkv, bkv, Wp, bp, Wss_q, bss_q, Wss_kv, bss_kv):
        import jax, jax.numpy as jnp
        import numpy as np
        EPS = 1e-05

        def _ada_ln(x, c, W_ss, b_ss):
            mu = jnp.mean(x, axis=-1, keepdims=True)
            var = jnp.mean((x - mu) ** 2, axis=-1, keepdims=True)
            h = (x - mu) / jnp.sqrt(var + EPS)
            ss = jax.nn.silu(c) @ W_ss + b_ss
            scale, bias = jnp.split(ss, 2, axis=-1)
            return (1.0 + scale)[:, None, :] * h + bias[:, None, :]
        B, Lq, H = x_q.shape
        Lkv = x_kv.shape[1]
        nh = 16
        dh = H // nh
        xq = _ada_ln(x_q, t_vec, Wss_q, bss_q)
        xkv = _ada_ln(x_kv, t_vec, Wss_kv, bss_kv)
        q = (xq @ Wq + bq).reshape(B, Lq, nh, dh)
        kv = (xkv @ Wkv + bkv).reshape(B, Lkv, 2, nh, dh)
        k = kv[:, :, 0]
        v = kv[:, :, 1]
        scores = jnp.einsum('bqhd,bkhd->bhqk', q, k) / jnp.sqrt(jnp.float32(dh))
        attn = jax.nn.softmax(scores, axis=-1)
        out = jnp.einsum('bhqk,bkhd->bqhd', attn, v).reshape(B, Lq, H)
        return x_q + (out @ Wp + bp)

    def _L1_xcond_ref(x, t_emb, context, adaln_w, adaln_b, qkv_w, qkv_b, sa_proj_w, sa_proj_b, q_w, q_b, kv_w, kv_b, ca_proj_w, ca_proj_b, fc1_w, fc1_b, fc2_w, fc2_b):
        import jax, jax.numpy as jnp
        import numpy as np
        D = 128
        H = 16
        HD = D // H
        MLP = 4 * D
        EPS = 1e-06
        SCALE = HD ** (-0.5)

        def _p(key, shape, s=0.02):
            return jax.random.normal(key, shape, dtype=jnp.float32) * s

        def _ln(x):
            mu = jnp.mean(x, axis=-1, keepdims=True)
            var = jnp.var(x, axis=-1, keepdims=True)
            return (x - mu) * jax.lax.rsqrt(var + EPS)

        def _heads(t):
            B, L, _ = t.shape
            return t.reshape(B, L, H, HD).transpose(0, 2, 1, 3)

        def _attend(q, k, v):
            attn = jnp.einsum('bhnd,bhsd->bhns', q, k) * SCALE
            attn = jax.nn.softmax(attn, axis=-1)
            o = jnp.einsum('bhns,bhsd->bhnd', attn, v)
            B, _, N, _ = q.shape
            return o.transpose(0, 2, 1, 3).reshape(B, N, D)
        B, N, _ = x.shape
        S = context.shape[1]
        mod = jax.nn.silu(t_emb) @ adaln_w + adaln_b
        sh_sa, sc_sa, g_sa, sh_ff, sc_ff, g_ff = jnp.split(mod[:, None, :], 6, axis=-1)
        xm = _ln(x) * (1.0 + sc_sa) + sh_sa
        qkv = (xm @ qkv_w + qkv_b).reshape(B, N, 3, H, HD)
        q = qkv[:, :, 0].transpose(0, 2, 1, 3)
        k = qkv[:, :, 1].transpose(0, 2, 1, 3)
        v = qkv[:, :, 2].transpose(0, 2, 1, 3)
        x_sa = _attend(q, k, v) @ sa_proj_w + sa_proj_b
        x = x + g_sa * x_sa
        xn = _ln(x)
        q = _heads(xn @ q_w + q_b)
        kv = (context @ kv_w + kv_b).reshape(B, S, 2, H, HD)
        k = kv[:, :, 0].transpose(0, 2, 1, 3)
        v = kv[:, :, 1].transpose(0, 2, 1, 3)
        x_ca = _attend(q, k, v) @ ca_proj_w + ca_proj_b
        x = x + x_ca
        xm = _ln(x) * (1.0 + sc_ff) + sh_ff
        h = jax.nn.gelu(xm @ fc1_w + fc1_b, approximate=True)
        x_ff = h @ fc2_w + fc2_b
        x = x + g_ff * x_ff
        return x

    def _L2_xcond_ref(x, c, context, W_mod, b_mod, W_qkv, b_qkv, W_proj, b_proj, W_qc, b_qc, W_kvc, b_kvc, W_cproj, b_cproj, W_mlp1, b_mlp1, W_mlp2, b_mlp2):
        import jax, jax.numpy as jnp
        import numpy as np
        LN_EPS = 1e-06

        def _ln(x):
            mu = jnp.mean(x, axis=-1, keepdims=True)
            var = jnp.var(x, axis=-1, keepdims=True)
            return (x - mu) * jax.lax.rsqrt(var + LN_EPS)
        B, N, H = x.shape
        NH = 16
        hd = H // NH
        scale = hd ** (-0.5)
        c_proj = jax.nn.silu(c) @ W_mod + b_mod
        shift_a, scale_a, gate_a, shift_m, scale_m, gate_m = jnp.split(c_proj, 6, axis=-1)

        def modulate(t, shift, sc):
            return t * (1 + sc[:, None]) + shift[:, None]
        x_norm = modulate(_ln(x), shift_a, scale_a)
        qkv = x_norm @ W_qkv + b_qkv
        q, k, v = jnp.split(qkv, 3, axis=-1)
        q = q.reshape(B, N, NH, hd).transpose(0, 2, 1, 3)
        k = k.reshape(B, N, NH, hd).transpose(0, 2, 1, 3)
        v = v.reshape(B, N, NH, hd).transpose(0, 2, 1, 3)
        attn_w = jax.nn.softmax(jnp.einsum('bhqd,bhkd->bhqk', q, k) * scale, axis=-1)
        attn_out = jnp.einsum('bhqk,bhkd->bhqd', attn_w, v)
        attn_out = attn_out.transpose(0, 2, 1, 3).reshape(B, N, H)
        attn_out = attn_out @ W_proj + b_proj
        x = x + gate_a[:, None] * attn_out
        S = context.shape[1]
        q_c = _ln(x) @ W_qc + b_qc
        kv_c = _ln(context) @ W_kvc + b_kvc
        k_c, v_c = jnp.split(kv_c, 2, axis=-1)
        q_c = q_c.reshape(B, N, NH, hd).transpose(0, 2, 1, 3)
        k_c = k_c.reshape(B, S, NH, hd).transpose(0, 2, 1, 3)
        v_c = v_c.reshape(B, S, NH, hd).transpose(0, 2, 1, 3)
        c_attn_w = jax.nn.softmax(jnp.einsum('bhqd,bhsd->bhqs', q_c, k_c) * scale, axis=-1)
        c_attn_out = jnp.einsum('bhqs,bhsd->bhqd', c_attn_w, v_c)
        c_attn_out = c_attn_out.transpose(0, 2, 1, 3).reshape(B, N, H)
        c_attn_out = c_attn_out @ W_cproj + b_cproj
        x = x + c_attn_out
        x_norm2 = modulate(_ln(x), shift_m, scale_m)
        h = jax.nn.gelu(x_norm2 @ W_mlp1 + b_mlp1)
        h = h @ W_mlp2 + b_mlp2
        x = x + gate_m[:, None] * h
        return x

    def _L3_xcond_ref(mix_hidden_states, global_anchor, prototype_bank, ln_gamma, ln_beta, Wq, Wk, Wv, router_W, router_b, e_w1, e_b1, e_w2, e_b2, gate_w1, gate_b1, gate_w2, gate_b2, out_w, out_b):
        import jax, jax.numpy as jnp
        import numpy as np
        H = 128
        RH = 2 * H
        E = 3
        B, T, P = (8, 256, 64)
        LN_EPS = 1e-05

        def _layer_norm(x, gamma, beta):
            mu = jnp.mean(x, axis=-1, keepdims=True)
            var = jnp.mean(jnp.square(x - mu), axis=-1, keepdims=True)
            return (x - mu) * jax.lax.rsqrt(var + LN_EPS) * gamma + beta
        x = mix_hidden_states
        nx = _layer_norm(x, ln_gamma, ln_beta)
        q = nx @ Wq
        k = prototype_bank @ Wk
        v = prototype_bank @ Wv
        scores = jnp.einsum('bth,bph->btp', q, k) * H ** (-0.5)
        weights = jax.nn.softmax(scores, axis=-1)
        evidence = jnp.einsum('btp,bph->bth', weights, v)
        anchor = jnp.broadcast_to(global_anchor[:, None, :], nx.shape)
        combined = jnp.concatenate([nx, evidence, anchor], axis=-1)
        router_logits = combined @ router_W + router_b
        router_probs = jax.nn.softmax(router_logits, axis=-1)
        h = jax.nn.silu(jnp.einsum('btc,ecr->bter', combined, e_w1) + e_b1)
        expert_out = jnp.einsum('bter,erh->bteh', h, e_w2) + e_b2
        routed = jnp.sum(expert_out * router_probs[..., None], axis=-2)
        g = jax.nn.sigmoid(jax.nn.silu(combined @ gate_w1 + gate_b1) @ gate_w2 + gate_b2)
        refined_delta = g * (routed @ out_w + out_b)
        return x + refined_delta
    x = _L0_xcond_ref(x, ctx_1024, cond_1024, L0_xcond_Wq, L0_xcond_bq, L0_xcond_Wkv, L0_xcond_bkv, L0_xcond_Wp, L0_xcond_bp, L0_xcond_Wss_q, L0_xcond_bss_q, L0_xcond_Wss_kv, L0_xcond_bss_kv)
    x = _L1_xcond_ref(x, cond_1024, ctx_1024, L1_xcond_adaln_w, L1_xcond_adaln_b, L1_xcond_qkv_w, L1_xcond_qkv_b, L1_xcond_sa_proj_w, L1_xcond_sa_proj_b, L1_xcond_q_w, L1_xcond_q_b, L1_xcond_kv_w, L1_xcond_kv_b, L1_xcond_ca_proj_w, L1_xcond_ca_proj_b, L1_xcond_fc1_w, L1_xcond_fc1_b, L1_xcond_fc2_w, L1_xcond_fc2_b)
    x = _L2_xcond_ref(x, cond_1024, ctx_1024, L2_xcond_W_mod, L2_xcond_b_mod, L2_xcond_W_qkv, L2_xcond_b_qkv, L2_xcond_W_proj, L2_xcond_b_proj, L2_xcond_W_qc, L2_xcond_b_qc, L2_xcond_W_kvc, L2_xcond_b_kvc, L2_xcond_W_cproj, L2_xcond_b_cproj, L2_xcond_W_mlp1, L2_xcond_b_mlp1, L2_xcond_W_mlp2, L2_xcond_b_mlp2)
    x = _L3_xcond_ref(x, cond_1024, ctx_1024, L3_xcond_ln_gamma, L3_xcond_ln_beta, L3_xcond_Wq, L3_xcond_Wk, L3_xcond_Wv, L3_xcond_router_W, L3_xcond_router_b, L3_xcond_e_w1, L3_xcond_e_b1, L3_xcond_e_w2, L3_xcond_e_b2, L3_xcond_gate_w1, L3_xcond_gate_b1, L3_xcond_gate_w2, L3_xcond_gate_b2, L3_xcond_out_w, L3_xcond_out_b)
    return x

_drawn_inputs = setup_inputs


def setup_inputs(seed=0):
    import zlib

    import numpy as np

    out = dict(_drawn_inputs(seed))
    spreads = {'L0_xcond_bq': (0.0, 2.0),
     'L0_xcond_bkv': (0.0, 0.353),
     'L0_xcond_bp': (0.0, 0.1),
     'L0_xcond_bss_q': (0.0, 2.0),
     'L0_xcond_bss_kv': (0.0, 0.8),
     'L2_xcond_b_mod': (0.0, 0.478),
     'L2_xcond_b_qkv': (0.0, 0.8),
     'L2_xcond_b_proj': (0.0, 0.8),
     'L2_xcond_b_qc': (0.0, 2.0),
     'L2_xcond_b_kvc': (0.0, 0.8),
     'L2_xcond_b_cproj': (0.0, 0.8),
     'L2_xcond_b_mlp1': (0.0, 0.8),
     'L2_xcond_b_mlp2': (0.0, 0.8),
     'L3_xcond_ln_gamma': (1.0, 0.6),
     'L3_xcond_ln_beta': (0.0, 2.0),
     'L3_xcond_router_b': (0.0, 2.0),
     'L3_xcond_e_b1': (0.0, 2.0),
     'L3_xcond_e_b2': (0.0, 2.0),
     'L3_xcond_gate_b1': (0.0, 2.0),
     'L3_xcond_gate_b2': (0.0, 2.0),
     'L3_xcond_out_b': (0.0, 0.8)}
    factors = {'L0_xcond_Wq': 8.0,
     'L0_xcond_Wss_q': 8.0,
     'L0_xcond_Wss_kv': 7.022,
     'L1_xcond_adaln_w': 7.644,
     'L1_xcond_adaln_b': 8.0,
     'L1_xcond_qkv_w': 8.0,
     'L1_xcond_qkv_b': 8.0,
     'L1_xcond_sa_proj_w': 8.0,
     'L1_xcond_sa_proj_b': 8.0,
     'L1_xcond_q_w': 64.0,
     'L1_xcond_q_b': 64.0,
     'L1_xcond_kv_b': 64.0,
     'L1_xcond_ca_proj_b': 18.176,
     'L1_xcond_fc1_w': 8.0,
     'L1_xcond_fc1_b': 8.0,
     'L1_xcond_fc2_w': 8.0,
     'L1_xcond_fc2_b': 30.845,
     'L1_xcond_kv_w': 8.0,
     'L1_xcond_ca_proj_w': 8.0,
     'L2_xcond_W_qc': 3.542,
     'L3_xcond_Wq': 8.0,
     'L3_xcond_Wk': 8.0,
     'L3_xcond_Wv': 6.279,
     'L3_xcond_router_W': 3.516,
     'L3_xcond_gate_w1': 8.0,
     'L3_xcond_gate_w2': 6.335}
    for name, (base, spread) in spreads.items():
        noise = np.random.default_rng([zlib.crc32(name.encode()), seed]).standard_normal(out[name].shape)
        drawn = base * np.exp(spread * noise) if base else spread * noise
        out[name] = jnp.asarray(drawn.astype(out[name].dtype))
    for name, factor in factors.items():
        out[name] = (out[name] * factor).astype(out[name].dtype)
    return out
```

```python
import numpy as np
import concourse.bass as bass
from concourse import mybir
from contextlib import ExitStack


B, N, D = 16, 256, 128
S = 1601
H, HD = 16, 8
G = 4
NG = H // G
R9 = 9 * HD
MR = 96
SCALE = float(HD) ** -0.5
MLPW = 4 * D
RH = 2 * D
E3 = 3
FULL = S // 128
LAST = S - FULL * 128
GELU_C, GELU_K = 0.044715, 0.7978845608028654

CHUNKS = [(0, 401), (401, 400), (801, 400), (1201, 400)]
CROSS_TILES = [128] * FULL + [LAST]
SELF_TILES = [128, 128]

M_L0 = dict(scq=0, shq=1, sck=2, shk=3)
M_L1 = dict(sh_a=4, sc_a=5, g_a=6, sh_m=7, sc_m=8, g_m=9)
M_L2 = dict(sh_a=10, sc_a=11, g_a=12, sh_m=13, sc_m=14, g_m=15)
NMOD = 16
MOD_SCALES = (0, 2, 5, 8, 11, 14)

ATT = ["a0", "s1", "c1", "s2", "c2"]
MLP = ["m1", "m2"]
NO_BANK = ("square", "norm", "stats", "ctx_scale", "ctx_norm")


PHASES = ("a0", "s1", "c1", "m1", "s2", "c2", "m2", "l3")


def _columns():
    cols, at = {}, 0
    main = [("mean", D), ("spread", D), ("ident", D), ("eps5", 1), ("eps6", 1), ("one", 1)]
    for a in ATT:
        main += [(a + "wq", D), (a + "wk", D), (a + "wv", D), (a + "wp", NG * D), (a + "bv", D),
                 (a + "bq", 1), (a + "bk", 1), (a + "bp", 1)]
    for m in MLP:
        main += [(m + "w1", MLPW), (m + "w2", MLPW), (m + "b1", 4), (m + "b2", 1)]
    for name, n in main:
        cols[name] = (at, n)
        at += n
    last, at3 = {}, 0
    for name, n in [("ew1", 18 * D), ("ew2", 6 * D), ("wq", D), ("wkT", D), ("wv", D), ("rw", 9),
                    ("gw1", 3 * D), ("gw2", D), ("ow", D), ("gamma", 1), ("beta", 1), ("rb", 3),
                    ("eb1", 6), ("eb2", 3), ("gb1", 1), ("gb2", 1), ("ob", 1)]:
        last[name] = (at3, n)
        at3 += n
    return cols, at, last, at3


COLS, NW, COLS3, NW3 = _columns()
SPLIT3 = COLS3["wq"][0]
NWM = NMOD * D + NMOD + B


class Count:

    def __init__(self, start, per, batches):
        self.start, self.per, self.batches = dict(start), per, batches

    def at(self, name, b, k):
        return self.start.get(name, 0) + b * self.per[name] + k

    def after(self):
        return {n: self.start.get(n, 0) + self.batches * p for n, p in self.per.items()}


class Phase:

    def __init__(self, name, start):
        self.name = name
        self.cross = name in ("a0", "c1", "c2")
        self.raw = name == "c1"
        self.tiles = CROSS_TILES if self.cross else SELF_TILES
        self.nt = len(self.tiles)
        self.nk = sum(self.tiles)
        self.eps = "eps5" if name == "a0" else "eps6"
        self.mod = {"a0": (0, 1), "s1": (5, 4), "s2": (11, 10)}.get(name)
        self.kvmod = (2, 3) if name == "a0" else None
        self.gate = {"s1": 6, "s2": 12}.get(name)
        self.nm = 2 * G * len(CHUNKS) if self.cross else G
        last = self.nt - 1
        per = 3 if self.cross else 3
        self.m_slot = [min(j // per, max(last - 1, 0) if self.cross else last) for j in range(self.nm)]
        self.o_slot, self.d_slot = min(1, last), min(3, last)
        if self.cross:
            prep = [(1, "mean"), (2, "square"), (3, "var"), (5, "norm"), (7, "q")]
            if not self.raw:
                prep += [(8, "stats"), (10, "ctx_scale"), (11, "ctx_norm")]
                prep += [(16 + 2 * j, "t%d" % j) for j in range(4)]
            prep += [(24 + 2 * j, "k%d" % j) for j in range(4)]
            prep += [(31 + 2 * j, "v%d" % j) for j in range(4)]
        else:
            prep = [(0, "mean"), (0, "square"), (1, "var"), (2, "norm"), (3, "q"), (5, "v0")]
        self.prep = [n for _, n in prep]
        post = [((g + 1) * self.nt + self.d_slot, "d%d" % g) for g in range(NG - 1)]
        tail = [(NG * self.nt, "d3"), (NG * self.nt, "y")]
        self.pieces = {True: sorted(prep + post, key=lambda x: x[0]), False: post}
        self.first_uses = [n for _, n in prep if n not in NO_BANK]
        self.body_uses = [n for _, n in sorted(prep + post + tail, key=lambda x: x[0]) if n not in NO_BANK]
        self.last_uses = [n for _, n in post + tail]
        self.c = Count(start, dict(
            scores_full=2 * self.nt * NG, probs_full=2 * self.nt * NG, pv_done=self.nt * NG,
            heads_copied=NG, group_done=NG, max_full=self.nm * NG, max_done=self.nm * NG,
            shift_step=2 * NG, shift_ready=NG, rows_full=2 * NG, rows_done=2 * NG, values_packed=NG,
            squared=1, rstd_done=1, unit_done=1, normed=1 if self.mod else 0,
            high_done=1 + (4 if self.cross else 1), 
            mid_done=1 + (4 if self.cross else 1), low_done=1 + (4 if self.cross else 1),
ctx_loaded=0 if not self.cross else (16 if self.raw else 32),
            stats_done=1 if self.cross and not self.raw else 0,
            stats_read=1 if self.cross and not self.raw else 0,
            ctx_log=1 if self.cross and not self.raw else 0,
            ctx_rstd=1 if self.cross and not self.raw else 0,
            ctx_offset=1 if self.cross and not self.raw else 0,
            ctx_normed=1 if self.cross and not self.raw else 0,
            split_stored=64, stream_done=1 if self.gate is not None else 0,
            **{"packed_loaded%d" % g: 64 for g in range(NG)}), B)
        self.misc0 = start.get("misc_full", 0)

    def misc(self, b, name):
        if b is None:
            return self.misc0 + self.first_uses.index(name)
        uses = self.last_uses if isinstance(b, int) and b == B - 1 else self.body_uses
        return self.misc0 + len(self.first_uses) + b * len(self.body_uses) + uses.index(name)

    def here(self, slot, more):
        return [n for s, n in self.pieces[more] if s == slot]

    def pieces_of_maximum(self, t):
        return [j for j in range(self.nm) if self.m_slot[j] == t]

    def after(self):
        out = self.c.after()
        out["misc_full"] = self.misc0 + len(self.first_uses) + (B - 1) * len(self.body_uses) + len(self.last_uses)
        return out


class MlpPhase:

    def __init__(self, name, start):
        self.name = name
        self.mod, self.gate = ((8, 7), 9) if name == "m1" else ((14, 13), 15)
        self.c = Count(start, dict(
            mlp_mean=1, mlp_centered=1, mlp_squared=1, mlp_var=1, mlp_log=1, mlp_rstd=1, mlp_unit=1, mlp_normed=1,
            mlp_hidden=4, mlp_act=4, mlp_out=1, mlp_gated=1, stream_done=1), B // 2)

    def after(self):
        return self.c.after()


class LastPhase:

    def __init__(self, start):
        self.start = dict(start)
        one = dict.fromkeys("""l_mean l_centered l_squared l_var l_log l_rstd l_unit l_normed l_q l_qf l_k l_qk
            l_shift l_shift_high l_shift_low l_rows l_rowed l_sum l_recip l_spread l_spreaded
            l_weighed l_ev l_evidence l_logits l_logit l_lmax l_lsub l_lexp l_lsum l_lrec l_prob l_pb""".split(), 1)
        nt = len(CROSS_TILES)
        one.update(l_max=2 * len(CHUNKS), l_maxed=2 * len(CHUNKS), l_scores=nt, l_probs=nt, l_pv=nt, l_acc=nt, l_pbc=2)
        self.c = Count({}, one, B)
        two = dict.fromkeys("""l_g2 l_tanh l_gate l_out l_delta l_stream""".split(), 1)
        two.update(l_hidden=7, l_silu=7, l_expert=3, l_w=3, l_routed=3)
        self.c2 = Count({}, two, B // 2)


def build(nc, xT, ctxN, ctxT, wmod, wmain, w3, outT, phases):
    f32, bf16 = mybir.dt.float32, mybir.dt.bfloat16
    ALU, ACT, AX = mybir.AluOpType, mybir.ActivationFunctionType, mybir.AxisListType
    ds = bass.ds

    start = dict(probs_full=2, pv_done=2, heads_copied=2, group_done=2, mlp_centered=1, mlp_gated=1)
    plan = []
    for name in phases:
        if name in ATT:
            ph = Phase(name, start)
            start = {**start, **ph.after()}
            plan.append(ph)
        elif name in MLP:
            plan.append(MlpPhase(name, start))
            start = {**start, **plan[-1].c.after()}
        else:
            plan.append(LastPhase(start))

    ctx = ExitStack()
    with ctx:
        def sb(name, shape, dt):
            return ctx.enter_context(nc.sbuf_tensor(name, shape, dt))

        sems = {}

        def sem(name):
            if name not in sems:
                sems[name] = ctx.enter_context(nc.semaphore(name))
            return sems[name]

        def wait(eng, name, n):
            if not (isinstance(n, int) and n <= 0):
                eng.wait_ge(sem(name), n)

        X = sb("X", [D, B * N], f32)
        W = sb("W", [128, NW], f32)
        MODT = sb("MODT", [D, NMOD * B], f32)
        KP = [sb("KP%d" % g, [128, G * S], bf16) for g in range(NG)]
        QP = [sb("QP%d" % g, [128, G * N], bf16) for g in range(NG)]
        VA = [sb("VA%d" % k, [128, len(CROSS_TILES), G, HD + 1], f32) for k in range(2)]
        VN = sb("VN", [128, len(CROSS_TILES), D], f32)
        P = [sb("P%d" % k, [128, G * N], f32) for k in range(2)]
        CN = sb("CN", [128, len(CROSS_TILES), D], f32)
        CT = sb("CT", [D, len(CROSS_TILES) * 128], f32)
        KSF = sb("KSF", [D, 3 * S + 1], bf16)
        KS = KSF[:, 0:3 * S].rearrange("p (r k) -> p r k", r=3)
        QS = sb("QS", [D, 3, N], bf16)
        REST = sb("REST", [D, N + S], f32)
        RS = [sb("RS%d" % k, [128, N], f32) for k in range(2)]
        ON = [sb("ON%d" % g, [128, N], f32) for g in range(NG)]
        REC = sb("REC", [128, N], f32)
        XU = sb("XU", [D, N], f32)
        XC = sb("XC", [D, 2 * N], f32)
        SQ = sb("SQ", [D, 2 * N], f32)
        LG = sb("LG", [D, 2 * N], f32)
        RSTD = sb("RSTD", [D, 2 * N], f32)
        XN = sb("XN", [D, 2 * N], f32)
        XM = sb("XM", [D, 2 * N], f32)
        ST = sb("ST", [128, len(CROSS_TILES), 6], f32)
        MV = sb("MV", [128, len(CROSS_TILES), 2], f32)
        CL = sb("CL", [128, len(CROSS_TILES)], f32)
        KVM = sb("KVM", [D, 2], f32)
        CR = sb("CR", [128, len(CROSS_TILES)], f32)
        CO = sb("CO", [128, len(CROSS_TILES)], f32)
        MX = sb("MX", [128, 2 * G, len(CHUNKS)], f32)
        NMF = sb("NMF", [128, 2 * G], f32)
        NMB = [sb("NMB%d" % k, [128, 2 * G, 2], bf16) for k in range(2)]
        XMA = sb("XMA", [D, B * N], f32)
        HM = [P[k][:, r * 2 * N:(r + 1) * 2 * N] for k in range(2) for r in range(2)]
        IDB = sb("IDB", [128, 128], bf16)

        bank = [ctx.enter_context(nc.psum_tensor("bank%d" % k, [128, 512], f32)) for k in range(8)]
        SC, OB, MB, MISC = bank[0:2], bank[2:4], bank[4:7], bank[7]

        scr_k = nc.dram_tensor("scr_k", [3 * HD, H, S], bf16, kind="Internal").ap()
        scr_ks = nc.dram_tensor("scr_ks", [3 * HD, H, N], bf16, kind="Internal").ap()
        scr_q = nc.dram_tensor("scr_q", [3, 3, HD, H, N], bf16, kind="Internal").ap()

        def w(name, k=0, n=None):
            at, width = COLS[name]
            return W[:, at + k:at + (width if n is None else k + n)]

        def modcol(k, b):
            return MODT[:, ds(b + k * B, 1)]

        def xcols(b, n=N):
            return X[:, ds(b * N, n)]

        def wait_apart(eng, name, n):
            eng.wait_ge(sem(name), n)
            eng.sem_inc(sem("passed"), 1)

        def stream_ready(eng, counts):
            wait(eng, "misc_free", counts.get("misc_full", 0))
            wait(eng, "stream_done", counts.get("stream_done", 0))

        WM = sb("WM", [D, NWM], f32)
        CND = sb("CND", [D, 3 * B], f32)

        W3A = KP[0][:, :].bitcast(f32)[:, 0:SPLIT3]
        W3B = KP[1][:, :].bitcast(f32)[:, 0:NW3 - SPLIT3]
        HID = [KP[2][:, :].bitcast(f32)[:, u * 2 * N:(u + 1) * 2 * N] for u in range(6)]
        T3 = KP[3][:, :].bitcast(f32)
        HID.append(T3[:, 0:2 * N])
        PB = T3[:, 2 * N:8 * N].rearrange("p (e q) -> p e q", e=E3)
        NX = T3[:, 8 * N:10 * N]
        EV = T3[:, 10 * N:12 * N]
        CTX_N = [CN, VN]
        CTX_T = [CT[:, :], KSF[:, :].bitcast(f32)]
        ACC = SQ[:, 0:N]
        ROW = sb("ROW", [2, N], bf16)
        ONE2 = sb("ONE2", [2, 128], bf16)
        EA = sb("EA", [D, 7 * B], f32)
        EAP = sb("EAP", [D, 7, 2], f32)
        RA = sb("RA", [D, B * E3], f32)
        HGB = sb("HGB", [D, 1], f32)
        RD = sb("RD", [128, 2], f32)
        LT = sb("LT", [128, 5, 2 * E3], f32)
        COND = WM[:, NMOD * (D + 1):NWM]

        def w3c(name, k=0, n=None):
            at, width = COLS3[name]
            src, at = (W3A, at) if at < SPLIT3 else (W3B, at - SPLIT3)
            return src[:, at + k:at + (width if n is None else k + n)]

        def mlp_tensor(pe, ph):
            at = ph.c.at
            stream_ready(pe, ph.c.start)
            with pe.Fori(0, B // 2) as i:
                pe.wait_ge(sem("mlp_centered"), at("mlp_centered", i, 0))
                nc.tensor.matmul(bank[0][:, :], w("mean"), X[:, ds(i * 2 * N, 2 * N)], start=True, stop=True).then_inc(
                    sem("mlp_mean"), 1)
                pe.wait_ge(sem("mlp_squared"), at("mlp_squared", i, 1))
                nc.tensor.matmul(bank[1][:, :], w("mean"), SQ[:, :], start=True, stop=True).then_inc(sem("mlp_var"), 1)
            with pe.Fori(0, B // 2) as i:
                pe.wait_ge(sem("mlp_normed"), at("mlp_normed", B // 2 - 1, 1))
                for c in range(4):
                    if c == 0:
                        pe.wait_ge(sem("mlp_gated"), at("mlp_gated", i, 0))
                    nc.tensor.matmul(bank[2 + c][:, :], w(ph.name + "w1", c * D, D), XMA[:, ds(i * 2 * N, 2 * N)],
                                     start=True, stop=True).then_inc(sem("mlp_hidden"), 1)
                for c in range(4):
                    pe.wait_ge(sem("mlp_act"), at("mlp_act", i, c + 1))
                    last = nc.tensor.matmul(bank[6][:, :], w(ph.name + "w2", c * D, D), HM[c], start=(c == 0),
                                            stop=(c == 3))
                last.then_inc(sem("mlp_out"), 1)

        def mlp_scalar(act, ph):
            at = ph.c.at
            with act.Fori(0, B // 2) as i:
                act.wait_ge(sem("mlp_centered"), at("mlp_centered", i, 1))
                nc.scalar.activation(SQ[:, :], XC[:, :], ACT.Square).then_inc(sem("mlp_squared"), 1)
                act.wait_ge(sem("mlp_var"), at("mlp_var", i, 1))
                nc.scalar.activation(LG[:, :], bank[1][:, :], ACT.Ln, bias=w("eps6")).then_inc(sem("mlp_log"), 1)
                act.wait_ge(sem("mlp_log"), at("mlp_log", i, 1))
                nc.scalar.activation(RSTD[:, :], LG[:, :], ACT.Exp, scale=-0.5).then_inc(sem("mlp_rstd"), 1)
            with act.Fori(0, B // 2) as i:
                for c in range(4):
                    act.wait_ge(sem("mlp_hidden"), at("mlp_hidden", i, c + 1))
                    nc.scalar.activation(HM[c], bank[2 + c][:, :], ACT.Gelu_apprx_tanh,
                                         bias=w(ph.name + "b1", c, 1)).then_inc(sem("mlp_act"), 1)

        def mlp_vector(dve, ph):
            at = ph.c.at
            with dve.Fori(0, B // 2) as i:
                dve.wait_ge(sem("mlp_mean"), at("mlp_mean", i, 1))
                nc.vector.tensor_tensor(XC[:, :], X[:, ds(i * 2 * N, 2 * N)], bank[0][:, :], ALU.subtract).then_inc(
                    sem("mlp_centered"), 1)
                dve.wait_ge(sem("mlp_rstd"), at("mlp_rstd", i, 1))
                nc.vector.tensor_tensor(XN[:, :], XC[:, :], RSTD[:, :], ALU.mult).then_inc(sem("mlp_unit"), 1)
                dve.wait_ge(sem("mlp_unit"), at("mlp_unit", i, 1))
                for r in range(2):
                    last = nc.vector.tensor_scalar(XMA[:, ds(i * 2 * N + r * N, N)], XN[:, r * N:(r + 1) * N],
                                                   modcol(ph.mod[0], i * 2 + r), modcol(ph.mod[1], i * 2 + r),
                                                   ALU.mult, ALU.add)
                last.then_inc(sem("mlp_normed"), 1)
                dve.wait_ge(sem("mlp_normed"), at("mlp_normed", i, 1))
            with dve.Fori(0, B // 2) as i:
                dve.wait_ge(sem("mlp_out"), at("mlp_out", i, 1))
                for r in range(2):
                    last = nc.vector.tensor_scalar(XC[:, r * N:(r + 1) * N], bank[6][:, r * N:(r + 1) * N],
                                                   w(ph.name + "b2"), modcol(ph.gate, i * 2 + r), ALU.add, ALU.mult)
                last.then_inc(sem("mlp_gated"), 1)
                dve.wait_ge(sem("mlp_gated"), at("mlp_gated", i, 1))
                nc.vector.tensor_tensor(X[:, ds(i * 2 * N, 2 * N)], X[:, ds(i * 2 * N, 2 * N)], XC[:, :],
                                        ALU.add).then_inc(sem("stream_done"), 1)
                dve.wait_ge(sem("stream_done"), at("stream_done", i, 1))

        def last_sync(sp, ph):
            at, at2 = ph.c.at, ph.c2.at

            def load(b, r):
                sp.dma_start(CTX_N[r][:, 0:FULL, :], ctxN[ds(b, 1), 0:FULL * 128, :].rearrange(
                    "o (t p) d -> (o p) t d", p=128)).then_inc(sem("l_ctx%d" % r), 16)
                sp.dma_start(CTX_N[r][0:LAST, FULL, :], ctxN[ds(b, 1), FULL * 128:S, :].rearrange(
                    "o p d -> (o p) d")).then_inc(sem("l_ctx%d" % r), 16)
                sp.dma_start(CTX_T[r][:, 0:S], ctxT[ds(b, 1)].rearrange("o d s -> (o d) s")).then_inc(
                    sem("l_ctx%d" % r), 16)

            c2 = [p for p in plan if isinstance(p, Phase)][-1]
            stream_ready(sp, c2.after())
            for r in range(2):
                load(r, r)
            with sp.Fori(0, B // 2 - 1) as i:
                for r in range(2):
                    sp.wait_ge(sem("l_weighed"), at("l_weighed", i * 2 + r, 1))
                    load(i * 2 + (2 + r), r)
                sp.wait_ge(sem("l_stream"), at2("l_stream", i, 1))
                sp.dma_start(outT[:, ds(i * 2 * N, 2 * N)], X[:, ds(i * 2 * N, 2 * N)]).then_inc(
                    sem("out_stored"), 16)
            sp.wait_ge(sem("l_stream"), B // 2)
            sp.dma_start(outT[:, B * N - 2 * N:B * N], X[:, B * N - 2 * N:B * N]).then_inc(sem("out_stored"), 16)
            sp.wait_ge(sem("out_stored"), 16 * (B // 2))

        def last_tensor(pe, ph):
            at, at2 = ph.c.at, ph.c2.at
            stream_ready(pe, ph.start)
            pe.wait_ge(sem("last_weights"), 32)
            for u in range(7):
                for_anchor = w3c("ew1", (2 * E3 + u // 2) * 2 * D + (u % 2) * D, D) if u < 6 else w3c("gw1", 2 * D, D)
                nc.tensor.matmul(bank[0][:, u * B:(u + 1) * B], for_anchor, COND, start=True, stop=True)
            for b in range(B):
                last = nc.tensor.matmul(bank[1][:, b * E3:(b + 1) * E3], COND[:, b:b + 1].to_broadcast([D, 128]),
                                        w3c("rw", 6, 3), start=True, stop=True)
            last.then_inc(sem("l_anchor"), 1)
            pe.wait_ge(sem("l_anchored"), 1)

            def attend(b, r):
                kn, kT = CTX_N[r], CTX_T[r]
                half = slice(r * N, (r + 1) * N)

                def one(name, after, out, lhsT, rhs):
                    pe.wait_ge(sem(after), at(after, b, 1))
                    nc.tensor.matmul(out, lhsT, rhs, start=True, stop=True).then_inc(sem(name), 1)

                nc.tensor.matmul(MISC[:, 0:N], w("mean"), X[:, ds(b * N, N)], start=True, stop=True).then_inc(
                    sem("l_mean"), 1)
                one("l_var", "l_squared", SC[0][:, 0:N], w("mean"), SQ[:, 0:N])
                one("l_q", "l_normed", MISC[:, 0:N], w3c("wq"), NX[:, half])
                one("l_k", "l_qf", SC[0][:, 0:N], w3c("wkT"), XM[:, 0:N])
                pe.wait_ge(sem("l_qk"), at("l_qk", b, 1))
                pe.wait_ge(sem("l_ctx%d" % r), (b - r) * 24 + 48)
                for j in range(2 * len(CHUNKS)):
                    qt, (c0, n) = j // len(CHUNKS), CHUNKS[j % len(CHUNKS)]
                    if j >= len(MB):
                        pe.wait_ge(sem("l_maxed"), at("l_maxed", b, j - len(MB) + 1))
                    nc.tensor.matmul(MB[j % 3][:, 0:n], XM[:, N + qt * 128:N + qt * 128 + 128], kT[:, c0:c0 + n],
                                     start=True, stop=True).then_inc(sem("l_max"), 1)
                pe.wait_ge(sem("l_shift_low"), at("l_shift_low", b, 1))
                for qt in range(2):
                    last = nc.tensor.matmul(MB[2][0:2, qt * 128:(qt + 1) * 128], NMB[0][:, qt, :], IDB[:, :],
                                            start=True, stop=True)
                last.then_inc(sem("l_rows"), 1)
                pe.wait_ge(sem("l_rowed"), at("l_rowed", b, 1))
                for t in range(len(CROSS_TILES) + 1):
                    if t < len(CROSS_TILES):
                        kt = CROSS_TILES[t]
                        if t >= 2:
                            pe.wait_ge(sem("l_probs"), at("l_probs", b, t - 1))
                        nc.tensor.matmul(SC[t % 2][0:kt, 0:N], kT[:, t * 128:t * 128 + kt], XM[:, N:2 * N],
                                         start=True, stop=False)
                        nc.tensor.matmul(SC[t % 2][0:kt, 0:N], ONE2[:, 0:kt], ROW[:, :], start=False,
                                         stop=True).then_inc(sem("l_scores"), 1)
                    if t:
                        kt = CROSS_TILES[t - 1]
                        pe.wait_ge(sem("l_probs"), at("l_probs", b, t))
                        nc.tensor.matmul(OB[0][:, 0:N], kn[0:kt, t - 1, :], P[(t - 1) % 2][0:kt, 0:N], start=(t == 1),
                                         stop=(t == len(CROSS_TILES))).then_inc(sem("l_pv"), 1)
                pe.wait_ge(sem("l_acc"), at("l_acc", b, len(CROSS_TILES)))
                for qt in range(2):
                    last = nc.tensor.matmul(MB[0][:, qt:qt + 1], ACC[:, qt * 128:(qt + 1) * 128], w("one"), start=True,
                                            stop=True)
                last.then_inc(sem("l_sum"), 1)
                pe.wait_ge(sem("l_recip"), at("l_recip", b, 1))
                for qt in range(2):
                    last = nc.tensor.matmul(MB[1][:, qt * 128:(qt + 1) * 128], RD[:, qt:qt + 1].to_broadcast([128, 128]),
                                            w("ident"), start=True, stop=True)
                last.then_inc(sem("l_spread"), 1)
                one("l_ev", "l_weighed", MISC[:, 0:N], w3c("wv"), XN[:, 0:N])
                pe.wait_ge(sem("l_evidence"), at("l_evidence", b, 1))
                for qt in range(2):
                    q = slice(r * N + qt * 128, r * N + (qt + 1) * 128)
                    nc.tensor.matmul(MB[2][:, qt * E3:(qt + 1) * E3], NX[:, q], w3c("rw", 0, 3), start=True, stop=False)
                    last = nc.tensor.matmul(MB[2][:, qt * E3:(qt + 1) * E3], EV[:, q], w3c("rw", 3, 3), start=False,
                                            stop=True)
                last.then_inc(sem("l_logits"), 1)
                pe.wait_ge(sem("l_prob"), at("l_prob", b, 1))
                for e in range(E3):
                    for qt in range(2):
                        c = (e % 2) * N + qt * 128
                        last = nc.tensor.matmul(SC[e // 2][:, c:c + 128],
                                                LT[:, 4, qt * E3 + e:qt * E3 + e + 1].to_broadcast([128, 128]),
                                                w("ident"), start=True, stop=True)
                last.then_inc(sem("l_pb"), 1)
                pe.wait_ge(sem("l_pbc"), at("l_pbc", b, 2))

            def experts(i):
                for u in range(7):
                    for k, src in ((0, NX), (1, EV)):
                        wt = w3c("ew1", (k * E3 + u // 2) * 2 * D + (u % 2) * D, D) if u < 6 else w3c("gw1", k * D, D)
                        last = nc.tensor.matmul(bank[u][:, :], wt, src[:, :], start=(k == 0), stop=(k == 1))
                    last.then_inc(sem("l_hidden"), 1)
                for e in range(E3):
                    pe.wait_ge(sem("l_silu"), at2("l_silu", i, 2 * e + 2))
                    for k in range(2):
                        last = nc.tensor.matmul(bank[(7, 0, 1)[e]][:, :], w3c("ew2", (2 * e + k) * D, D), HID[2 * e + k],
                                                start=(k == 0), stop=(k == 1))
                    last.then_inc(sem("l_expert"), 1)
                pe.wait_ge(sem("l_silu"), at2("l_silu", i, 7))
                nc.tensor.matmul(bank[3][:, :], w3c("gw2"), HID[6], start=True, stop=True).then_inc(sem("l_g2"), 1)
                pe.wait_ge(sem("l_routed"), at2("l_routed", i, 3))
                nc.tensor.matmul(bank[4][:, :], w3c("ow"), XN[:, :], start=True, stop=True).then_inc(sem("l_out"), 1)
                pe.wait_ge(sem("l_stream"), at2("l_stream", i, 1))

            with pe.Fori(0, B // 2) as i:
                for r in range(2):
                    attend(i * 2 + r, r)
                experts(i)

        def last_scalar(act, ph):
            at, at2 = ph.c.at, ph.c2.at

            def attend(b, r):
                half = slice(r * N, (r + 1) * N)

                def one(name, after, k, *args, **kw):
                    act.wait_ge(sem(after), at(after, b, k))
                    nc.scalar.activation(*args, **kw).then_inc(sem(name), 1)

                one("l_squared", "l_centered", 1, SQ[:, 0:N], XC[:, 0:N], ACT.Square)
                one("l_log", "l_var", 1, LG[:, 0:N], SC[0][:, 0:N], ACT.Ln, bias=w("eps5"))
                one("l_rstd", "l_log", 1, RSTD[:, 0:N], LG[:, 0:N], ACT.Exp, scale=-0.5)
                one("l_qf", "l_q", 1, XM[:, 0:N], MISC[:, 0:N], ACT.Copy)
                one("l_qk", "l_k", 1, XM[:, N:2 * N], SC[0][:, 0:N], ACT.Copy)
                one("l_rowed", "l_rows", 1, ROW[:, :], MB[2][0:2, 0:N], ACT.Copy)
                for t, kt in enumerate(CROSS_TILES):
                    if t >= 2:
                        act.wait_ge(sem("l_pv"), at("l_pv", b, t - 1))
                        act.wait_ge(sem("l_acc"), at("l_acc", b, t - 1))
                    one("l_probs", "l_scores", t + 1, P[t % 2][0:kt, 0:N], SC[t % 2][0:kt, 0:N], ACT.Exp,
                        scale=float(D) ** -0.5)
                one("l_spreaded", "l_spread", 1, REC[:, :], MB[1][:, 0:N], ACT.Copy)
                one("l_evidence", "l_ev", 1, EV[:, half], MISC[:, 0:N], ACT.Copy)
                one("l_lexp", "l_lsub", 1, LT[:, 2, :], LT[:, 1, :], ACT.Exp)
                one("l_pbc", "l_pb", 1, PB[:, 0:2, half], SC[0][:, :].rearrange("p (e q) -> p e q", e=2), ACT.Copy)
                one("l_pbc", "l_pb", 1, PB[:, 2, half], SC[1][:, 0:N], ACT.Copy)

            with act.Fori(0, B // 2) as i:
                for r in range(2):
                    attend(i * 2 + r, r)
                for u in range(7):
                    act.wait_ge(sem("l_hidden"), at2("l_hidden", i, u + 1))
                    for r in range(2):
                        last = nc.scalar.activation(HID[u][:, r * N:(r + 1) * N], bank[u][:, r * N:(r + 1) * N],
                                                    ACT.Silu, bias=EAP[:, u, r:r + 1])
                    last.then_inc(sem("l_silu"), 1)
                act.wait_ge(sem("l_g2"), at2("l_g2", i, 1))
                nc.scalar.activation(LG[:, :], bank[3][:, :], ACT.Tanh, bias=HGB[:, :], scale=0.5).then_inc(
                    sem("l_tanh"), 1)

        def last_vector(dve, ph):
            at, at2 = ph.c.at, ph.c2.at
            dve.wait_ge(sem("l_anchor"), 1)
            nc.vector.tensor_tensor(EA[:, 0:6 * B].rearrange("p (u b) -> p u b", b=B),
                                    bank[0][:, 0:6 * B].rearrange("p (u b) -> p u b", b=B),
                                    w3c("eb1").unsqueeze(2).to_broadcast([D, 6, B]), ALU.add)
            nc.vector.tensor_scalar(EA[:, 6 * B:7 * B], bank[0][:, 6 * B:7 * B], w3c("gb1"), None, ALU.add)
            nc.vector.tensor_tensor(RA[:, :].rearrange("p (b e) -> p b e", e=E3),
                                    bank[1][:, 0:B * E3].rearrange("p (b e) -> p b e", e=E3),
                                    w3c("rb").unsqueeze(1).to_broadcast([D, B, E3]), ALU.add)
            nc.vector.memset(ONE2[:, :], 1.0)
            nc.vector.tensor_scalar(HGB[:, :], w3c("gb2"), 0.5, None, ALU.mult).then_inc(sem("l_anchored"), 1)
            dve.wait_ge(sem("l_anchored"), 1)

            def attend(b, r):
                def after(name, k=1):
                    dve.wait_ge(sem(name), at(name, b, k))

                half = slice(r * N, (r + 1) * N)
                after("l_mean")
                nc.vector.tensor_tensor(XC[:, 0:N], X[:, ds(b * N, N)], MISC[:, 0:N], ALU.subtract).then_inc(
                    sem("l_centered"), 1)
                after("l_rstd")
                nc.vector.tensor_tensor(XN[:, 0:N], XC[:, 0:N], RSTD[:, 0:N], ALU.mult).then_inc(sem("l_unit"), 1)
                after("l_unit")
                nc.vector.tensor_scalar(NX[:, half], XN[:, 0:N], w3c("gamma"), w3c("beta"), ALU.mult,
                                        ALU.add).then_inc(sem("l_normed"), 1)
                for j in range(2 * len(CHUNKS)):
                    qt, c = j // len(CHUNKS), j % len(CHUNKS)
                    after("l_max", j + 1)
                    nc.vector.tensor_reduce(MX[:, qt, c:c + 1], MB[j % 3][:, 0:CHUNKS[c][1]], AX.X, ALU.max).then_inc(
                        sem("l_maxed"), 1)
                after("l_maxed", 2 * len(CHUNKS))
                nc.vector.tensor_reduce(NMF[:, 0:2], MX[:, 0:2, :], AX.X, ALU.max, negate=True).then_inc(
                    sem("l_shift"), 1)
                after("l_shift")
                nc.vector.tensor_copy(NMB[0][:, 0:2, 0], NMF[:, 0:2]).then_inc(sem("l_shift_high"), 1)
                after("l_shift_high")
                nc.vector.tensor_tensor(NMB[0][:, 0:2, 1], NMF[:, 0:2], NMB[0][:, 0:2, 0], ALU.subtract).then_inc(
                    sem("l_shift_low"), 1)
                for t, kt in enumerate(CROSS_TILES):
                    after("l_probs", t + 1)
                    if t == 0:
                        nc.vector.tensor_copy(ACC, P[0][:, 0:N]).then_inc(sem("l_acc"), 1)
                    else:
                        after("l_acc", t)
                        nc.vector.tensor_tensor(ACC[0:kt, :], ACC[0:kt, :], P[t % 2][0:kt, 0:N], ALU.add).then_inc(
                            sem("l_acc"), 1)
                after("l_sum")
                nc.vector.reciprocal(RD[:, :], MB[0][:, 0:2]).then_inc(sem("l_recip"), 1)
                after("l_spreaded")
                nc.vector.tensor_tensor(XN[:, 0:N], OB[0][:, 0:N], REC[:, :], ALU.mult).then_inc(sem("l_weighed"), 1)
                after("l_logits")
                nc.vector.tensor_tensor(LT[:, 0, :].rearrange("p (t e) -> p t e", e=E3),
                                        MB[2][:, 0:2 * E3].rearrange("p (t e) -> p t e", e=E3),
                                        RA[:, ds(b * E3, E3)].unsqueeze(1).to_broadcast([128, 2, E3]),
                                        ALU.add).then_inc(sem("l_logit"), 1)
                after("l_logit")
                nc.vector.tensor_reduce(LT[:, 3, 0:2], LT[:, 0, :].rearrange("p (t e) -> p t e", e=E3), AX.X,
                                        ALU.max).then_inc(sem("l_lmax"), 1)
                after("l_lmax")
                nc.vector.tensor_tensor(LT[:, 1, :].rearrange("p (t e) -> p t e", e=E3),
                                        LT[:, 0, :].rearrange("p (t e) -> p t e", e=E3),
                                        LT[:, 3, 0:2].unsqueeze(2).to_broadcast([128, 2, E3]),
                                        ALU.subtract).then_inc(sem("l_lsub"), 1)
                after("l_lexp")
                nc.vector.tensor_reduce(LT[:, 3, 2:4], LT[:, 2, :].rearrange("p (t e) -> p t e", e=E3), AX.X,
                                        ALU.add).then_inc(sem("l_lsum"), 1)
                after("l_lsum")
                nc.vector.reciprocal(LT[:, 3, 4:6], LT[:, 3, 2:4]).then_inc(sem("l_lrec"), 1)
                after("l_lrec")
                nc.vector.tensor_tensor(LT[:, 4, :].rearrange("p (t e) -> p t e", e=E3),
                                        LT[:, 2, :].rearrange("p (t e) -> p t e", e=E3),
                                        LT[:, 3, 4:6].unsqueeze(2).to_broadcast([128, 2, E3]),
                                        ALU.mult).then_inc(sem("l_prob"), 1)

            with dve.Fori(0, B // 2) as i:
                nc.vector.tensor_scalar(EAP[:, :, :], EA[:, :].rearrange("p (u b) -> p u b", b=B)[:, :, ds(i * 2, 2)],
                                        1.0, None, ALU.mult)
                for r in range(2):
                    attend(i * 2 + r, r)
                for e in range(E3):
                    dve.wait_ge(sem("l_expert"), at2("l_expert", i, e + 1))
                    dst = XN if e == 0 else (XC, XM)[e - 1]
                    nc.vector.scalar_tensor_tensor(out=dst[:, :], in0=bank[(7, 0, 1)[e]][:, :], scalar=w3c("eb2", e, 1),
                                                   in1=PB[:, e, :], op0=ALU.add, op1=ALU.mult).then_inc(sem("l_w"), 1)
                dve.wait_ge(sem("l_w"), at2("l_w", i, 3))
                nc.vector.tensor_tensor(XC[:, :], XC[:, :], XM[:, :], ALU.add).then_inc(sem("l_routed"), 1)
                dve.wait_ge(sem("l_routed"), at2("l_routed", i, 1))
                nc.vector.tensor_tensor(XN[:, :], XN[:, :], XC[:, :], ALU.add).then_inc(sem("l_routed"), 2)
                dve.wait_ge(sem("l_tanh"), at2("l_tanh", i, 1))
                nc.vector.tensor_scalar(RSTD[:, :], LG[:, :], 0.5, 0.5, ALU.mult, ALU.add).then_inc(sem("l_gate"), 1)
                dve.wait_ge(sem("l_gate"), at2("l_gate", i, 1))
                dve.wait_ge(sem("l_out"), at2("l_out", i, 1))
                nc.vector.scalar_tensor_tensor(out=XC[:, :], in0=bank[4][:, :], scalar=w3c("ob"), in1=RSTD[:, :],
                                               op0=ALU.add, op1=ALU.mult).then_inc(sem("l_delta"), 1)
                dve.wait_ge(sem("l_delta"), at2("l_delta", i, 1))
                nc.vector.tensor_tensor(X[:, ds(i * 2 * N, 2 * N)], X[:, ds(i * 2 * N, 2 * N)], XC[:, :],
                                        ALU.add).then_inc(sem("l_stream"), 1)
                dve.wait_ge(sem("l_stream"), at2("l_stream", i, 1))

        block = ctx.enter_context(nc.Block())

        @block.sync
        def _(sp):
            sp.dma_start(WM[:, :], wmod).then_inc(sem("wmod_loaded"), 16)
            sp.dma_start(W[:, :], wmain).then_inc(sem("weights_loaded"), 16)
            sp.dma_start(X[:, :], xT).then_inc(sem("x_loaded"), 16)

            def load_context(ph, b, uses):
                if not ph.cross:
                    return
                wait(sp, "misc_full", uses)
                if ph.raw:
                    sp.dma_start(CT[:, 0:S], ctxT[ds(b, 1)].rearrange("o d s -> (o d) s")).then_inc(sem("ctx_loaded"), 16)
                else:
                    sp.dma_start(CN[:, 0:FULL, :], ctxN[ds(b, 1), 0:FULL * 128, :].rearrange(
                        "o (p t) d -> (o p) t d", t=FULL)).then_inc(sem("ctx_loaded"), 16)
                    sp.dma_start(CN[0:LAST, FULL, :], ctxN[ds(b, 1), FULL * 128:S, :].rearrange(
                        "o p d -> (o p) d")).then_inc(sem("ctx_loaded"), 16)

            def store_split(ph, b):
                at = ph.c.at
                for g in range(NG):
                    wait(sp, "packed_loaded%d" % g, at("packed_loaded%d" % g, b, 0))
                sp.wait_ge(sem("low_done"), at("low_done", b, 1))
                for r in range(3):
                    sp.dma_start(scr_q[:, r].rearrange("a d h q -> (d h) a q"), QS[:, :, :]).then_inc(
                        sem("split_stored"), 16)
                sp.wait_ge(sem("low_done"), at("low_done", b, ph.c.per["low_done"]))
                kscr = scr_k if ph.cross else scr_ks
                sp.dma_start(kscr.rearrange("(r d) h k -> (d h) r k", r=3), KS[:, :, 0:ph.nk]).then_inc(
                    sem("split_stored"), 16)

            def load_packed(ph, b, g):
                at = ph.c.at
                if g == 0:
                    sp.wait_ge(sem("split_stored"), at("split_stored", b, 64))
                back = 2 * ph.nt * (g + 1 - NG)
                wait(sp, "scores_full", at("scores_full", b, 0 if isinstance(b, int) else back))
                kscr = scr_k if ph.cross else scr_ks
                for a in range(3):
                    sp.dma_start(KP[g][24 * a:24 * a + 24, 0:G * ph.nk],
                                 kscr[:, G * g:G * g + G, :].rearrange("r h k -> r (h k)")).then_inc(
                        sem("packed_loaded%d" % g), 16)
                sp.dma_start(QP[g][0:R9, :], scr_q[:, :, :, G * g:G * g + G, :].rearrange(
                    "a r d h q -> (a r d) (h q)")).then_inc(sem("packed_loaded%d" % g), 16)

            sp.wait_ge(sem("cleared"), 1)
            for ph in plan:
                if isinstance(ph, Phase):
                    load_context(ph, 0, ph.misc0)
                    store_split(ph, 0)
                    for g in range(NG):
                        load_packed(ph, 0, g)
                    with sp.Fori(0, B - 1) as i:
                        load_context(ph, i + 1, ph.misc0 + len(ph.first_uses) + i * len(ph.body_uses))
                        store_split(ph, i + 1)
                        for g in range(NG):
                            load_packed(ph, i + 1, g)
                    if ph.name == "c2" and "l3" in phases:
                        stream_ready(sp, ph.after())
                        sp.dma_start(W3A, w3[:, 0:SPLIT3]).then_inc(sem("last_weights"), 16)
                        sp.dma_start(W3B, w3[:, SPLIT3:NW3]).then_inc(sem("last_weights"), 16)
                elif isinstance(ph, LastPhase):
                    last_sync(sp, ph)
            if not isinstance(plan[-1], LastPhase):
                stream_ready(sp, start)
                sp.dma_start(outT, X[:, :]).then_inc(sem("out_stored"), 16)
                sp.wait_ge(sem("out_stored"), 16)

        @block.tensor
        def _(pe):
            pe.wait_ge(sem("wmod_loaded"), 16)
            pe.wait_ge(sem("cond_done"), 1)
            for k in range(NMOD):
                last = nc.tensor.matmul(MISC[:, k * B:(k + 1) * B], WM[:, k * D:(k + 1) * D], CND[:, 2 * B:3 * B],
                                        start=True, stop=True)
            last.then_inc(sem("mod_full"), 1)
            pe.wait_ge(sem("weights_loaded"), 16)
            pe.wait_ge(sem("x_loaded"), 16)
            pe.wait_ge(sem("mod_done"), 1)
            pe.wait_ge(sem("cleared"), 1)
            pe.wait_ge(sem("ones_set"), 1)

            def piece(ph, run, b, name):
                if name in NO_BANK:
                    return
                at, use = ph.c.at, ph.misc(run, name)
                wait(pe, "misc_free", use)
                if name == "mean":
                    last = nc.tensor.matmul(MISC[:, 0:N], w("mean"), xcols(b), start=True, stop=True)
                elif name == "var":
                    pe.wait_ge(sem("squared"), at("squared", b, 1))
                    last = nc.tensor.matmul(MISC[:, 0:N], w("mean"), SQ[:, 0:N], start=True, stop=True)
                elif name == "q":
                    done = "normed" if ph.mod else "unit_done"
                    pe.wait_ge(sem(done), at(done, b, 1))
                    last = nc.tensor.matmul(MISC[:, 0:N], w(ph.name + "wq"), XM[:, 0:N], start=True, stop=True)
                    if not ph.cross:
                        last = nc.tensor.matmul(MISC[:, N:2 * N], w(ph.name + "wk"), XM[:, 0:N], start=True, stop=True)
                elif name[0] == "t":
                    j = int(name[1])
                    pe.wait_ge(sem("ctx_normed"), at("ctx_normed", b, 1))
                    for k, t in enumerate(range(4 * j, min(4 * j + 4, ph.nt))):
                        last = nc.tensor.transpose(MISC[:, k * 128:(k + 1) * 128], CN[:, t, :], w("ident"))
                elif name[0] == "k":
                    c0, n = CHUNKS[int(name[1])]
                    if ph.raw:
                        pe.wait_ge(sem("ctx_loaded"), at("ctx_loaded", b, 16))
                    last = nc.tensor.matmul(MISC[:, 0:n], w(ph.name + "wk"), CT[:, c0:c0 + n], start=True, stop=True)
                elif name[0] == "v":
                    src = CT if ph.cross else XM
                    for k, t in enumerate(range(4 * int(name[1]), min(4 * int(name[1]) + 4, ph.nt))):
                        kt = ph.tiles[t]
                        last = nc.tensor.matmul(MISC[0:kt, k * D:(k + 1) * D], src[:, t * 128:t * 128 + kt],
                                                w(ph.name + "wv"), start=True, stop=True)
                elif name[0] == "d":
                    g = int(name[1])
                    pe.wait_ge(sem("heads_copied"), at("heads_copied", b, g + 1))
                    last = nc.tensor.matmul(MISC[:, 0:N], w("spread"), RS[g % 2][:, :], start=True, stop=True)
                elif name == "y":
                    pe.wait_ge(sem("group_done"), at("group_done", b, NG))
                    for g in range(NG):
                        last = nc.tensor.matmul(MISC[:, 0:N], w(ph.name + "wp", g * D, D), ON[g][:, :],
                                                start=(g == 0), stop=(g == NG - 1))
                last.then_inc(sem("misc_full"), 1)

            def scores(ph, b, g, t):
                at, kt = ph.c.at, ph.tiles[t]
                if t == 0:
                    pe.wait_ge(sem("rows_done"), at("rows_done", b, 2 * (g + 1)))
                for half in range(2):
                    pe.wait_ge(sem("probs_full"), at("probs_full", b, 2 * (g * ph.nt + t) + half - 1))
                    for k in range(2):
                        h = 2 * half + k
                        c0 = h * ph.nk + t * 128
                        last = nc.tensor.matmul(SC[half][0:kt, k * N:(k + 1) * N], KP[g][:, c0:c0 + kt],
                                                QP[g][:, h * N:(h + 1) * N], start=True, stop=True)
                    last.then_inc(sem("scores_full"), 1)

            def maximum(ph, b, g, j):
                at = ph.c.at
                if j == 0:
                    pe.wait_ge(sem("packed_loaded%d" % g), at("packed_loaded%d" % g, b, 64))
                    wait(pe, "rows_done", at("rows_done", b, 2 * g))
                if j >= len(MB):
                    pe.wait_ge(sem("max_done"), at("max_done", b, g * ph.nm + j - len(MB) + 1))
                dst = MB[j % len(MB)]
                if ph.cross:
                    r, c = j // len(CHUNKS), j % len(CHUNKS)
                    h, qt, (c0, n) = r // 2, r % 2, CHUNKS[c]
                    last = nc.tensor.matmul(dst[:, 0:n], QP[g][0:MR, h * N + qt * 128:h * N + qt * 128 + 128],
                                            KP[g][0:MR, h * ph.nk + c0:h * ph.nk + c0 + n], start=True, stop=True)
                else:
                    for qt in range(2):
                        last = nc.tensor.matmul(dst[:, qt * N:(qt + 1) * N],
                                                QP[g][0:MR, j * N + qt * 128:j * N + qt * 128 + 128],
                                                KP[g][0:MR, j * ph.nk:(j + 1) * ph.nk], start=True, stop=True)
                last.then_inc(sem("max_full"), 1)

            def shift_rows(ph, b, g):
                pe.wait_ge(sem("shift_ready"), ph.c.at("shift_ready", b, g + 1))
                for half in range(2):
                    dst = MB[(ph.nm + half) % len(MB)]
                    for r in range(4):
                        last = nc.tensor.matmul(dst[MR:MR + 2, r * 128:(r + 1) * 128], NMB[g % 2][:, 4 * half + r, :],
                                                IDB[:, :], start=True, stop=True)
                    last.then_inc(sem("rows_full"), 1)

            def head_values(ph, b, g, t):
                at, kt = ph.c.at, ph.tiles[t]
                if t == 0:
                    pe.wait_ge(sem("values_packed"), at("values_packed", b, g + 1))
                    pe.wait_ge(sem("heads_copied"), at("heads_copied", b, g - 1))
                pe.wait_ge(sem("probs_full"), at("probs_full", b, 2 * (g * ph.nt + t + 1)))
                for h in range(G):
                    last = nc.tensor.matmul(OB[g % 2][32 * h:32 * h + HD + 1, 0:N], VA[g % 2][0:kt, t, h, :],
                                            P[(g * ph.nt + t) % 2][0:kt, h * N:(h + 1) * N],
                                            start=(t == 0), stop=(t == ph.nt - 1))
                last.then_inc(sem("pv_done"), 1)

            def element(ph, b, nxt):
                before = None
                for g in range(NG):
                    ahead = (b, g + 1) if g + 1 < NG else (nxt, 0)
                    for t in range(ph.nt):
                        scores(ph, b, g, t)
                        if ahead[0] is not None:
                            for j in ph.pieces_of_maximum(t):
                                maximum(ph, *ahead, j)
                        if before:
                            head_values(ph, b, *before)
                        before = (g, t)
                        for name in ph.here(g * ph.nt + t, nxt is not None):
                            piece(ph, b, b if name[0] == "d" else nxt, name)
                        if t == ph.nt - 1 and ahead[0] is not None:
                            shift_rows(ph, *ahead)
                head_values(ph, b, *before)
                piece(ph, b, b, "d3")
                piece(ph, b, b, "y")

            for ph in plan:
                if isinstance(ph, Phase):
                    stream_ready(pe, ph.c.start)
                    for name in ph.first_uses:
                        piece(ph, None, 0, name)
                    for j in range(ph.nm):
                        maximum(ph, 0, 0, j)
                    shift_rows(ph, 0, 0)
                    with pe.Fori(0, B - 1) as i:
                        element(ph, i, i + 1)
                    element(ph, B - 1, None)
                elif isinstance(ph, MlpPhase):
                    mlp_tensor(pe, ph)
                else:
                    last_tensor(pe, ph)

        @block.scalar
        def _(act):
            act.wait_ge(sem("weights_loaded"), 16)
            nc.scalar.activation(CL[:, 0:1], w("one"), ACT.Ln).then_inc(sem("act_ready"), 1)
            act.wait_ge(sem("wmod_loaded"), 16)
            nc.scalar.activation(CND[:, 0:B], WM[:, NMOD * (D + 1):NWM], ACT.Exp, scale=-1.0).then_inc(
                sem("cond_exp"), 1)
            act.wait_ge(sem("ones_set"), 1)

            def piece(ph, run, b, name):
                at = ph.c.at
                if name == "square":
                    act.wait_ge(sem("misc_free"), ph.misc(run, "mean") + 1)
                    nc.scalar.activation(SQ[:, 0:N], XC[:, 0:N], ACT.Square).then_inc(sem("squared"), 1)
                elif name == "var":
                    act.wait_ge(sem("misc_full"), ph.misc(run, name) + 1)
                    nc.scalar.activation(LG[:, 0:N], MISC[:, 0:N], ACT.Ln, bias=w(ph.eps)).then_inc(sem("misc_free"), 1)
                    act.wait_ge(sem("misc_free"), ph.misc(run, name) + 1)
                    nc.scalar.activation(RSTD[:, 0:N], LG[:, 0:N], ACT.Exp, scale=-0.5).then_inc(sem("rstd_done"), 1)
                elif name == "ctx_scale":
                    act.wait_ge(sem("stats_done"), at("stats_done", b, 1))
                    nc.scalar.activation(CL[:, :], MV[:, :, 1], ACT.Ln, bias=w(ph.eps)).then_inc(sem("ctx_log"), 1)
                    act.wait_ge(sem("ctx_log"), at("ctx_log", b, 1))
                    nc.scalar.activation(CR[:, :], CL[:, :], ACT.Exp, scale=-0.5).then_inc(sem("ctx_rstd"), 1)
                elif name == "q":
                    act.wait_ge(sem("misc_full"), ph.misc(run, name) + 1)
                    wait(act, "split_stored", at("split_stored", b, 0))
                    nc.scalar.activation(QS[:, 0, :], MISC[:, 0:N], ACT.Identity, bias=w(ph.name + "bq")).then_inc(
                        sem("high_done"), 1)
                    if not ph.cross:
                        nc.scalar.activation(KS[:, 0, 0:N], MISC[:, N:2 * N], ACT.Identity,
                                             bias=w(ph.name + "bk")).then_inc(sem("high_done"), 1)
                elif name[0] == "k":
                    c0, n = CHUNKS[int(name[1])]
                    act.wait_ge(sem("misc_full"), ph.misc(run, name) + 1)
                    nc.scalar.activation(KS[:, 0, c0:c0 + n], MISC[:, 0:n], ACT.Identity,
                                         bias=w(ph.name + "bk")).then_inc(sem("high_done"), 1)
                elif name[0] == "t":
                    j = int(name[1])
                    n = 128 * min(4, ph.nt - 4 * j)
                    act.wait_ge(sem("misc_full"), ph.misc(run, name) + 1)
                    if ph.kvmod:
                        last = nc.scalar.activation(CT[:, 512 * j:512 * j + n], MISC[:, 0:n], ACT.Identity,
                                                    bias=KVM[:, 1:2], scale=KVM[:, 0:1])
                    else:
                        last = nc.scalar.copy(CT[:, 512 * j:512 * j + n], MISC[:, 0:n])
                    last.then_inc(sem("misc_free"), 1)

            def exponentials(ph, b, g, t):
                at, kt, v = ph.c.at, ph.tiles[t], g * ph.nt + t
                pe_done = at("pv_done", b, v - 1)
                for half in range(2):
                    act.wait_ge(sem("scores_full"), at("scores_full", b, 2 * v + half + 1))
                    if half == 0:
                        act.wait_ge(sem("pv_done"), pe_done)
                    nc.scalar.activation(P[v % 2][0:kt, half * 2 * N:(half + 1) * 2 * N], SC[half][0:kt, :], ACT.Exp,
                                         scale=SCALE).then_inc(sem("probs_full"), 1)

            def copy_heads(ph, b, g):
                at = ph.c.at
                act.wait_ge(sem("pv_done"), at("pv_done", b, (g + 1) * ph.nt))
                act.wait_ge(sem("group_done"), at("group_done", b, g - 1))
                nc.scalar.copy(RS[g % 2][:, :], OB[g % 2][:, 0:N]).then_inc(sem("heads_copied"), 1)

            def copy_rows(ph, b, g):
                for half in range(2):
                    act.wait_ge(sem("rows_full"), ph.c.at("rows_full", b, 2 * g + half + 1))
                    nc.scalar.copy(QP[g][MR:MR + 2, half * 2 * N:(half + 1) * 2 * N],
                                   MB[(ph.nm + half) % len(MB)][MR:MR + 2, :]).then_inc(sem("rows_done"), 1)

            def element(ph, b, nxt):
                for g in range(NG):
                    ahead = (b, g + 1) if g + 1 < NG else (nxt, 0)
                    for t in range(ph.nt):
                        exponentials(ph, b, g, t)
                        if g > 0 and t == ph.o_slot:
                            copy_heads(ph, b, g - 1)
                        for name in ph.here(g * ph.nt + t, nxt is not None):
                            piece(ph, b, nxt, name)
                    if ahead[0] is not None:
                        copy_rows(ph, *ahead)
                copy_heads(ph, b, NG - 1)

            for ph in plan:
                if isinstance(ph, Phase):
                    for name in ph.prep:
                        piece(ph, None, 0, name)
                    copy_rows(ph, 0, 0)
                    with act.Fori(0, B - 1) as i:
                        element(ph, i, i + 1)
                    element(ph, B - 1, None)
                elif isinstance(ph, MlpPhase):
                    mlp_scalar(act, ph)
                else:
                    last_scalar(act, ph)

        @block.vector
        def _(dve):
            nc.vector.memset(CN[:, :, :], 0.0)
            for k in range(2):
                nc.vector.memset(VA[k][:, :, :, :], 1.0)
            nc.vector.memset(VN[:, :, :], 0.0)
            for k in range(2):
                nc.vector.memset(OB[k][:, :], 0.0)
            for g in range(NG):
                nc.vector.memset(QP[g][:, :], 0.0)
                last = nc.vector.memset(KP[g][:, :], 0.0)
            last.then_inc(sem("cleared"), 1)
            dve.wait_ge(sem("cleared"), 1)
            for g in range(NG):
                last = nc.vector.memset(KP[g][MR:MR + 2, :], 1.0)
            last.then_inc(sem("ones_set"), 1)
            for name in ("probs_full", "pv_done", "heads_copied", "group_done"):
                dve.sem_inc(sem(name), 2)
            for name in ("mlp_centered", "mlp_gated"):
                dve.sem_inc(sem(name), 1)
            dve.wait_ge(sem("cond_exp"), 1)
            nc.vector.tensor_scalar_add(CND[:, B:2 * B], CND[:, 0:B], 1.0).then_inc(sem("cond_step"), 1)
            dve.wait_ge(sem("cond_step"), 1)
            nc.vector.reciprocal(CND[:, 0:B], CND[:, B:2 * B]).then_inc(sem("cond_step"), 1)
            dve.wait_ge(sem("cond_step"), 2)
            nc.vector.tensor_tensor(CND[:, 2 * B:3 * B], CND[:, 0:B], WM[:, NMOD * (D + 1):NWM], ALU.mult).then_inc(
                sem("cond_done"), 1)
            dve.wait_ge(sem("weights_loaded"), 16)
            nc.vector.tensor_copy(IDB[:, :], w("ident"))
            dve.wait_ge(sem("mod_full"), 1)
            nc.vector.tensor_tensor(MODT[:, :].rearrange("p (k b) -> p k b", b=B),
                                    MISC[:, 0:NMOD * B].rearrange("p (k b) -> p k b", b=B),
                                    WM[:, NMOD * D:NMOD * (D + 1)].unsqueeze(2).to_broadcast([D, NMOD, B]),
                                    ALU.add).then_inc(sem("cond_step"), 1)
            dve.wait_ge(sem("cond_step"), 3)
            for k in MOD_SCALES:
                last = nc.vector.tensor_scalar_add(MODT[:, k * B:(k + 1) * B], MODT[:, k * B:(k + 1) * B], 1.0)
            last.then_inc(sem("mod_done"), 1)
            dve.wait_ge(sem("mod_done"), 1)
            dve.wait_ge(sem("x_loaded"), 16)

            def piece(ph, run, b, name):
                at = ph.c.at
                use = None if name in NO_BANK else ph.misc(run, name)
                if name == "mean":
                    dve.wait_ge(sem("misc_full"), use + 1)
                    nc.vector.tensor_tensor(XC[:, 0:N], xcols(b), MISC[:, 0:N], ALU.subtract).then_inc(
                        sem("misc_free"), 1)
                elif name == "norm":
                    dve.wait_ge(sem("rstd_done"), at("rstd_done", b, 1))
                    dst = XN if ph.mod else XM
                    nc.vector.tensor_tensor(dst[:, 0:N], XC[:, 0:N], RSTD[:, 0:N], ALU.mult).then_inc(
                        sem("unit_done"), 1)
                    if ph.mod:
                        dve.wait_ge(sem("unit_done"), at("unit_done", b, 1))
                        nc.vector.tensor_scalar(XM[:, 0:N], XN[:, 0:N], modcol(ph.mod[0], b), modcol(ph.mod[1], b),
                                                ALU.mult, ALU.add).then_inc(sem("normed"), 1)
                elif name == "stats":
                    dve.wait_ge(sem("ctx_loaded"), at("ctx_loaded", b, 32))
                    for t in range(ph.nt):
                        last = nc.vector.bn_stats(ST[:, t, :], CN[:, t, :])
                    last.then_inc(sem("stats_read"), 1)
                    wait_apart(dve, "stats_read", at("stats_read", b, 1))
                    for t in range(ph.nt):
                        last = nc.vector.bn_aggr(MV[:, t, :], ST[:, t, :])
                    last.then_inc(sem("stats_done"), 1)
                elif name == "ctx_norm":
                    dve.wait_ge(sem("ctx_rstd"), at("ctx_rstd", b, 1))
                    if ph.kvmod:
                        nc.vector.tensor_scalar(KVM[:, :].unsqueeze(2),
                                                MODT[:, :].rearrange("p (k b) -> p k b", b=B)[
                                                    :, ph.kvmod[0]:ph.kvmod[0] + 2, ds(b, 1)],
                                                1.0, None, ALU.mult)
                    nc.vector.scalar_tensor_tensor(out=CO[:, :], in0=MV[:, :, 0], scalar=-1.0, in1=CR[:, :],
                                                   op0=ALU.mult, op1=ALU.mult).then_inc(sem("ctx_offset"), 1)
                elif name == "q" or name[0] == "k":
                    units = [("bq", 0, 0, N, QS[:, 0, :])] if name == "q" else []
                    if name == "q" and not ph.cross:
                        units.append(("bk", N, N, N, KS[:, 0, 0:N]))
                    if name[0] == "k":
                        c0, n = CHUNKS[int(name[1])]
                        units.append(("bk", 0, N + c0, n, KS[:, 0, c0:c0 + n]))
                    first = 0 if name == "q" else 1 + int(name[1])
                    dve.wait_ge(sem("high_done"), at("high_done", b, first + len(units)))
                    for bias, c, r, n, high in units:
                        last = nc.vector.scalar_tensor_tensor(
                            out=REST[:, r:r + n], in0=MISC[:, c:c + n], scalar=w(ph.name + bias), in1=high,
                            op0=ALU.add, op1=ALU.subtract)
                    last.then_inc(sem("misc_free"), 1)
                elif name[0] == "v" and name != "var":
                    j = int(name[1])
                    tiles = list(range(4 * j, min(4 * j + 4, ph.nt)))
                    dve.wait_ge(sem("misc_full"), use + 1)
                    if j == 0:
                        wait(dve, "values_packed", at("values_packed", b, 0))
                    kt, n = ph.tiles[tiles[0]], len(tiles)
                    nc.vector.tensor_tensor(
                        VN[0:kt, tiles[0]:tiles[0] + n, :],
                        MISC[0:kt, 0:n * D].rearrange("p (t d) -> p t d", d=D),
                        w(ph.name + "bv")[0:kt, :].unsqueeze(1).to_broadcast([kt, n, D]), ALU.add).then_inc(
                        sem("misc_free"), 1)
                elif name[0] == "d":
                    g = int(name[1])
                    dve.wait_ge(sem("misc_full"), use + 1)
                    dve.wait_ge(sem("group_done"), at("group_done", b, g))
                    nc.vector.reciprocal(REC[:, :], MISC[:, 0:N]).then_inc(sem("misc_free"), 1)
                    dve.wait_ge(sem("misc_free"), use + 1)
                    nc.vector.tensor_tensor(ON[g][:, :], RS[g % 2][:, :], REC[:, :], ALU.mult).then_inc(
                        sem("group_done"), 1)
                elif name == "y":
                    dve.wait_ge(sem("misc_full"), use + 1)
                    if ph.gate is None:
                        nc.vector.scalar_tensor_tensor(out=xcols(b), in0=MISC[:, 0:N], scalar=w(ph.name + "bp"),
                                                       in1=xcols(b), op0=ALU.add, op1=ALU.add).then_inc(
                            sem("misc_free"), 1)
                    else:
                        nc.vector.tensor_scalar(XU[:, :], MISC[:, 0:N], w(ph.name + "bp"), modcol(ph.gate, b),
                                                ALU.add, ALU.mult).then_inc(sem("misc_free"), 1)
                        dve.wait_ge(sem("misc_free"), use + 1)
                        nc.vector.tensor_tensor(xcols(b), xcols(b), XU[:, :], ALU.add).then_inc(
                            sem("stream_done"), 1)

            def maximum(ph, b, g, j):
                at = ph.c.at
                dve.wait_ge(sem("max_full"), at("max_full", b, g * ph.nm + j + 1))
                src = MB[j % len(MB)]
                if ph.cross:
                    r, c = j // len(CHUNKS), j % len(CHUNKS)
                    nc.vector.tensor_reduce(MX[:, r, c:c + 1], src[:, 0:CHUNKS[c][1]], AX.X, ALU.max).then_inc(
                        sem("max_done"), 1)
                else:
                    nc.vector.tensor_reduce(MX[:, 2 * j:2 * j + 2, 0], src[:, :].rearrange("p (t k) -> p t k", t=2),
                                            AX.X, ALU.max).then_inc(sem("max_done"), 1)

            def shifts(ph, b, g):
                at = ph.c.at
                dve.wait_ge(sem("max_done"), at("max_done", b, (g + 1) * ph.nm))
                parts = MX[:, :, :] if ph.cross else MX[:, :, 0:1]
                nc.vector.tensor_reduce(NMF[:, :], parts, AX.X, ALU.max, negate=True).then_inc(sem("shift_step"), 1)
                dve.wait_ge(sem("shift_step"), at("shift_step", b, 2 * g + 1))
                nc.vector.tensor_copy(NMB[g % 2][:, :, 0], NMF[:, :]).then_inc(sem("shift_step"), 1)
                dve.wait_ge(sem("shift_step"), at("shift_step", b, 2 * g + 2))
                nc.vector.tensor_tensor(NMB[g % 2][:, :, 1], NMF[:, :], NMB[g % 2][:, :, 0], ALU.subtract).then_inc(
                    sem("shift_ready"), 1)

            def element(ph, b, nxt):
                for g in range(NG):
                    ahead = (b, g + 1) if g + 1 < NG else (nxt, 0)
                    for t in range(ph.nt):
                        if ahead[0] is not None:
                            mine = ph.pieces_of_maximum(t)
                            for j in mine:
                                maximum(ph, *ahead, j)
                            if mine and mine[-1] == ph.nm - 1:
                                shifts(ph, *ahead)
                        for name in ph.here(g * ph.nt + t, nxt is not None):
                            piece(ph, b, b if name[0] == "d" else nxt, name)
                piece(ph, b, b, "d3")
                piece(ph, b, b, "y")

            for ph in plan:
                if isinstance(ph, Phase):
                    for name in ph.prep:
                        piece(ph, None, 0, name)
                    for j in range(ph.nm):
                        maximum(ph, 0, 0, j)
                    shifts(ph, 0, 0)
                    with dve.Fori(0, B - 1) as i:
                        element(ph, i, i + 1)
                    element(ph, B - 1, None)
                elif isinstance(ph, MlpPhase):
                    mlp_vector(dve, ph)
                else:
                    last_vector(dve, ph)

        @block.gpsimd
        def _(pool):
            pool.wait_ge(sem("cleared"), 1)

            def piece(ph, run, b, name):
                at = ph.c.at
                if name == "ctx_norm":
                    wait_apart(pool, "ctx_offset", at("ctx_offset", b, 1))
                    for t in range(ph.nt):
                        last = nc.gpsimd.tensor_scalar(CN[:, t, :], CN[:, t, :], CR[:, t:t + 1], CO[:, t:t + 1],
                                                       ALU.mult, ALU.add)
                    last.then_inc(sem("ctx_normed"), 1)
                elif name == "q" or name[0] == "k":
                    units = [(QS, 0, N, 0)] if name == "q" else []
                    if name == "q" and not ph.cross:
                        units.append((KS, 0, N, N))
                    if name[0] == "k":
                        c0, n = CHUNKS[int(name[1])]
                        units.append((KS, c0, n, N + c0))
                    first = 0 if name == "q" else 1 + int(name[1])
                    wait_apart(pool, "misc_free", ph.misc(run, name) + 1)
                    for k, (dst, c, n, r) in enumerate(units):
                        nc.gpsimd.tensor_copy(dst[:, 1, c:c + n], REST[:, r:r + n]).then_inc(sem("mid_done"), 1)
                        pool.wait_ge(sem("mid_done"), at("mid_done", b, first + k + 1))
                        nc.gpsimd.tensor_tensor(dst[:, 2, c:c + n], REST[:, r:r + n], dst[:, 1, c:c + n],
                                                ALU.subtract).then_inc(sem("low_done"), 1)

            def pack_values(ph, run, b, g):
                at = ph.c.at
                if g == 0:
                    pool.wait_ge(sem("misc_free"), ph.misc(run, "v3" if ph.cross else "v0") + 1)
                back = (g - 1) * ph.nt
                wait_apart(pool, "pv_done", at("pv_done", b, max(back, 0) if isinstance(b, int) and b == 0 else back))
                nc.gpsimd.tensor_copy(
                    VA[g % 2][:, 0:ph.nt, :, 0:HD],
                    VN[:, 0:ph.nt, G * HD * g:G * HD * (g + 1)].rearrange("p t (h d) -> p t h d", d=HD)).then_inc(
                    sem("values_packed"), 1)

            def element(ph, b, nxt):
                for g in range(NG):
                    ahead = (b, g + 1) if g + 1 < NG else (nxt, 0)
                    for t in range(ph.nt):
                        for name in ph.here(g * ph.nt + t, nxt is not None):
                            if name[0] != "d":
                                piece(ph, b, nxt, name)
                        if ahead[0] is not None and t == (ph.nt - 1 if g == NG - 1 else min(1, ph.nt - 1)):
                            pack_values(ph, b, *ahead)

            for ph in plan:
                if isinstance(ph, Phase):
                    for name in ph.prep:
                        piece(ph, None, 0, name)
                    pack_values(ph, None, 0, 0)
                    with pool.Fori(0, B - 1) as i:
                        element(ph, i, i + 1)
                    element(ph, B - 1, None)


def lay_out(a):
    f = np.float32

    def dh(m):
        return m.reshape(m.shape[:-1] + (H, HD)).swapaxes(-1, -2).reshape(m.shape)

    def col(v):
        return v.reshape(-1, D).T

    def row(v):
        return np.broadcast_to(v, (D, v.size))

    def strips(m):
        p = np.zeros((4, 32, NG, D), f)
        p[:, :HD] = m.reshape(NG, 4, HD, D).transpose(1, 2, 0, 3)
        return p.reshape(128, NG * D)

    k = np.arange(128)
    main = {"mean": np.full((D, D), 1.0 / D, f), "ident": np.eye(D, dtype=f),
            "spread": (k[:, None] == (k[None, :] // 32) * 32 + HD).astype(f),
            "eps5": np.full((D, 1), 1e-5, f), "eps6": np.full((D, 1), 1e-6, f), "one": np.ones((D, 1), f)}

    def attention(n, wq, bq, wk, bk, wv, bv, wp, bp):
        main.update({n + "wq": dh(wq), n + "wk": dh(wk), n + "wv": wv, n + "wp": strips(wp), n + "bv": row(bv),
                     n + "bq": col(dh(bq)), n + "bk": col(dh(bk)), n + "bp": col(bp)})

    l0, l1, l2, l3 = ({k[len(p):]: v for k, v in a.items() if k.startswith(p)}
                      for p in ("L0_xcond_", "L1_xcond_", "L2_xcond_", "L3_xcond_"))
    attention("a0", l0["Wq"], l0["bq"], l0["Wkv"][:, :D], l0["bkv"][:D], l0["Wkv"][:, D:], l0["bkv"][D:], l0["Wp"],
              l0["bp"])
    for n, wqkv, bqkv, wp, bp in (("s1", l1["qkv_w"], l1["qkv_b"], l1["sa_proj_w"], l1["sa_proj_b"]),
                                  ("s2", l2["W_qkv"], l2["b_qkv"], l2["W_proj"], l2["b_proj"])):
        attention(n, wqkv[:, :D], bqkv[:D], wqkv[:, D:2 * D], bqkv[D:2 * D], wqkv[:, 2 * D:], bqkv[2 * D:], wp, bp)
    for n, wq, bq, wkv, bkv, wp, bp in (
            ("c1", l1["q_w"], l1["q_b"], l1["kv_w"], l1["kv_b"], l1["ca_proj_w"], l1["ca_proj_b"]),
            ("c2", l2["W_qc"], l2["b_qc"], l2["W_kvc"], l2["b_kvc"], l2["W_cproj"], l2["b_cproj"])):
        attention(n, wq, bq, wkv[:, :D], bkv[:D], wkv[:, D:], bkv[D:], wp, bp)
    for n, w1, b1, w2, b2 in (("m1", l1["fc1_w"], l1["fc1_b"], l1["fc2_w"], l1["fc2_b"]),
                              ("m2", l2["W_mlp1"], l2["b_mlp1"], l2["W_mlp2"], l2["b_mlp2"])):
        main.update({n + "w1": w1, n + "w2": w2.reshape(4, D, D).transpose(1, 0, 2).reshape(D, 4 * D),
                     n + "b1": col(b1), n + "b2": col(b2)})
    thirds = (3, D)
    last = {"wq": l3["Wq"], "wkT": l3["Wk"].T, "wv": l3["Wv"],
            "rw": l3["router_W"].reshape(3, D, E3).transpose(1, 0, 2),
            "ew1": l3["e_w1"].reshape((E3,) + thirds + (2, D)).transpose(2, 1, 0, 3, 4),
            "ew2": l3["e_w2"].reshape(E3, 2, D, D).transpose(2, 0, 1, 3),
            "gw1": l3["gate_w1"].reshape(thirds + (D,)).transpose(1, 0, 2), "gw2": l3["gate_w2"],
            "ow": l3["out_w"], "gamma": col(l3["ln_gamma"]), "beta": col(l3["ln_beta"]), "rb": row(l3["router_b"]),
            "eb1": col(l3["e_b1"]), "eb2": col(l3["e_b2"]), "gb1": col(l3["gate_b1"]), "gb2": col(l3["gate_b2"]),
            "ob": col(l3["out_b"])}
    wm = [l0["Wss_q"], l0["Wss_kv"], l1["adaln_w"], l2["W_mod"]]
    bm = [l0["bss_q"], l0["bss_kv"], l1["adaln_b"], l2["b_mod"]]
    return {
        "x_t": np.ascontiguousarray(a["x"].transpose(2, 0, 1).reshape(D, B * N)),
        "ctx_n": np.ascontiguousarray(a["ctx_1024"]),
        "ctx_t": np.ascontiguousarray(a["ctx_1024"].transpose(0, 2, 1)),
        "w_mod": np.concatenate(wm + [col(b) for b in bm] + [a["cond_1024"].T], axis=1),
        "w_main": np.concatenate([main[n].reshape(D, -1) for n in COLS], axis=1),
        "w_last": np.concatenate([last[n].reshape(D, -1) for n in COLS3], axis=1),
    }


def kernel(**inputs):
    import numpy as _np
    import concourse.bacc as _bacc
    from concourse import mybir as _mybir
    from concourse.bass_utils import run_bass_kernel_spmd as _run

    nc = _bacc.Bacc("TRN2", target_bir_lowering=False, num_devices=1)
    arrays = lay_out({k: _np.asarray(v) for k, v in inputs.items()})
    aps = {n: nc.dram_tensor(n, v.shape, _mybir.dt.from_np(v.dtype), kind="ExternalInput").ap()
           for n, v in arrays.items()}
    out = nc.dram_tensor("out_t", (D, B * N), _mybir.dt.float32, kind="ExternalOutput").ap()
    build(nc, aps["x_t"], aps["ctx_n"], aps["ctx_t"], aps["w_mod"], aps["w_main"], aps["w_last"], out, PHASES)
    r = _run(nc, [arrays], core_ids=[0])
    return _np.ascontiguousarray(r.results[0]["out_t"].reshape(D, B, N).transpose(1, 2, 0))
```

```python
import numpy as np
import concourse.bass as bass
from concourse import mybir
from contextlib import ExitStack


B, N, D = 16, 256, 128
S = 1601
H, HD = 16, 8
G = 4
NG = H // G
R9 = 9 * HD
MR = 96
SCALE = float(HD) ** -0.5
MLPW = 4 * D
RH = 2 * D
E3 = 3
FULL = S // 128
LAST = S - FULL * 128
LN_EXP = "natural_log_exp_and_others"

CHUNKS = [(0, 401), (401, 400), (801, 400), (1201, 400)]
CROSS_TILES = [128] * FULL + [LAST]
SELF_TILES = [128, 128]

M_L0 = dict(scq=0, shq=1, sck=2, shk=3)
M_L1 = dict(sh_a=4, sc_a=5, g_a=6, sh_m=7, sc_m=8, g_m=9)
M_L2 = dict(sh_a=10, sc_a=11, g_a=12, sh_m=13, sc_m=14, g_m=15)
NMOD = 16
MOD_SCALES = (0, 2, 5, 8, 11, 14)

ATT = ["a0", "s1", "c1", "s2", "c2"]
MLP = ["m1", "m2"]
STATS = ["stats%d" % t for t in range(FULL + 1)]
NO_BANK = ["square", "norm", "ctx_scale", "ctx_norm"] + STATS


PHASES = ("a0", "s1", "c1", "m1", "s2", "c2", "m2", "l3")


def _columns():
    cols, at = {}, 0
    main = [("mean", D), ("pick", G), ("ident", D), ("eps5", 1), ("eps6", 1), ("one", 1)]
    for a in ATT:
        main += [(a + "wq", D), (a + "wk", D), (a + "wv", D), (a + "wp", NG * D), (a + "bv", NG),
                 (a + "bq", 1), (a + "bk", 1), (a + "bp", 1)]
    for m in MLP:
        main += [(m + "w1", MLPW), (m + "w2", MLPW), (m + "b1", 4), (m + "b2", 1)]
    for name, n in main:
        cols[name] = (at, n)
        at += n
    last, at3 = {}, 0
    for name, n in [("ew1", 18 * D), ("ew2", 6 * D), ("wq", D), ("wkT", D), ("wv", D), ("rw", 9),
                    ("gw1", 3 * D), ("gw2", D), ("ow", D), ("gamma", 1), ("beta", 1), ("rb", 3),
                    ("eb1", 6), ("eb2", 3), ("gb1", 1), ("gb2", 1), ("ob", 1)]:
        last[name] = (at3, n)
        at3 += n
    return cols, at, last, at3


COLS, NW, COLS3, NW3 = _columns()
SPLIT3 = COLS3["wq"][0]
NWM = NMOD * D + NMOD + B


class Count:

    def __init__(self, start, per, batches):
        self.start, self.per, self.batches = dict(start), per, batches

    def at(self, name, b, k):
        return self.start.get(name, 0) + b * self.per[name] + k

    def after(self):
        return {n: self.start.get(n, 0) + self.batches * p for n, p in self.per.items()}


class Phase:

    def __init__(self, name, start, before):
        self.name, self.before = name, before
        self.cross = name in ("a0", "c1", "c2")
        self.raw = name == "c1"
        self.tiles = CROSS_TILES if self.cross else SELF_TILES
        self.nt = len(self.tiles)
        self.nk = sum(self.tiles)
        self.eps = "eps5" if name == "a0" else "eps6"
        self.mod = {"a0": (0, 1), "s1": (5, 4), "s2": (11, 10)}.get(name)
        self.kvmod = (2, 3) if name == "a0" else None
        self.gate = {"s1": 6, "s2": 12}.get(name)
        self.layer = ATT.index(name)
        self.nm = 2 * G * len(CHUNKS) if self.cross else G
        ctx = self.cross and not self.raw
        if self.cross:
            self.prep = ["mean", "square", "var", "norm", "q"]
            if ctx:
                self.prep += STATS + ["ctx_scale", "ctx_norm", "t0", "t1", "t2", "t3"]
            self.prep += ["k0", "k1", "k2", "k3", "v0", "v1", "v2", "v3"]
        else:
            self.prep = ["mean", "square", "var", "norm", "q", "v0"]
        units = 5 if self.cross else 2
        self.key_stores = [(3, 0, CHUNKS[2][0]), (5, CHUNKS[2][0], S - CHUNKS[2][0])] if self.cross else [(2, 0, N)]
        self.c = Count(start, dict(
            scores_full=2 * self.nt * NG, probs_full=2 * self.nt * NG, pv_done=self.nt * NG,
            heads_copied=NG, group_done=NG, inverse_ready=1, max_full=self.nm * NG, max_done=self.nm * NG,
            shift_step=2 * NG, shift_ready=NG, rows_full=2 * NG, rows_done=2 * NG, values_packed=NG,
            squared=1, rstd_done=1, unit_done=1, normed=1 if self.mod else 0,
            rest_done=units, mid_done=units, low_done=units,
            ctx_loaded=0 if not self.cross else (16 if self.raw else 32),
            stats_done=1 if ctx else 0, stats_read=FULL + 1 if ctx else 0, ctx_log=1 if ctx else 0,
            ctx_rstd=1 if ctx else 0, ctx_offset=1 if ctx else 0, ctx_normed=1 if ctx else 0,
            split_stored=16 + 16 * len(self.key_stores), stream_done=1 if self.gate is not None else 0,
            **{"packed_loaded%d" % g: 64 for g in range(NG)}), B)
        self.shift_tile = self.nt - 2 if self.cross else self.nt - 1

    def after(self):
        return self.c.after()

    def maximum_at(self, slot):
        t, n = slot
        spread = max(n - 2, 1)
        return [j for j in range(self.nm) if min(j * spread // self.nm, n - 1) == t]

    def prep_slots(self, host):
        if host.cross:
            at = dict(mean=2, square=3, var=4, norm=6, q=8, v0=34)
            if self.cross:
                at.update({n: 4 + j * 8 // 13 for j, n in enumerate(STATS)})
                at.update(ctx_scale=12, ctx_norm=12, t0=17, t1=18, k0=19, t2=20, k1=22, t3=23, k2=25, k3=27)
                at.update({"v%d" % j: 34 + 2 * j for j in range(4)})
        else:
            at = dict(mean=0, square=0, var=1, norm=1, q=2, v0=6)
            if self.cross:
                at.update({n: 1 for n in STATS})
                at.update(ctx_scale=2, ctx_norm=2, t0=3, t1=3, t2=3, t3=3,
                          k0=4, k1=4, k2=5, k3=5, v0=6, v1=6, v2=7, v3=7)
        return [(at[n], "prep", n) for n in sorted(self.prep, key=lambda n: at[n])]


class Element:

    def __init__(self, ph, b, prev, nxt, misc):
        self.ph, self.b, self.prev, self.nxt, self.misc = ph, b, prev, nxt, misc
        pieces = []
        if ph is None:
            if nxt:
                pieces += [(0, "prep", n) for n in nxt[0].prep]
            if prev:
                pieces += [(0, "post", n) for n in ("d", "e0", "e1", "y")]
        else:
            if prev:
                at = dict(d=3, e0=5, e1=7, y=9) if ph.cross else dict(d=1, e0=2, e1=3, y=4)
                pieces += [(at[n], "post", n) for n in at]
            if nxt:
                pieces += nxt[0].prep_slots(ph)
        self.pieces = sorted(pieces, key=lambda x: x[0])
        self.uses = [(role, n) for _, role, n in self.pieces if n not in NO_BANK]
        self.slots = 1 if ph is None else ph.nt * NG

    def owner(self, role):
        return {"post": self.prev, "prep": self.nxt}[role]

    def use(self, role, name):
        return self.misc + self.uses.index((role, name))

    def here(self, slot):
        found = [(r, n) for s, r, n in self.pieces if s == slot]
        return found[:1], found[1:]


def elements(ph, misc, chained, follows):
    last = B - 1
    out = {}
    out["before"] = None if chained else Element(None, None, None, (ph, 0), misc)
    misc += 0 if chained else len(out["before"].uses)
    out["first"] = Element(ph, 0, (chained, last) if chained else None, (ph, 1), misc)
    misc += len(out["first"].uses)
    n = len(Element(ph, 1, (ph, 0), (ph, 2), 0).uses)
    out["middle"] = lambda i, m=misc: Element(ph, i, (ph, i + -1), (ph, i + 1), m + (i + -1) * n)
    misc += (B - 2) * n
    out["last"] = Element(ph, last, (ph, last - 1), (follows, 0) if follows else None, misc)
    misc += len(out["last"].uses)
    out["after"] = None if follows else Element(None, None, (ph, last), None, misc)
    misc += 0 if follows else len(out["after"].uses)
    return out, misc


class MlpPhase:

    def __init__(self, name, start):
        self.name = name
        self.mod, self.gate = ((8, 7), 9) if name == "m1" else ((14, 13), 15)
        self.c = Count(start, dict(
            mlp_mean=1, mlp_centered=1, mlp_squared=1, mlp_var=1, mlp_log=1, mlp_rstd=1, mlp_unit=1, mlp_normed=1,
            mlp_hidden=4, mlp_act=4, mlp_out=1, mlp_gated=1, stream_done=1), B // 2)

    def after(self):
        return self.c.after()


class LastPhase:

    def __init__(self, start):
        self.start = dict(start)
        one = dict.fromkeys("""l_mean l_centered l_squared l_var l_log l_rstd l_unit l_normed l_q l_qf l_k l_qk
            l_shift l_shift_high l_shift_low l_rows l_rowed l_sum l_recip l_spread l_spreaded
            l_weighed l_ev l_evidence l_logits l_logit l_lmax l_lsub l_lexp l_lsum l_lrec l_prob l_pb""".split(), 1)
        nt = len(CROSS_TILES)
        one.update(l_max=2 * len(CHUNKS), l_maxed=2 * len(CHUNKS), l_scores=nt, l_probs=nt, l_pv=nt, l_acc=nt, l_pbc=2)
        self.c = Count({}, one, B)
        two = dict.fromkeys("""l_g2 l_tanh l_gate l_out l_delta l_stream""".split(), 1)
        two.update(l_hidden=7, l_silu=7, l_expert=3, l_w=3, l_routed=3)
        self.c2 = Count({}, two, B // 2)


def build(nc, xT, ctxN, ctxT, wmod, wmain, w3, outT, phases):
    f32, bf16 = mybir.dt.float32, mybir.dt.bfloat16
    ALU, ACT, AX = mybir.AluOpType, mybir.ActivationFunctionType, mybir.AxisListType
    ds = bass.ds

    start = dict(probs_full=2, pv_done=2, heads_copied=2, mlp_centered=1, mlp_gated=1)
    start["misc_full"] = 0
    names = {}
    plan = []
    for name in phases:
        before = plan[-1] if plan and isinstance(plan[-1], Phase) else None
        plan.append(Phase(name, start, before) if name in ATT else
                    MlpPhase(name, start) if name in MLP else LastPhase(start))
        if name != "l3":
            start = {**start, **plan[-1].after()}
    misc = 0
    for k, ph in enumerate(plan):
        if isinstance(ph, Phase):
            follows = plan[k + 1] if k + 1 < len(plan) and isinstance(plan[k + 1], Phase) else None
            ph.el, misc = elements(ph, misc, ph.before, follows)
        ph.misc_after = misc
    stream_total = {k: (ph.misc_after, ph.after().get("stream_done", 0) if not isinstance(ph, LastPhase) else 0)
                    for k, ph in enumerate(plan)}

    ctx = ExitStack()
    with ctx:
        def sb(name, shape, dt):
            return ctx.enter_context(nc.sbuf_tensor(name, shape, dt))

        sems = {}

        def sem(name):
            if name not in sems:
                sems[name] = ctx.enter_context(nc.semaphore(name))
            return sems[name]

        def wait(eng, name, n):
            if not (isinstance(n, int) and n <= 0):
                eng.wait_ge(sem(name), n)

        X = sb("X", [D, B * N], f32)
        W = sb("W", [128, NW], f32)
        MODT = sb("MODT", [D, NMOD * B], f32)
        KP = [sb("KP%d" % g, [128, G * S], bf16) for g in range(NG)]
        QP = [sb("QP%d" % g, [128, G * N], bf16) for g in range(NG)]
        VA = [sb("VA%d" % k, [128, len(CROSS_TILES), G, HD + 1], f32) for k in range(2)]
        VN = sb("VN", [128, len(CROSS_TILES), D], f32)
        P = [sb("P%d" % k, [128, G * N], f32) for k in range(2)]
        CN = sb("CN", [128, len(CROSS_TILES), D], f32)
        CT = sb("CT", [D, len(CROSS_TILES) * 128], f32)
        KSF = sb("KSF", [D, 3 * S + 1], bf16)
        KS = KSF[:, 0:3 * S].rearrange("p (r k) -> p r k", r=3)
        QS = sb("QS", [D, 3, N], bf16)
        REST = sb("REST", [D, N + S], f32)
        RS = [sb("RS%d" % g, [128, N], f32) for g in range(NG)]
        ON = [sb("ON%d" % g, [128, N], f32) for g in range(NG)]
        REC = sb("REC", [128, N], f32)
        RDN = sb("RDN", [128, 2 * H], f32)
        RDX = sb("RDX", [128, 2 * NG * 128], f32)
        BPT = sb("BPT", [D, len(ATT)], f32)
        XU = sb("XU", [D, N], f32)
        XC = sb("XC", [D, 2 * N], f32)
        SQ = sb("SQ", [D, 2 * N], f32)
        LG = sb("LG", [D, 2 * N], f32)
        RSTD = sb("RSTD", [D, 2 * N], f32)
        XN = sb("XN", [D, 2 * N], f32)
        XM = sb("XM", [D, 2 * N], f32)
        ST = sb("ST", [128, len(CROSS_TILES), 6], f32)
        MV = sb("MV", [128, len(CROSS_TILES), 2], f32)
        CL = sb("CL", [128, len(CROSS_TILES)], f32)
        KVM = sb("KVM", [D, 2], f32)
        CR = sb("CR", [128, len(CROSS_TILES)], f32)
        CO = sb("CO", [128, len(CROSS_TILES)], f32)
        MX = sb("MX", [128, 2 * G, len(CHUNKS)], f32)
        NMF = sb("NMF", [128, 2 * G], f32)
        NMB = [sb("NMB%d" % k, [128, 2 * G, 2], bf16) for k in range(2)]
        XMA = sb("XMA", [D, B * N], f32)
        HM = [P[k][:, r * 2 * N:(r + 1) * 2 * N] for k in range(2) for r in range(2)]
        IDB = sb("IDB", [128, 128], bf16)

        bank = [ctx.enter_context(nc.psum_tensor("bank%d" % k, [128, 512], f32)) for k in range(8)]
        SC, OB, MB, MISC = bank[0:2], bank[2:4], bank[4:7], bank[7]

        scr_k = nc.dram_tensor("scr_k", [3 * HD, H, S], bf16, kind="Internal").ap()
        scr_ks = nc.dram_tensor("scr_ks", [3 * HD, H, N], bf16, kind="Internal").ap()
        scr_q = nc.dram_tensor("scr_q", [3, HD, H, N], bf16, kind="Internal").ap()

        def w(name, k=0, n=None):
            at, width = COLS[name]
            return W[:, at + k:at + (width if n is None else k + n)]

        def modcol(k, b):
            return MODT[:, ds(b + k * B, 1)]

        def xcols(b, n=N):
            return X[:, ds(b * N, n)]

        def wait_apart(eng, name, n):
            eng.wait_ge(sem(name), n)
            eng.sem_inc(sem("passed"), 1)

        def stream_ready(eng, ph):
            if ph is not None:
                wait(eng, "misc_free", ph.misc_after)
                wait(eng, "stream_done", ph.after().get("stream_done", 0))

        def before(ph):
            k = plan.index(ph)
            return plan[k - 1] if k else None

        WM = sb("WM", [D, NWM], f32)
        CND = sb("CND", [D, 3 * B], f32)

        W3A = KP[0][:, :].bitcast(f32)[:, 0:SPLIT3]
        W3B = KP[1][:, :].bitcast(f32)[:, 0:NW3 - SPLIT3]
        HID = [KP[2][:, :].bitcast(f32)[:, u * 2 * N:(u + 1) * 2 * N] for u in range(6)]
        T3 = KP[3][:, :].bitcast(f32)
        HID.append(T3[:, 0:2 * N])
        PB = T3[:, 2 * N:8 * N].rearrange("p (e q) -> p e q", e=E3)
        NX = T3[:, 8 * N:10 * N]
        EV = T3[:, 10 * N:12 * N]
        CTX_N = [CN, VN]
        CTX_T = [CT[:, :], KSF[:, :].bitcast(f32)]
        ACC = SQ[:, 0:N]
        ROW = sb("ROW", [2, N], bf16)
        ONE2 = sb("ONE2", [2, 128], bf16)
        EA = sb("EA", [D, 7 * B], f32)
        EAP = sb("EAP", [D, 7, 2], f32)
        RA = sb("RA", [D, B * E3], f32)
        HGB = sb("HGB", [D, 1], f32)
        RD = sb("RD", [128, 2], f32)
        LT = sb("LT", [128, 5, 2 * E3], f32)
        COND = WM[:, NMOD * (D + 1):NWM]

        def w3c(name, k=0, n=None):
            at, width = COLS3[name]
            src, at = (W3A, at) if at < SPLIT3 else (W3B, at - SPLIT3)
            return src[:, at + k:at + (width if n is None else k + n)]

        def mlp_tensor(pe, ph):
            at = ph.c.at
            stream_ready(pe, before(ph))
            with pe.Fori(0, B // 2) as i:
                pe.wait_ge(sem("mlp_centered"), at("mlp_centered", i, 0))
                nc.tensor.matmul(bank[0][:, :], w("mean"), X[:, ds(i * 2 * N, 2 * N)], start=True, stop=True).then_inc(
                    sem("mlp_mean"), 1)
                pe.wait_ge(sem("mlp_squared"), at("mlp_squared", i, 1))
                nc.tensor.matmul(bank[1][:, :], w("mean"), SQ[:, :], start=True, stop=True).then_inc(sem("mlp_var"), 1)
            with pe.Fori(0, B // 2) as i:
                pe.wait_ge(sem("mlp_normed"), at("mlp_normed", B // 2 - 1, 1))
                for c in range(4):
                    if c == 0:
                        pe.wait_ge(sem("mlp_gated"), at("mlp_gated", i, 0))
                    nc.tensor.matmul(bank[2 + c][:, :], w(ph.name + "w1", c * D, D), XMA[:, ds(i * 2 * N, 2 * N)],
                                     start=True, stop=True).then_inc(sem("mlp_hidden"), 1)
                for c in range(4):
                    pe.wait_ge(sem("mlp_act"), at("mlp_act", i, c + 1))
                    last = nc.tensor.matmul(bank[6][:, :], w(ph.name + "w2", c * D, D), HM[c], start=(c == 0),
                                            stop=(c == 3))
                last.then_inc(sem("mlp_out"), 1)

        def mlp_scalar(act, ph):
            at = ph.c.at
            with act.Fori(0, B // 2) as i:
                act.wait_ge(sem("mlp_centered"), at("mlp_centered", i, 1))
                nc.scalar.activation(SQ[:, :], XC[:, :], ACT.Square).then_inc(sem("mlp_squared"), 1)
                act.wait_ge(sem("mlp_var"), at("mlp_var", i, 1))
                nc.scalar.activation(LG[:, :], bank[1][:, :], ACT.Ln, bias=w("eps6")).then_inc(sem("mlp_log"), 1)
                act.wait_ge(sem("mlp_log"), at("mlp_log", i, 1))
                nc.scalar.activation(RSTD[:, :], LG[:, :], ACT.Exp, scale=-0.5).then_inc(sem("mlp_rstd"), 1)
            nc.scalar.preload_act_table(ACT.Gelu_apprx_tanh)
            with act.Fori(0, B // 2) as i:
                for c in range(4):
                    act.wait_ge(sem("mlp_hidden"), at("mlp_hidden", i, c + 1))
                    nc.scalar.activation(HM[c], bank[2 + c][:, :], ACT.Gelu_apprx_tanh,
                                         bias=w(ph.name + "b1", c, 1)).then_inc(sem("mlp_act"), 1)
            nc.scalar.preload_act_table_set(LN_EXP)

        def mlp_vector(dve, ph):
            at = ph.c.at
            with dve.Fori(0, B // 2) as i:
                dve.wait_ge(sem("mlp_mean"), at("mlp_mean", i, 1))
                nc.vector.tensor_tensor(XC[:, :], X[:, ds(i * 2 * N, 2 * N)], bank[0][:, :], ALU.subtract).then_inc(
                    sem("mlp_centered"), 1)
                dve.wait_ge(sem("mlp_rstd"), at("mlp_rstd", i, 1))
                nc.vector.tensor_tensor(XN[:, :], XC[:, :], RSTD[:, :], ALU.mult).then_inc(sem("mlp_unit"), 1)
                dve.wait_ge(sem("mlp_unit"), at("mlp_unit", i, 1))
                for r in range(2):
                    last = nc.vector.tensor_scalar(XMA[:, ds(i * 2 * N + r * N, N)], XN[:, r * N:(r + 1) * N],
                                                   modcol(ph.mod[0], i * 2 + r), modcol(ph.mod[1], i * 2 + r),
                                                   ALU.mult, ALU.add)
                last.then_inc(sem("mlp_normed"), 1)
                dve.wait_ge(sem("mlp_normed"), at("mlp_normed", i, 1))
            with dve.Fori(0, B // 2) as i:
                dve.wait_ge(sem("mlp_out"), at("mlp_out", i, 1))
                for r in range(2):
                    last = nc.vector.tensor_scalar(XC[:, r * N:(r + 1) * N], bank[6][:, r * N:(r + 1) * N],
                                                   w(ph.name + "b2"), modcol(ph.gate, i * 2 + r), ALU.add, ALU.mult)
                last.then_inc(sem("mlp_gated"), 1)
                dve.wait_ge(sem("mlp_gated"), at("mlp_gated", i, 1))
                nc.vector.tensor_tensor(X[:, ds(i * 2 * N, 2 * N)], X[:, ds(i * 2 * N, 2 * N)], XC[:, :],
                                        ALU.add).then_inc(sem("stream_done"), 1)
                dve.wait_ge(sem("stream_done"), at("stream_done", i, 1))

        def last_sync(sp, ph):
            at, at2 = ph.c.at, ph.c2.at

            def load(b, r):
                sp.dma_start(CTX_N[r][:, 0:FULL, :], ctxN[ds(b, 1), 0:FULL * 128, :].rearrange(
                    "o (t p) d -> (o p) t d", p=128)).then_inc(sem("l_ctx%d" % r), 16)
                sp.dma_start(CTX_N[r][0:LAST, FULL, :], ctxN[ds(b, 1), FULL * 128:S, :].rearrange(
                    "o p d -> (o p) d")).then_inc(sem("l_ctx%d" % r), 16)
                sp.dma_start(CTX_T[r][:, 0:S], ctxT[ds(b, 1)].rearrange("o d s -> (o d) s")).then_inc(
                    sem("l_ctx%d" % r), 16)

            c2 = [p for p in plan if isinstance(p, Phase)][-1]
            stream_ready(sp, c2)
            for r in range(2):
                load(r, r)
            with sp.Fori(0, B // 2 - 1) as i:
                for r in range(2):
                    sp.wait_ge(sem("l_weighed"), at("l_weighed", i * 2 + r, 1))
                    load(i * 2 + (2 + r), r)
                sp.wait_ge(sem("l_stream"), at2("l_stream", i, 1))
                sp.dma_start(outT[:, ds(i * 2 * N, 2 * N)], X[:, ds(i * 2 * N, 2 * N)]).then_inc(
                    sem("out_stored"), 16)
            sp.wait_ge(sem("l_stream"), B // 2)
            sp.dma_start(outT[:, B * N - 2 * N:B * N], X[:, B * N - 2 * N:B * N]).then_inc(sem("out_stored"), 16)
            sp.wait_ge(sem("out_stored"), 16 * (B // 2))

        def last_tensor(pe, ph):
            at, at2 = ph.c.at, ph.c2.at
            stream_ready(pe, before(ph))
            pe.wait_ge(sem("last_weights"), 32)
            for u in range(7):
                for_anchor = w3c("ew1", (2 * E3 + u // 2) * 2 * D + (u % 2) * D, D) if u < 6 else w3c("gw1", 2 * D, D)
                nc.tensor.matmul(bank[0][:, u * B:(u + 1) * B], for_anchor, COND, start=True, stop=True)
            for b in range(B):
                last = nc.tensor.matmul(bank[1][:, b * E3:(b + 1) * E3], COND[:, b:b + 1].to_broadcast([D, 128]),
                                        w3c("rw", 6, 3), start=True, stop=True)
            last.then_inc(sem("l_anchor"), 1)
            pe.wait_ge(sem("l_anchored"), 1)

            def attend(b, r):
                kn, kT = CTX_N[r], CTX_T[r]
                half = slice(r * N, (r + 1) * N)

                def one(name, after, out, lhsT, rhs):
                    pe.wait_ge(sem(after), at(after, b, 1))
                    nc.tensor.matmul(out, lhsT, rhs, start=True, stop=True).then_inc(sem(name), 1)

                nc.tensor.matmul(MISC[:, 0:N], w("mean"), X[:, ds(b * N, N)], start=True, stop=True).then_inc(
                    sem("l_mean"), 1)
                one("l_var", "l_squared", SC[0][:, 0:N], w("mean"), SQ[:, 0:N])
                one("l_q", "l_normed", MISC[:, 0:N], w3c("wq"), NX[:, half])
                one("l_k", "l_qf", SC[0][:, 0:N], w3c("wkT"), XM[:, 0:N])
                pe.wait_ge(sem("l_qk"), at("l_qk", b, 1))
                pe.wait_ge(sem("l_ctx%d" % r), (b - r) * 24 + 48)
                for j in range(2 * len(CHUNKS)):
                    qt, (c0, n) = j // len(CHUNKS), CHUNKS[j % len(CHUNKS)]
                    if j >= len(MB):
                        pe.wait_ge(sem("l_maxed"), at("l_maxed", b, j - len(MB) + 1))
                    nc.tensor.matmul(MB[j % 3][:, 0:n], XM[:, N + qt * 128:N + qt * 128 + 128], kT[:, c0:c0 + n],
                                     start=True, stop=True).then_inc(sem("l_max"), 1)
                pe.wait_ge(sem("l_shift_low"), at("l_shift_low", b, 1))
                for qt in range(2):
                    last = nc.tensor.matmul(MB[2][0:2, qt * 128:(qt + 1) * 128], NMB[0][:, qt, :], IDB[:, :],
                                            start=True, stop=True)
                last.then_inc(sem("l_rows"), 1)
                pe.wait_ge(sem("l_rowed"), at("l_rowed", b, 1))
                for t in range(len(CROSS_TILES) + 1):
                    if t < len(CROSS_TILES):
                        kt = CROSS_TILES[t]
                        if t >= 2:
                            pe.wait_ge(sem("l_probs"), at("l_probs", b, t - 1))
                        nc.tensor.matmul(SC[t % 2][0:kt, 0:N], kT[:, t * 128:t * 128 + kt], XM[:, N:2 * N],
                                         start=True, stop=False)
                        nc.tensor.matmul(SC[t % 2][0:kt, 0:N], ONE2[:, 0:kt], ROW[:, :], start=False,
                                         stop=True).then_inc(sem("l_scores"), 1)
                    if t:
                        kt = CROSS_TILES[t - 1]
                        pe.wait_ge(sem("l_probs"), at("l_probs", b, t))
                        nc.tensor.matmul(OB[0][:, 0:N], kn[0:kt, t - 1, :], P[(t - 1) % 2][0:kt, 0:N], start=(t == 1),
                                         stop=(t == len(CROSS_TILES))).then_inc(sem("l_pv"), 1)
                pe.wait_ge(sem("l_acc"), at("l_acc", b, len(CROSS_TILES)))
                for qt in range(2):
                    last = nc.tensor.matmul(MB[0][:, qt:qt + 1], ACC[:, qt * 128:(qt + 1) * 128], w("one"), start=True,
                                            stop=True)
                last.then_inc(sem("l_sum"), 1)
                pe.wait_ge(sem("l_recip"), at("l_recip", b, 1))
                for qt in range(2):
                    last = nc.tensor.matmul(MB[1][:, qt * 128:(qt + 1) * 128], RD[:, qt:qt + 1].to_broadcast([128, 128]),
                                            w("ident"), start=True, stop=True)
                last.then_inc(sem("l_spread"), 1)
                one("l_ev", "l_weighed", MISC[:, 0:N], w3c("wv"), XN[:, 0:N])
                pe.wait_ge(sem("l_evidence"), at("l_evidence", b, 1))
                for qt in range(2):
                    q = slice(r * N + qt * 128, r * N + (qt + 1) * 128)
                    nc.tensor.matmul(MB[2][:, qt * E3:(qt + 1) * E3], NX[:, q], w3c("rw", 0, 3), start=True, stop=False)
                    last = nc.tensor.matmul(MB[2][:, qt * E3:(qt + 1) * E3], EV[:, q], w3c("rw", 3, 3), start=False,
                                            stop=True)
                last.then_inc(sem("l_logits"), 1)
                pe.wait_ge(sem("l_prob"), at("l_prob", b, 1))
                for e in range(E3):
                    for qt in range(2):
                        c = (e % 2) * N + qt * 128
                        last = nc.tensor.matmul(SC[e // 2][:, c:c + 128],
                                                LT[:, 4, qt * E3 + e:qt * E3 + e + 1].to_broadcast([128, 128]),
                                                w("ident"), start=True, stop=True)
                last.then_inc(sem("l_pb"), 1)
                pe.wait_ge(sem("l_pbc"), at("l_pbc", b, 2))

            def experts(i):
                for u in range(7):
                    for k, src in ((0, NX), (1, EV)):
                        wt = w3c("ew1", (k * E3 + u // 2) * 2 * D + (u % 2) * D, D) if u < 6 else w3c("gw1", k * D, D)
                        last = nc.tensor.matmul(bank[u][:, :], wt, src[:, :], start=(k == 0), stop=(k == 1))
                    last.then_inc(sem("l_hidden"), 1)
                for e in range(E3):
                    pe.wait_ge(sem("l_silu"), at2("l_silu", i, 2 * e + 2))
                    for k in range(2):
                        last = nc.tensor.matmul(bank[(7, 0, 1)[e]][:, :], w3c("ew2", (2 * e + k) * D, D), HID[2 * e + k],
                                                start=(k == 0), stop=(k == 1))
                    last.then_inc(sem("l_expert"), 1)
                pe.wait_ge(sem("l_silu"), at2("l_silu", i, 7))
                nc.tensor.matmul(bank[3][:, :], w3c("gw2"), HID[6], start=True, stop=True).then_inc(sem("l_g2"), 1)
                pe.wait_ge(sem("l_routed"), at2("l_routed", i, 3))
                nc.tensor.matmul(bank[4][:, :], w3c("ow"), XN[:, :], start=True, stop=True).then_inc(sem("l_out"), 1)
                pe.wait_ge(sem("l_stream"), at2("l_stream", i, 1))

            with pe.Fori(0, B // 2) as i:
                for r in range(2):
                    attend(i * 2 + r, r)
                experts(i)

        def last_scalar(act, ph):
            at, at2 = ph.c.at, ph.c2.at

            def attend(b, r):
                half = slice(r * N, (r + 1) * N)

                def one(name, after, k, *args, **kw):
                    act.wait_ge(sem(after), at(after, b, k))
                    nc.scalar.activation(*args, **kw).then_inc(sem(name), 1)

                one("l_squared", "l_centered", 1, SQ[:, 0:N], XC[:, 0:N], ACT.Square)
                one("l_log", "l_var", 1, LG[:, 0:N], SC[0][:, 0:N], ACT.Ln, bias=w("eps5"))
                one("l_rstd", "l_log", 1, RSTD[:, 0:N], LG[:, 0:N], ACT.Exp, scale=-0.5)
                one("l_qf", "l_q", 1, XM[:, 0:N], MISC[:, 0:N], ACT.Copy)
                one("l_qk", "l_k", 1, XM[:, N:2 * N], SC[0][:, 0:N], ACT.Copy)
                one("l_rowed", "l_rows", 1, ROW[:, :], MB[2][0:2, 0:N], ACT.Copy)
                for t, kt in enumerate(CROSS_TILES):
                    if t >= 2:
                        act.wait_ge(sem("l_pv"), at("l_pv", b, t - 1))
                        act.wait_ge(sem("l_acc"), at("l_acc", b, t - 1))
                    one("l_probs", "l_scores", t + 1, P[t % 2][0:kt, 0:N], SC[t % 2][0:kt, 0:N], ACT.Exp,
                        scale=float(D) ** -0.5)
                one("l_spreaded", "l_spread", 1, REC[:, :], MB[1][:, 0:N], ACT.Copy)
                one("l_evidence", "l_ev", 1, EV[:, half], MISC[:, 0:N], ACT.Copy)
                one("l_lexp", "l_lsub", 1, LT[:, 2, :], LT[:, 1, :], ACT.Exp)
                one("l_pbc", "l_pb", 1, PB[:, 0:2, half], SC[0][:, :].rearrange("p (e q) -> p e q", e=2), ACT.Copy)
                one("l_pbc", "l_pb", 1, PB[:, 2, half], SC[1][:, 0:N], ACT.Copy)

            with act.Fori(0, B // 2) as i:
                nc.scalar.preload_act_table_set(LN_EXP)
                for r in range(2):
                    attend(i * 2 + r, r)
                nc.scalar.preload_act_table(ACT.Silu)
                for u in range(7):
                    act.wait_ge(sem("l_hidden"), at2("l_hidden", i, u + 1))
                    for r in range(2):
                        last = nc.scalar.activation(HID[u][:, r * N:(r + 1) * N], bank[u][:, r * N:(r + 1) * N],
                                                    ACT.Silu, bias=EAP[:, u, r:r + 1])
                    last.then_inc(sem("l_silu"), 1)
                act.wait_ge(sem("l_g2"), at2("l_g2", i, 1))
                nc.scalar.activation(LG[:, :], bank[3][:, :], ACT.Tanh, bias=HGB[:, :], scale=0.5).then_inc(
                    sem("l_tanh"), 1)

        def last_vector(dve, ph):
            at, at2 = ph.c.at, ph.c2.at
            dve.wait_ge(sem("l_anchor"), 1)
            nc.vector.tensor_tensor(EA[:, 0:6 * B].rearrange("p (u b) -> p u b", b=B),
                                    bank[0][:, 0:6 * B].rearrange("p (u b) -> p u b", b=B),
                                    w3c("eb1").unsqueeze(2).to_broadcast([D, 6, B]), ALU.add)
            nc.vector.tensor_scalar(EA[:, 6 * B:7 * B], bank[0][:, 6 * B:7 * B], w3c("gb1"), None, ALU.add)
            nc.vector.tensor_tensor(RA[:, :].rearrange("p (b e) -> p b e", e=E3),
                                    bank[1][:, 0:B * E3].rearrange("p (b e) -> p b e", e=E3),
                                    w3c("rb").unsqueeze(1).to_broadcast([D, B, E3]), ALU.add)
            nc.vector.memset(ONE2[:, :], 1.0)
            nc.vector.tensor_scalar(HGB[:, :], w3c("gb2"), 0.5, None, ALU.mult).then_inc(sem("l_anchored"), 1)
            dve.wait_ge(sem("l_anchored"), 1)

            def attend(b, r):
                def after(name, k=1):
                    dve.wait_ge(sem(name), at(name, b, k))

                half = slice(r * N, (r + 1) * N)
                after("l_mean")
                nc.vector.tensor_tensor(XC[:, 0:N], X[:, ds(b * N, N)], MISC[:, 0:N], ALU.subtract).then_inc(
                    sem("l_centered"), 1)
                after("l_rstd")
                nc.vector.tensor_tensor(XN[:, 0:N], XC[:, 0:N], RSTD[:, 0:N], ALU.mult).then_inc(sem("l_unit"), 1)
                after("l_unit")
                nc.vector.tensor_scalar(NX[:, half], XN[:, 0:N], w3c("gamma"), w3c("beta"), ALU.mult,
                                        ALU.add).then_inc(sem("l_normed"), 1)
                for j in range(2 * len(CHUNKS)):
                    qt, c = j // len(CHUNKS), j % len(CHUNKS)
                    after("l_max", j + 1)
                    nc.vector.tensor_reduce(MX[:, qt, c:c + 1], MB[j % 3][:, 0:CHUNKS[c][1]], AX.X, ALU.max).then_inc(
                        sem("l_maxed"), 1)
                after("l_maxed", 2 * len(CHUNKS))
                nc.vector.tensor_reduce(NMF[:, 0:2], MX[:, 0:2, :], AX.X, ALU.max, negate=True).then_inc(
                    sem("l_shift"), 1)
                after("l_shift")
                nc.vector.tensor_copy(NMB[0][:, 0:2, 0], NMF[:, 0:2]).then_inc(sem("l_shift_high"), 1)
                after("l_shift_high")
                nc.vector.tensor_tensor(NMB[0][:, 0:2, 1], NMF[:, 0:2], NMB[0][:, 0:2, 0], ALU.subtract).then_inc(
                    sem("l_shift_low"), 1)
                for t, kt in enumerate(CROSS_TILES):
                    after("l_probs", t + 1)
                    if t == 0:
                        nc.vector.tensor_copy(ACC, P[0][:, 0:N]).then_inc(sem("l_acc"), 1)
                    else:
                        after("l_acc", t)
                        nc.vector.tensor_tensor(ACC[0:kt, :], ACC[0:kt, :], P[t % 2][0:kt, 0:N], ALU.add).then_inc(
                            sem("l_acc"), 1)
                after("l_sum")
                nc.vector.reciprocal(RD[:, :], MB[0][:, 0:2]).then_inc(sem("l_recip"), 1)
                after("l_spreaded")
                nc.vector.tensor_tensor(XN[:, 0:N], OB[0][:, 0:N], REC[:, :], ALU.mult).then_inc(sem("l_weighed"), 1)
                after("l_logits")
                nc.vector.tensor_tensor(LT[:, 0, :].rearrange("p (t e) -> p t e", e=E3),
                                        MB[2][:, 0:2 * E3].rearrange("p (t e) -> p t e", e=E3),
                                        RA[:, ds(b * E3, E3)].unsqueeze(1).to_broadcast([128, 2, E3]),
                                        ALU.add).then_inc(sem("l_logit"), 1)
                after("l_logit")
                nc.vector.tensor_reduce(LT[:, 3, 0:2], LT[:, 0, :].rearrange("p (t e) -> p t e", e=E3), AX.X,
                                        ALU.max).then_inc(sem("l_lmax"), 1)
                after("l_lmax")
                nc.vector.tensor_tensor(LT[:, 1, :].rearrange("p (t e) -> p t e", e=E3),
                                        LT[:, 0, :].rearrange("p (t e) -> p t e", e=E3),
                                        LT[:, 3, 0:2].unsqueeze(2).to_broadcast([128, 2, E3]),
                                        ALU.subtract).then_inc(sem("l_lsub"), 1)
                after("l_lexp")
                nc.vector.tensor_reduce(LT[:, 3, 2:4], LT[:, 2, :].rearrange("p (t e) -> p t e", e=E3), AX.X,
                                        ALU.add).then_inc(sem("l_lsum"), 1)
                after("l_lsum")
                nc.vector.reciprocal(LT[:, 3, 4:6], LT[:, 3, 2:4]).then_inc(sem("l_lrec"), 1)
                after("l_lrec")
                nc.vector.tensor_tensor(LT[:, 4, :].rearrange("p (t e) -> p t e", e=E3),
                                        LT[:, 2, :].rearrange("p (t e) -> p t e", e=E3),
                                        LT[:, 3, 4:6].unsqueeze(2).to_broadcast([128, 2, E3]),
                                        ALU.mult).then_inc(sem("l_prob"), 1)

            with dve.Fori(0, B // 2) as i:
                nc.vector.tensor_scalar(EAP[:, :, :], EA[:, :].rearrange("p (u b) -> p u b", b=B)[:, :, ds(i * 2, 2)],
                                        1.0, None, ALU.mult)
                for r in range(2):
                    attend(i * 2 + r, r)
                for e in range(E3):
                    dve.wait_ge(sem("l_expert"), at2("l_expert", i, e + 1))
                    dst = XN if e == 0 else (XC, XM)[e - 1]
                    nc.vector.scalar_tensor_tensor(out=dst[:, :], in0=bank[(7, 0, 1)[e]][:, :], scalar=w3c("eb2", e, 1),
                                                   in1=PB[:, e, :], op0=ALU.add, op1=ALU.mult).then_inc(sem("l_w"), 1)
                dve.wait_ge(sem("l_w"), at2("l_w", i, 3))
                nc.vector.tensor_tensor(XC[:, :], XC[:, :], XM[:, :], ALU.add).then_inc(sem("l_routed"), 1)
                dve.wait_ge(sem("l_routed"), at2("l_routed", i, 1))
                nc.vector.tensor_tensor(XN[:, :], XN[:, :], XC[:, :], ALU.add).then_inc(sem("l_routed"), 2)
                dve.wait_ge(sem("l_tanh"), at2("l_tanh", i, 1))
                nc.vector.tensor_scalar(RSTD[:, :], LG[:, :], 0.5, 0.5, ALU.mult, ALU.add).then_inc(sem("l_gate"), 1)
                dve.wait_ge(sem("l_gate"), at2("l_gate", i, 1))
                dve.wait_ge(sem("l_out"), at2("l_out", i, 1))
                nc.vector.scalar_tensor_tensor(out=XC[:, :], in0=bank[4][:, :], scalar=w3c("ob"), in1=RSTD[:, :],
                                               op0=ALU.add, op1=ALU.mult).then_inc(sem("l_delta"), 1)
                dve.wait_ge(sem("l_delta"), at2("l_delta", i, 1))
                nc.vector.tensor_tensor(X[:, ds(i * 2 * N, 2 * N)], X[:, ds(i * 2 * N, 2 * N)], XC[:, :],
                                        ALU.add).then_inc(sem("l_stream"), 1)
                dve.wait_ge(sem("l_stream"), at2("l_stream", i, 1))

        block = ctx.enter_context(nc.Block())

        @block.sync
        def _(sp):
            sp.dma_start(WM[:, :], wmod).then_inc(sem("wmod_loaded"), 16)
            sp.dma_start(W[:, :], wmain).then_inc(sem("weights_loaded"), 16)
            sp.dma_start(X[:, :], xT).then_inc(sem("x_loaded"), 16)

            def prepare(el):
                ph, b = el.nxt
                at = ph.c.at
                if ph.cross:
                    wait(sp, "misc_full", el.misc)
                    if ph.raw:
                        sp.dma_start(CT[:, 0:S], ctxT[ds(b, 1)].rearrange("o d s -> (o d) s")).then_inc(
                            sem("ctx_loaded"), 16)
                    else:
                        sp.dma_start(CN[:, 0:FULL, :], ctxN[ds(b, 1), 0:FULL * 128, :].rearrange(
                            "o (p t) d -> (o p) t d", t=FULL)).then_inc(sem("ctx_loaded"), 16)
                        sp.dma_start(CN[0:LAST, FULL, :], ctxN[ds(b, 1), FULL * 128:S, :].rearrange(
                            "o p d -> (o p) d")).then_inc(sem("ctx_loaded"), 16)
                for g in range(NG):
                    wait(sp, "packed_loaded%d" % g, at("packed_loaded%d" % g, b, 0))
                sp.wait_ge(sem("low_done"), at("low_done", b, 1))
                sp.dma_start(scr_q.rearrange("a d h q -> (d h) a q"), QS[:, :, :]).then_inc(sem("split_stored"), 16)
                kscr = scr_k if ph.cross else scr_ks
                for made, k0, n in ph.key_stores:
                    sp.wait_ge(sem("low_done"), at("low_done", b, made))
                    sp.dma_start(kscr[:, :, k0:k0 + n].rearrange("(r d) h k -> (d h) r k", r=3),
                                 KS[:, :, k0:k0 + n]).then_inc(sem("split_stored"), 16)
                sp.wait_ge(sem("split_stored"), at("split_stored", b, ph.c.per["split_stored"]))
                for g in range(NG):
                    if el.ph is None:
                        stream_ready(sp, before(ph))
                    else:
                        sp.wait_ge(sem("scores_full"), el.ph.c.at("scores_full", el.b, 2 * el.ph.nt * (g + 1)))
                    sp.dma_start(KP[g][0:R9, 0:G * ph.nk], kscr[:, G * g:G * g + G, :].rearrange(
                        "r h k -> r (h k)").unsqueeze(0).to_broadcast([3, 3 * HD, G * ph.nk])).then_inc(
                        sem("packed_loaded%d" % g), 16)
                    for a in range(3):
                        sp.dma_start(QP[g][24 * a:24 * a + 24, :], scr_q[a, :, G * g:G * g + G, :].rearrange(
                            "d h q -> d (h q)").unsqueeze(0).to_broadcast([3, HD, G * N])).then_inc(
                            sem("packed_loaded%d" % g), 16)

            sp.wait_ge(sem("cleared"), 1)
            for ph in plan:
                if isinstance(ph, Phase):
                    if ph.el["before"]:
                        prepare(ph.el["before"])
                    prepare(ph.el["first"])
                    with sp.Fori(1, B - 1) as i:
                        prepare(ph.el["middle"](i))
                    if ph.el["last"].nxt:
                        prepare(ph.el["last"])
                    if ph.name == "c2" and "l3" in phases:
                        stream_ready(sp, ph)
                        sp.dma_start(W3A, w3[:, 0:SPLIT3]).then_inc(sem("last_weights"), 16)
                        sp.dma_start(W3B, w3[:, SPLIT3:NW3]).then_inc(sem("last_weights"), 16)
                elif isinstance(ph, LastPhase):
                    last_sync(sp, ph)
            if not isinstance(plan[-1], LastPhase):
                stream_ready(sp, plan[-1])
                sp.dma_start(outT, X[:, :]).then_inc(sem("out_stored"), 16)
                sp.wait_ge(sem("out_stored"), 16)

        @block.tensor
        def _(pe):
            pe.wait_ge(sem("wmod_loaded"), 16)
            pe.wait_ge(sem("cond_done"), 1)
            for k in range(NMOD):
                last = nc.tensor.matmul(MISC[:, k * B:(k + 1) * B], WM[:, k * D:(k + 1) * D], CND[:, 2 * B:3 * B],
                                        start=True, stop=True)
            last.then_inc(sem("mod_full"), 1)
            pe.wait_ge(sem("weights_loaded"), 16)
            for k, a in enumerate(ATT):
                for g in range(NG):
                    last = nc.tensor.matmul(bank[0][:, k:k + 1], w(a + "wp", g * D, D), w(a + "bv", g, 1),
                                            start=(g == 0), stop=(g == NG - 1))
            last.then_inc(sem("bias_full"), 1)
            pe.wait_ge(sem("bias_done"), 1)
            pe.wait_ge(sem("x_loaded"), 16)
            pe.wait_ge(sem("mod_done"), 1)
            pe.wait_ge(sem("cleared"), 1)
            pe.wait_ge(sem("ones_set"), 1)

            def piece(el, role, name):
                if name in NO_BANK:
                    return
                ph, b = el.owner(role)
                at, use = ph.c.at, el.use(role, name)
                wait(pe, "misc_free", use)
                if name == "mean":
                    if ph.before and ph.before.gate is not None:
                        pe.wait_ge(sem("stream_done"), ph.before.c.at("stream_done", b, 1))
                    last = nc.tensor.matmul(MISC[:, 0:N], w("mean"), xcols(b), start=True, stop=True)
                elif name == "var":
                    pe.wait_ge(sem("squared"), at("squared", b, 1))
                    last = nc.tensor.matmul(MISC[:, 0:N], w("mean"), SQ[:, 0:N], start=True, stop=True)
                elif name == "q":
                    done = "normed" if ph.mod else "unit_done"
                    pe.wait_ge(sem(done), at(done, b, 1))
                    last = nc.tensor.matmul(MISC[:, 0:N], w(ph.name + "wq"), XM[:, 0:N], start=True, stop=True)
                    if not ph.cross:
                        last = nc.tensor.matmul(MISC[:, N:2 * N], w(ph.name + "wk"), XM[:, 0:N], start=True, stop=True)
                elif name[0] == "t":
                    j = int(name[1])
                    pe.wait_ge(sem("ctx_normed"), at("ctx_normed", b, 1))
                    for k, t in enumerate(range(4 * j, min(4 * j + 4, ph.nt))):
                        last = nc.tensor.transpose(MISC[:, k * 128:(k + 1) * 128], CN[:, t, :], w("ident"))
                elif name[0] == "k":
                    c0, n = CHUNKS[int(name[1])]
                    if ph.raw:
                        pe.wait_ge(sem("ctx_loaded"), at("ctx_loaded", b, 16))
                    last = nc.tensor.matmul(MISC[:, 0:n], w(ph.name + "wk"), CT[:, c0:c0 + n], start=True, stop=True)
                elif name[0] == "v":
                    src = CT if ph.cross else XM
                    for k, t in enumerate(range(4 * int(name[1]), min(4 * int(name[1]) + 4, ph.nt))):
                        kt = ph.tiles[t]
                        last = nc.tensor.matmul(MISC[0:kt, k * D:(k + 1) * D], src[:, t * 128:t * 128 + kt],
                                                w(ph.name + "wv"), start=True, stop=True)
                elif name == "d":
                    pe.wait_ge(sem("heads_copied"), at("heads_copied", b, NG))
                    for g in range(NG):
                        for qt in range(2):
                            c = (2 * g + qt) * G
                            last = nc.tensor.matmul(MISC[:, c:c + G], RS[g][:, qt * 128:(qt + 1) * 128], w("pick"),
                                                    start=True, stop=True)
                elif name[0] == "e":
                    pe.wait_ge(sem("inverse_ready"), at("inverse_ready", b, 1))
                    for k in range(4):
                        c = (4 * int(name[1]) + k) * 128
                        last = nc.tensor.matmul(MISC[:, k * 128:(k + 1) * 128], RDX[:, c:c + 128], w("ident"),
                                                start=True, stop=True)
                elif name == "y":
                    pe.wait_ge(sem("group_done"), at("group_done", b, NG))
                    for g in range(NG):
                        last = nc.tensor.matmul(MISC[:, 0:N], w(ph.name + "wp", g * D, D), ON[g][:, :],
                                                start=(g == 0), stop=(g == NG - 1))
                last.then_inc(sem("misc_full"), 1)

            def scores(ph, b, g, t, half):
                at, kt = ph.c.at, ph.tiles[t]
                if t == 0 and half == 0:
                    pe.wait_ge(sem("rows_done"), at("rows_done", b, 2 * (g + 1)))
                pe.wait_ge(sem("probs_full"), at("probs_full", b, 2 * (g * ph.nt + t) + half - 1))
                for k in range(2):
                    h = 2 * half + k
                    c0 = h * ph.nk + t * 128
                    last = nc.tensor.matmul(SC[half][0:kt, k * N:(k + 1) * N], KP[g][:, c0:c0 + kt],
                                            QP[g][:, h * N:(h + 1) * N], start=True, stop=True)
                last.then_inc(sem("scores_full"), 1)

            def maximum(ph, b, g, j):
                at = ph.c.at
                if j == 0:
                    pe.wait_ge(sem("packed_loaded%d" % g), at("packed_loaded%d" % g, b, 64))
                    wait(pe, "rows_done", at("rows_done", b, 2 * g))
                if j >= len(MB):
                    pe.wait_ge(sem("max_done"), at("max_done", b, g * ph.nm + j - len(MB) + 1))
                dst = MB[j % len(MB)]
                if ph.cross:
                    r, c = j // len(CHUNKS), j % len(CHUNKS)
                    h, qt, (c0, n) = r // 2, r % 2, CHUNKS[c]
                    last = nc.tensor.matmul(dst[:, 0:n], QP[g][0:MR, h * N + qt * 128:h * N + qt * 128 + 128],
                                            KP[g][0:MR, h * ph.nk + c0:h * ph.nk + c0 + n], start=True, stop=True)
                else:
                    for qt in range(2):
                        last = nc.tensor.matmul(dst[:, qt * N:(qt + 1) * N],
                                                QP[g][0:MR, j * N + qt * 128:j * N + qt * 128 + 128],
                                                KP[g][0:MR, j * ph.nk:(j + 1) * ph.nk], start=True, stop=True)
                last.then_inc(sem("max_full"), 1)

            def shift_rows(ph, b, g):
                pe.wait_ge(sem("shift_ready"), ph.c.at("shift_ready", b, g + 1))
                for half in range(2):
                    dst = MB[(ph.nm + half) % len(MB)]
                    for r in range(4):
                        last = nc.tensor.matmul(dst[MR:MR + 2, r * 128:(r + 1) * 128], NMB[g % 2][:, 4 * half + r, :],
                                                IDB[:, :], start=True, stop=True)
                    last.then_inc(sem("rows_full"), 1)

            def head_values(ph, b, g, t):
                at, kt = ph.c.at, ph.tiles[t]
                if t == 0:
                    pe.wait_ge(sem("values_packed"), at("values_packed", b, g + 1))
                    pe.wait_ge(sem("heads_copied"), at("heads_copied", b, g - 1))
                pe.wait_ge(sem("probs_full"), at("probs_full", b, 2 * (g * ph.nt + t + 1)))
                for h in range(G):
                    last = nc.tensor.matmul(OB[g % 2][32 * h:32 * h + HD + 1, 0:N], VA[g % 2][0:kt, t, h, :],
                                            P[(g * ph.nt + t) % 2][0:kt, h * N:(h + 1) * N],
                                            start=(t == 0), stop=(t == ph.nt - 1))
                last.then_inc(sem("pv_done"), 1)

            def element(el):
                ph, b = el.ph, el.b
                last_tile = (el.prev[0], el.prev[1], NG - 1, el.prev[0].nt - 1) if el.prev else None
                for g in range(NG):
                    ahead = (ph, b, g + 1) if g + 1 < NG else (*el.nxt, 0) if el.nxt else None
                    for t in range(ph.nt):
                        js = ahead[0].maximum_at((t, ph.nt)) if ahead else []
                        third = -(-len(js) // 3)
                        among, behind = el.here(g * ph.nt + t)
                        scores(ph, b, g, t, 0)
                        for j in js[:third]:
                            maximum(*ahead, j)
                        for piece_ in among:
                            piece(el, *piece_)
                        scores(ph, b, g, t, 1)
                        for j in js[third:2 * third]:
                            maximum(*ahead, j)
                        if last_tile:
                            head_values(*last_tile)
                        last_tile = (ph, b, g, t)
                        for j in js[2 * third:]:
                            maximum(*ahead, j)
                        if ahead and t == ph.shift_tile:
                            shift_rows(*ahead)
                        for piece_ in behind:
                            piece(el, *piece_)

            for ph in plan:
                if isinstance(ph, Phase):
                    if ph.el["before"]:
                        stream_ready(pe, before(ph))
                        for piece_ in sum(ph.el["before"].here(0), []):
                            piece(ph.el["before"], *piece_)
                        for j in range(ph.nm):
                            maximum(ph, 0, 0, j)
                        shift_rows(ph, 0, 0)
                    element(ph.el["first"])
                    with pe.Fori(1, B - 1) as i:
                        element(ph.el["middle"](i))
                    element(ph.el["last"])
                    if ph.el["after"]:
                        head_values(ph, B - 1, NG - 1, ph.nt - 1)
                        for piece_ in sum(ph.el["after"].here(0), []):
                            piece(ph.el["after"], *piece_)
                elif isinstance(ph, MlpPhase):
                    mlp_tensor(pe, ph)
                else:
                    last_tensor(pe, ph)

        @block.scalar
        def _(act):
            act.wait_ge(sem("weights_loaded"), 16)
            nc.scalar.preload_act_table_set(LN_EXP)
            nc.scalar.activation(CL[:, 0:1], w("one"), ACT.Ln).then_inc(sem("act_ready"), 1)
            act.wait_ge(sem("wmod_loaded"), 16)
            nc.scalar.activation(CND[:, 0:B], WM[:, NMOD * (D + 1):NWM], ACT.Exp, scale=-1.0).then_inc(
                sem("cond_exp"), 1)
            act.wait_ge(sem("ones_set"), 1)

            def piece(el, role, name):
                ph, b = el.owner(role)
                at = ph.c.at
                use = None if name in NO_BANK else el.use(role, name)
                if name == "square":
                    act.wait_ge(sem("misc_free"), el.use(role, "mean") + 1)
                    nc.scalar.activation(SQ[:, 0:N], XC[:, 0:N], ACT.Square).then_inc(sem("squared"), 1)
                elif name == "var":
                    act.wait_ge(sem("misc_full"), use + 1)
                    nc.scalar.activation(LG[:, 0:N], MISC[:, 0:N], ACT.Ln, bias=w(ph.eps)).then_inc(sem("misc_free"), 1)
                    act.wait_ge(sem("misc_free"), use + 1)
                    nc.scalar.activation(RSTD[:, 0:N], LG[:, 0:N], ACT.Exp, scale=-0.5).then_inc(sem("rstd_done"), 1)
                elif name == "ctx_scale":
                    act.wait_ge(sem("stats_done"), at("stats_done", b, 1))
                    nc.scalar.activation(CL[:, :], MV[:, :, 1], ACT.Ln, bias=w(ph.eps)).then_inc(sem("ctx_log"), 1)
                    act.wait_ge(sem("ctx_log"), at("ctx_log", b, 1))
                    nc.scalar.activation(CR[:, :], CL[:, :], ACT.Exp, scale=-0.5).then_inc(sem("ctx_rstd"), 1)
                elif name == "q" or name[0] == "k":
                    act.wait_ge(sem("misc_full"), use + 1)
                    if name == "q":
                        wait(act, "split_stored", at("split_stored", b, 0))
                        units = [("bq", 0, 0, N, QS[:, 0, :])]
                        if not ph.cross:
                            units.append(("bk", N, N, N, KS[:, 0, 0:N]))
                    else:
                        c0, n = CHUNKS[int(name[1])]
                        units = [("bk", 0, N + c0, n, KS[:, 0, c0:c0 + n])]
                    for bias, c, r, n, high in units:
                        nc.scalar.activation(high, MISC[:, c:c + n], ACT.Identity, bias=w(ph.name + bias))
                        last = nc.scalar.activation(REST[:, r:r + n], MISC[:, c:c + n], ACT.Identity,
                                                    bias=w(ph.name + bias))
                    last.then_inc(sem("misc_free"), 1)
                elif name[0] == "t":
                    j = int(name[1])
                    n = 128 * min(4, ph.nt - 4 * j)
                    act.wait_ge(sem("misc_full"), use + 1)
                    if ph.kvmod:
                        last = nc.scalar.activation(CT[:, 512 * j:512 * j + n], MISC[:, 0:n], ACT.Identity,
                                                    bias=KVM[:, 1:2], scale=KVM[:, 0:1])
                    else:
                        last = nc.scalar.copy(CT[:, 512 * j:512 * j + n], MISC[:, 0:n])
                    last.then_inc(sem("misc_free"), 1)
                elif name[0] == "v":
                    j = int(name[1])
                    t0, n = 4 * j, min(4, ph.nt - 4 * j)
                    kt = ph.tiles[t0]
                    act.wait_ge(sem("misc_full"), use + 1)
                    if j == 0:
                        wait(act, "values_packed", at("values_packed", b, 0))
                    nc.scalar.copy(VN[0:kt, t0:t0 + n, :],
                                   MISC[0:kt, 0:n * D].rearrange("p (t d) -> p t d", d=D)).then_inc(
                        sem("misc_free"), 1)

            def exponentials(ph, b, g, t, half):
                at, kt, v = ph.c.at, ph.tiles[t], g * ph.nt + t
                act.wait_ge(sem("scores_full"), at("scores_full", b, 2 * v + half + 1))
                if half == 0:
                    act.wait_ge(sem("pv_done"), at("pv_done", b, v - 1))
                nc.scalar.activation(P[v % 2][0:kt, half * 2 * N:(half + 1) * 2 * N], SC[half][0:kt, :], ACT.Exp,
                                     scale=SCALE).then_inc(sem("probs_full"), 1)

            def copy_heads(ph, b, g):
                at = ph.c.at
                act.wait_ge(sem("pv_done"), at("pv_done", b, (g + 1) * ph.nt))
                wait(act, "group_done", at("group_done", b, g + 1 - NG))
                nc.scalar.copy(RS[g][:, :], OB[g % 2][:, 0:N]).then_inc(sem("heads_copied"), 1)

            def copy_rows(ph, b, g):
                for half in range(2):
                    act.wait_ge(sem("rows_full"), ph.c.at("rows_full", b, 2 * g + half + 1))
                    nc.scalar.copy(QP[g][MR:MR + 2, half * 2 * N:(half + 1) * 2 * N],
                                   MB[(ph.nm + half) % len(MB)][MR:MR + 2, :]).then_inc(sem("rows_done"), 1)

            def element(el):
                ph, b = el.ph, el.b
                for g in range(NG):
                    ahead = (ph, b, g + 1) if g + 1 < NG else (*el.nxt, 0) if el.nxt else None
                    for t in range(ph.nt):
                        among, behind = el.here(g * ph.nt + t)
                        exponentials(ph, b, g, t, 0)
                        if not ph.cross:
                            for piece_ in among:
                                piece(el, *piece_)
                        exponentials(ph, b, g, t, 1)
                        if ph.cross:
                            for piece_ in among:
                                piece(el, *piece_)
                        if t == (1 if ph.cross else 0) and g:
                            copy_heads(ph, b, g - 1)
                        elif t == (1 if ph.cross else 0) and el.prev:
                            copy_heads(*el.prev, NG - 1)
                        if ahead and t == ph.shift_tile:
                            copy_rows(*ahead)
                        for piece_ in behind:
                            piece(el, *piece_)

            for ph in plan:
                if isinstance(ph, Phase):
                    if ph.el["before"]:
                        for piece_ in sum(ph.el["before"].here(0), []):
                            piece(ph.el["before"], *piece_)
                        copy_rows(ph, 0, 0)
                    element(ph.el["first"])
                    with act.Fori(1, B - 1) as i:
                        element(ph.el["middle"](i))
                    element(ph.el["last"])
                    if ph.el["after"]:
                        copy_heads(ph, B - 1, NG - 1)
                elif isinstance(ph, MlpPhase):
                    mlp_scalar(act, ph)
                else:
                    last_scalar(act, ph)

        @block.vector
        def _(dve):
            nc.vector.memset(CN[:, :, :], 0.0)
            for k in range(2):
                nc.vector.memset(VA[k][:, :, :, :], 1.0)
            nc.vector.memset(VN[:, :, :], 0.0)
            for k in range(2):
                nc.vector.memset(OB[k][:, :], 0.0)
            for g in range(NG):
                nc.vector.memset(QP[g][:, :], 0.0)
                last = nc.vector.memset(KP[g][:, :], 0.0)
            last.then_inc(sem("cleared"), 1)
            dve.wait_ge(sem("cleared"), 1)
            for g in range(NG):
                last = nc.vector.memset(KP[g][MR:MR + 2, :], 1.0)
            last.then_inc(sem("ones_set"), 1)
            for name in ("probs_full", "pv_done", "heads_copied"):
                dve.sem_inc(sem(name), 2)
            for name in ("mlp_centered", "mlp_gated"):
                dve.sem_inc(sem(name), 1)
            dve.wait_ge(sem("cond_exp"), 1)
            nc.vector.tensor_scalar_add(CND[:, B:2 * B], CND[:, 0:B], 1.0).then_inc(sem("cond_step"), 1)
            dve.wait_ge(sem("cond_step"), 1)
            nc.vector.reciprocal(CND[:, 0:B], CND[:, B:2 * B]).then_inc(sem("cond_step"), 1)
            dve.wait_ge(sem("cond_step"), 2)
            nc.vector.tensor_tensor(CND[:, 2 * B:3 * B], CND[:, 0:B], WM[:, NMOD * (D + 1):NWM], ALU.mult).then_inc(
                sem("cond_done"), 1)
            dve.wait_ge(sem("weights_loaded"), 16)
            nc.vector.tensor_copy(IDB[:, :], w("ident"))
            dve.wait_ge(sem("bias_full"), 1)
            for k, a in enumerate(ATT):
                last = nc.vector.tensor_tensor(BPT[:, k:k + 1], bank[0][:, k:k + 1], w(a + "bp"), ALU.add)
            last.then_inc(sem("bias_done"), 1)
            dve.wait_ge(sem("mod_full"), 1)
            nc.vector.tensor_tensor(MODT[:, :].rearrange("p (k b) -> p k b", b=B),
                                    MISC[:, 0:NMOD * B].rearrange("p (k b) -> p k b", b=B),
                                    WM[:, NMOD * D:NMOD * (D + 1)].unsqueeze(2).to_broadcast([D, NMOD, B]),
                                    ALU.add).then_inc(sem("cond_step"), 1)
            dve.wait_ge(sem("cond_step"), 3)
            for k in MOD_SCALES:
                last = nc.vector.tensor_scalar_add(MODT[:, k * B:(k + 1) * B], MODT[:, k * B:(k + 1) * B], 1.0)
            last.then_inc(sem("mod_done"), 1)
            dve.wait_ge(sem("mod_done"), 1)
            dve.wait_ge(sem("x_loaded"), 16)

            def piece(el, role, name):
                ph, b = el.owner(role)
                at = ph.c.at
                use = None if name in NO_BANK else el.use(role, name)
                if name == "mean":
                    dve.wait_ge(sem("misc_full"), use + 1)
                    nc.vector.tensor_tensor(XC[:, 0:N], xcols(b), MISC[:, 0:N], ALU.subtract).then_inc(
                        sem("misc_free"), 1)
                elif name == "norm":
                    dve.wait_ge(sem("rstd_done"), at("rstd_done", b, 1))
                    dst = XN if ph.mod else XM
                    nc.vector.tensor_tensor(dst[:, 0:N], XC[:, 0:N], RSTD[:, 0:N], ALU.mult).then_inc(
                        sem("unit_done"), 1)
                    if ph.mod:
                        dve.wait_ge(sem("unit_done"), at("unit_done", b, 1))
                        nc.vector.tensor_scalar(XM[:, 0:N], XN[:, 0:N], modcol(ph.mod[0], b), modcol(ph.mod[1], b),
                                                ALU.mult, ALU.add).then_inc(sem("normed"), 1)
                elif name[:5] == "stats":
                    t = int(name[5:])
                    if t == 0:
                        dve.wait_ge(sem("ctx_loaded"), at("ctx_loaded", b, 32))
                    nc.vector.bn_stats(ST[:, t, :], CN[:, t, :]).then_inc(sem("stats_read"), 1)
                    wait_apart(dve, "stats_read", at("stats_read", b, t + 1))
                    last = nc.vector.bn_aggr(MV[:, t, :], ST[:, t, :])
                    if t == FULL:
                        last.then_inc(sem("stats_done"), 1)
                elif name == "ctx_norm":
                    dve.wait_ge(sem("ctx_rstd"), at("ctx_rstd", b, 1))
                    if ph.kvmod:
                        nc.vector.tensor_scalar(KVM[:, :].unsqueeze(2),
                                                MODT[:, :].rearrange("p (k b) -> p k b", b=B)[
                                                    :, ph.kvmod[0]:ph.kvmod[0] + 2, ds(b, 1)],
                                                1.0, None, ALU.mult)
                    nc.vector.scalar_tensor_tensor(out=CO[:, :], in0=MV[:, :, 0], scalar=-1.0, in1=CR[:, :],
                                                   op0=ALU.mult, op1=ALU.mult).then_inc(sem("ctx_offset"), 1)
                elif name == "d":
                    dve.wait_ge(sem("misc_full"), use + 1)
                    nc.vector.reciprocal(RDN[:, :], MISC[:, 0:2 * H]).then_inc(sem("misc_free"), 1)
                    dve.wait_ge(sem("misc_free"), use + 1)
                    nc.vector.tensor_scalar(RDX[:, :].rearrange("p (h r) -> p h r", r=32),
                                            RDN[:, :].unsqueeze(2).to_broadcast([128, 2 * H, 32]), 1.0, None,
                                            ALU.mult).then_inc(sem("inverse_ready"), 1)
                elif name[0] == "e":
                    dve.wait_ge(sem("misc_full"), use + 1)
                    for k in range(2):
                        g = 2 * int(name[1]) + k
                        last = nc.vector.tensor_tensor(ON[g][:, :], RS[g][:, :], MISC[:, k * N:(k + 1) * N], ALU.mult)
                    last.then_inc(sem("misc_free"), 1)
                    dve.wait_ge(sem("misc_free"), use + 1)
                    dve.sem_inc(sem("group_done"), 2)
                elif name == "y":
                    bias = BPT[:, ph.layer:ph.layer + 1]
                    dve.wait_ge(sem("misc_full"), use + 1)
                    if ph.gate is None:
                        nc.vector.scalar_tensor_tensor(out=xcols(b), in0=MISC[:, 0:N], scalar=bias,
                                                       in1=xcols(b), op0=ALU.add, op1=ALU.add).then_inc(
                            sem("misc_free"), 1)
                    else:
                        nc.vector.tensor_scalar(XU[:, :], MISC[:, 0:N], bias, modcol(ph.gate, b),
                                                ALU.add, ALU.mult).then_inc(sem("misc_free"), 1)
                        dve.wait_ge(sem("misc_free"), use + 1)
                        nc.vector.tensor_tensor(xcols(b), xcols(b), XU[:, :], ALU.add).then_inc(
                            sem("stream_done"), 1)

            def maximum(ph, b, g, j):
                at = ph.c.at
                dve.wait_ge(sem("max_full"), at("max_full", b, g * ph.nm + j + 1))
                src = MB[j % len(MB)]
                if ph.cross:
                    r, c = j // len(CHUNKS), j % len(CHUNKS)
                    nc.vector.tensor_reduce(MX[:, r, c:c + 1], src[:, 0:CHUNKS[c][1]], AX.X, ALU.max).then_inc(
                        sem("max_done"), 1)
                else:
                    nc.vector.tensor_reduce(MX[:, 2 * j:2 * j + 2, 0], src[:, :].rearrange("p (t k) -> p t k", t=2),
                                            AX.X, ALU.max).then_inc(sem("max_done"), 1)

            def shifts(ph, b, g):
                at = ph.c.at
                dve.wait_ge(sem("max_done"), at("max_done", b, (g + 1) * ph.nm))
                parts = MX[:, :, :] if ph.cross else MX[:, :, 0:1]
                nc.vector.tensor_reduce(NMF[:, :], parts, AX.X, ALU.max, negate=True).then_inc(sem("shift_step"), 1)
                dve.wait_ge(sem("shift_step"), at("shift_step", b, 2 * g + 1))
                nc.vector.tensor_copy(NMB[g % 2][:, :, 0], NMF[:, :]).then_inc(sem("shift_step"), 1)
                dve.wait_ge(sem("shift_step"), at("shift_step", b, 2 * g + 2))
                nc.vector.tensor_tensor(NMB[g % 2][:, :, 1], NMF[:, :], NMB[g % 2][:, :, 0], ALU.subtract).then_inc(
                    sem("shift_ready"), 1)

            def element(el):
                ph, b = el.ph, el.b
                for g in range(NG):
                    ahead = (ph, b, g + 1) if g + 1 < NG else (*el.nxt, 0) if el.nxt else None
                    for t in range(ph.nt):
                        among, behind = el.here(g * ph.nt + t)
                        mine = ahead[0].maximum_at((t, ph.nt)) if ahead else []
                        third = -(-len(mine) // 3)
                        for j in mine[:third]:
                            maximum(*ahead, j)
                        if not ph.cross:
                            for piece_ in among:
                                piece(el, *piece_)
                        for j in mine[third:]:
                            maximum(*ahead, j)
                        if mine and mine[-1] == ahead[0].nm - 1:
                            shifts(*ahead)
                        for piece_ in (among if ph.cross else []) + behind:
                            piece(el, *piece_)

            for ph in plan:
                if isinstance(ph, Phase):
                    if ph.el["before"]:
                        for piece_ in sum(ph.el["before"].here(0), []):
                            piece(ph.el["before"], *piece_)
                        for j in range(ph.nm):
                            maximum(ph, 0, 0, j)
                        shifts(ph, 0, 0)
                    element(ph.el["first"])
                    with dve.Fori(1, B - 1) as i:
                        element(ph.el["middle"](i))
                    element(ph.el["last"])
                    if ph.el["after"]:
                        for piece_ in sum(ph.el["after"].here(0), []):
                            piece(ph.el["after"], *piece_)
                elif isinstance(ph, MlpPhase):
                    mlp_vector(dve, ph)
                else:
                    last_vector(dve, ph)

        @block.gpsimd
        def _(pool):
            pool.wait_ge(sem("cleared"), 1)

            def piece(el, role, name):
                if role != "prep":
                    return
                ph, b = el.nxt
                at = ph.c.at
                if name == "ctx_norm":
                    wait_apart(pool, "ctx_offset", at("ctx_offset", b, 1))
                    for t in range(ph.nt):
                        last = nc.gpsimd.tensor_scalar(CN[:, t, :], CN[:, t, :], CR[:, t:t + 1], CO[:, t:t + 1],
                                                       ALU.mult, ALU.add)
                    last.then_inc(sem("ctx_normed"), 1)
                elif name == "q" or name[0] == "k":
                    units = [(QS, 0, N, 0)] if name == "q" else []
                    if name == "q" and not ph.cross:
                        units.append((KS, 0, N, N))
                    if name[0] == "k":
                        c0, n = CHUNKS[int(name[1])]
                        units.append((KS, c0, n, N + c0))
                    first = 0 if name == "q" else 1 + int(name[1])
                    pool.wait_ge(sem("misc_free"), el.use(role, name) + 1)
                    for k, (dst, c, n, r) in enumerate(units):
                        rest = REST[:, r:r + n]
                        nc.gpsimd.tensor_tensor(rest, rest, dst[:, 0, c:c + n], ALU.subtract).then_inc(
                            sem("rest_done"), 1)
                        wait_apart(pool, "rest_done", at("rest_done", b, first + k + 1))
                        nc.gpsimd.tensor_copy(dst[:, 1, c:c + n], rest).then_inc(sem("mid_done"), 1)
                        pool.wait_ge(sem("mid_done"), at("mid_done", b, first + k + 1))
                        nc.gpsimd.tensor_tensor(dst[:, 2, c:c + n], rest, dst[:, 1, c:c + n],
                                                ALU.subtract).then_inc(sem("low_done"), 1)

            def pack_values(prev, ph, b, g, el):
                at = ph.c.at
                if g == 0:
                    pool.wait_ge(sem("misc_free"), el.use("prep", "v3" if ph.cross else "v0") + 1)
                if g >= 2:
                    wait_apart(pool, "pv_done", at("pv_done", b, (g - 1) * ph.nt))
                elif prev:
                    wait_apart(pool, "pv_done", prev[0].c.at("pv_done", prev[1], (g + 3) * prev[0].nt))
                else:
                    stream_ready(pool, before(ph))
                nc.gpsimd.tensor_copy(
                    VA[g % 2][:, 0:ph.nt, :, 0:HD],
                    VN[:, 0:ph.nt, G * HD * g:G * HD * (g + 1)].rearrange("p t (h d) -> p t h d", d=HD)).then_inc(
                    sem("values_packed"), 1)

            def element(el):
                ph, b = el.ph, el.b
                for g in range(NG):
                    for t in range(ph.nt):
                        for piece_ in sum(el.here(g * ph.nt + t), []):
                            piece(el, *piece_)
                        if g < NG - 1 and t == 1:
                            pack_values(el.prev, ph, b, g + 1, el)
                if el.nxt:
                    pack_values((ph, b), *el.nxt, 0, el)

            for ph in plan:
                if isinstance(ph, Phase):
                    if ph.el["before"]:
                        for piece_ in sum(ph.el["before"].here(0), []):
                            piece(ph.el["before"], *piece_)
                        pack_values(None, ph, 0, 0, ph.el["before"])
                    element(ph.el["first"])
                    with pool.Fori(1, B - 1) as i:
                        element(ph.el["middle"](i))
                    element(ph.el["last"])


def lay_out(a):
    f = np.float32

    def dh(m):
        return m.reshape(m.shape[:-1] + (H, HD)).swapaxes(-1, -2).reshape(m.shape)

    def col(v):
        return v.reshape(-1, D).T

    def row(v):
        return np.broadcast_to(v, (D, v.size))

    def strips(m):
        p = np.zeros((4, 32, NG, m.shape[1]), f)
        p[:, :HD] = m.reshape(NG, 4, HD, -1).transpose(1, 2, 0, 3)
        return p.reshape(128, -1)

    k = np.arange(128)
    main = {"mean": np.full((D, D), 1.0 / D, f), "ident": np.eye(D, dtype=f),
            "pick": (k[:, None] == 32 * np.arange(G)[None, :] + HD).astype(f),
            "eps5": np.full((D, 1), 1e-5, f), "eps6": np.full((D, 1), 1e-6, f), "one": np.ones((D, 1), f)}

    def attention(n, wq, bq, wk, bk, wv, bv, wp, bp):
        main.update({n + "wq": dh(wq), n + "wk": dh(wk), n + "wv": wv, n + "wp": strips(wp), n + "bv": strips(bv[:, None]),
                     n + "bq": col(dh(bq)), n + "bk": col(dh(bk)), n + "bp": col(bp)})

    l0, l1, l2, l3 = ({k[len(p):]: v for k, v in a.items() if k.startswith(p)}
                      for p in ("L0_xcond_", "L1_xcond_", "L2_xcond_", "L3_xcond_"))
    attention("a0", l0["Wq"], l0["bq"], l0["Wkv"][:, :D], l0["bkv"][:D], l0["Wkv"][:, D:], l0["bkv"][D:], l0["Wp"],
              l0["bp"])
    for n, wqkv, bqkv, wp, bp in (("s1", l1["qkv_w"], l1["qkv_b"], l1["sa_proj_w"], l1["sa_proj_b"]),
                                  ("s2", l2["W_qkv"], l2["b_qkv"], l2["W_proj"], l2["b_proj"])):
        attention(n, wqkv[:, :D], bqkv[:D], wqkv[:, D:2 * D], bqkv[D:2 * D], wqkv[:, 2 * D:], bqkv[2 * D:], wp, bp)
    for n, wq, bq, wkv, bkv, wp, bp in (
            ("c1", l1["q_w"], l1["q_b"], l1["kv_w"], l1["kv_b"], l1["ca_proj_w"], l1["ca_proj_b"]),
            ("c2", l2["W_qc"], l2["b_qc"], l2["W_kvc"], l2["b_kvc"], l2["W_cproj"], l2["b_cproj"])):
        attention(n, wq, bq, wkv[:, :D], bkv[:D], wkv[:, D:], bkv[D:], wp, bp)
    for n, w1, b1, w2, b2 in (("m1", l1["fc1_w"], l1["fc1_b"], l1["fc2_w"], l1["fc2_b"]),
                              ("m2", l2["W_mlp1"], l2["b_mlp1"], l2["W_mlp2"], l2["b_mlp2"])):
        main.update({n + "w1": w1, n + "w2": w2.reshape(4, D, D).transpose(1, 0, 2).reshape(D, 4 * D),
                     n + "b1": col(b1), n + "b2": col(b2)})
    thirds = (3, D)
    last = {"wq": l3["Wq"], "wkT": l3["Wk"].T, "wv": l3["Wv"],
            "rw": l3["router_W"].reshape(3, D, E3).transpose(1, 0, 2),
            "ew1": l3["e_w1"].reshape((E3,) + thirds + (2, D)).transpose(2, 1, 0, 3, 4),
            "ew2": l3["e_w2"].reshape(E3, 2, D, D).transpose(2, 0, 1, 3),
            "gw1": l3["gate_w1"].reshape(thirds + (D,)).transpose(1, 0, 2), "gw2": l3["gate_w2"],
            "ow": l3["out_w"], "gamma": col(l3["ln_gamma"]), "beta": col(l3["ln_beta"]), "rb": row(l3["router_b"]),
            "eb1": col(l3["e_b1"]), "eb2": col(l3["e_b2"]), "gb1": col(l3["gate_b1"]), "gb2": col(l3["gate_b2"]),
            "ob": col(l3["out_b"])}
    wm = [l0["Wss_q"], l0["Wss_kv"], l1["adaln_w"], l2["W_mod"]]
    bm = [l0["bss_q"], l0["bss_kv"], l1["adaln_b"], l2["b_mod"]]
    return {
        "x_t": np.ascontiguousarray(a["x"].transpose(2, 0, 1).reshape(D, B * N)),
        "ctx_n": np.ascontiguousarray(a["ctx_1024"]),
        "ctx_t": np.ascontiguousarray(a["ctx_1024"].transpose(0, 2, 1)),
        "w_mod": np.concatenate(wm + [col(b) for b in bm] + [a["cond_1024"].T], axis=1),
        "w_main": np.concatenate([main[n].reshape(D, -1) for n in COLS], axis=1),
        "w_last": np.concatenate([last[n].reshape(D, -1) for n in COLS3], axis=1),
    }


def kernel(**inputs):
    import numpy as _np
    import concourse.bacc as _bacc
    from concourse import mybir as _mybir
    from concourse.bass_utils import run_bass_kernel_spmd as _run

    nc = _bacc.Bacc("TRN2", target_bir_lowering=False, num_devices=1)
    arrays = lay_out({k: _np.asarray(v) for k, v in inputs.items()})
    aps = {n: nc.dram_tensor(n, v.shape, _mybir.dt.from_np(v.dtype), kind="ExternalInput").ap()
           for n, v in arrays.items()}
    out = nc.dram_tensor("out_t", (D, B * N), _mybir.dt.float32, kind="ExternalOutput").ap()
    build(nc, aps["x_t"], aps["ctx_n"], aps["ctx_t"], aps["w_mod"], aps["w_main"], aps["w_last"], out, PHASES)
    r = _run(nc, [arrays], core_ids=[0])
    return _np.ascontiguousarray(r.results[0]["out_t"].reshape(D, B, N).transpose(1, 2, 0))
```

```python
import numpy as np
import concourse.bass as bass
from concourse import mybir
from contextlib import ExitStack


B, N, D = 16, 256, 128
S = 1601
H, HD = 16, 8
G = 4
NG = H // G
R9 = 9 * HD
MR = 96
SCALE = float(HD) ** -0.5
MLPW = 4 * D
RH = 2 * D
E3 = 3
FULL = S // 128
LAST = S - FULL * 128
LN_EXP = "natural_log_exp_and_others"

CHUNKS = [(0, 401), (401, 400), (801, 400), (1201, 400)]
CROSS_TILES = [128] * FULL + [LAST]
SELF_TILES = [128, 128]

M_L0 = dict(scq=0, shq=1, sck=2, shk=3)
M_L1 = dict(sh_a=4, sc_a=5, g_a=6, sh_m=7, sc_m=8, g_m=9)
M_L2 = dict(sh_a=10, sc_a=11, g_a=12, sh_m=13, sc_m=14, g_m=15)
NMOD = 16
MOD_SCALES = (0, 2, 5, 8, 11, 14)

ATT = ["a0", "s1", "c1", "s2", "c2"]
MLP = ["m1", "m2"]
STATS = ["stats%d" % t for t in range(FULL + 1)]
NO_BANK = ["square", "norm", "ctx_scale", "ctx_norm"] + STATS


PHASES = ("a0", "s1", "c1", "m1", "s2", "c2", "m2", "l3")


def _columns():
    cols, at = {}, 0
    main = [("mean", D), ("pick", G), ("ident", D), ("eps5", 1), ("eps6", 1), ("one", 1)]
    for a in ATT:
        main += [(a + "wq", D), (a + "wk", D), (a + "wv", D), (a + "wp", NG * D), (a + "bv", NG),
                 (a + "bq", 1), (a + "bk", 1), (a + "bp", 1)]
    for m in MLP:
        main += [(m + "w1", MLPW), (m + "w2", MLPW), (m + "b1", 4), (m + "b2", 1)]
    for name, n in main:
        cols[name] = (at, n)
        at += n
    last, at3 = {}, 0
    for name, n in [("ew1", 18 * D), ("ew2", 6 * D), ("wq", D), ("wkT", D), ("wv", D), ("rw", 9),
                    ("gw1", 3 * D), ("gw2", D), ("ow", D), ("gamma", 1), ("beta", 1), ("rb", 3),
                    ("eb1", 6), ("eb2", 3), ("gb1", 1), ("gb2", 1), ("ob", 1)]:
        last[name] = (at3, n)
        at3 += n
    return cols, at, last, at3


COLS, NW, COLS3, NW3 = _columns()
SPLIT3 = COLS3["wq"][0]
NWM = NMOD * D + NMOD + B


class Count:

    def __init__(self, start, per, batches):
        self.start, self.per, self.batches = dict(start), per, batches

    def at(self, name, b, k):
        return self.start.get(name, 0) + b * self.per[name] + k

    def after(self):
        return {n: self.start.get(n, 0) + self.batches * p for n, p in self.per.items()}


class Phase:

    def __init__(self, name, start, before):
        self.name, self.before = name, before
        self.cross = name in ("a0", "c1", "c2")
        self.raw = name == "c1"
        self.tiles = CROSS_TILES if self.cross else SELF_TILES
        self.nt = len(self.tiles)
        self.nk = sum(self.tiles)
        self.eps = "eps5" if name == "a0" else "eps6"
        self.mod = {"a0": (0, 1), "s1": (5, 4), "s2": (11, 10)}.get(name)
        self.kvmod = (2, 3) if name == "a0" else None
        self.gate = {"s1": 6, "s2": 12}.get(name)
        self.layer = ATT.index(name)
        self.nm = 2 * G * len(CHUNKS) if self.cross else G
        ctx = self.cross and not self.raw
        if self.cross:
            self.prep = ["mean", "square", "var", "norm", "q"]
            if ctx:
                self.prep += STATS + ["ctx_scale", "ctx_norm", "t0", "t1", "t2", "t3"]
            self.prep += ["k0", "k1", "k2", "k3", "v0", "v1", "v2", "v3"]
        else:
            self.prep = ["mean", "square", "var", "norm", "q", "v0"]
        units = 5 if self.cross else 2
        self.key_stores = [(3, 0, CHUNKS[2][0]), (5, CHUNKS[2][0], S - CHUNKS[2][0])] if self.cross else [(2, 0, N)]
        self.c = Count(start, dict(
            scores_full=2 * self.nt * NG, probs_full=2 * self.nt * NG, pv_done=self.nt * NG,
            heads_copied=NG, group_done=NG, inverse_ready=1, max_full=self.nm * NG, max_done=self.nm * NG,
            shift_step=2 * NG, shift_ready=NG, rows_full=2 * NG, rows_done=2 * NG, values_packed=NG,
            squared=1, rstd_done=1, unit_done=1, normed=1 if self.mod else 0,
            rest_done=units, mid_done=units, low_done=units,
            ctx_loaded=0 if not self.cross else (16 if self.raw else 32),
            stats_done=1 if ctx else 0, stats_read=FULL + 1 if ctx else 0, ctx_log=1 if ctx else 0,
            ctx_rstd=1 if ctx else 0, ctx_offset=1 if ctx else 0, ctx_normed=1 if ctx else 0,
            split_stored=16 + 16 * len(self.key_stores), stream_done=1 if self.gate is not None else 0,
            **{"packed_loaded%d" % g: 64 for g in range(NG)}), B)
        self.shift_tile = self.nt - 2 if self.cross else self.nt - 1

    def after(self):
        return self.c.after()

    def maximum_at(self, slot):
        t, n = slot
        spread = max(n - 2, 1)
        return [j for j in range(self.nm) if min(j * spread // self.nm, n - 1) == t]

    def prep_slots(self, host):
        if host.cross:
            at = dict(mean=0, square=1, var=2, norm=2, q=6, v0=36)
            if self.cross:
                at.update({n: 5 + j * 8 // 13 for j, n in enumerate(STATS)})
                at.update(ctx_scale=12, ctx_norm=12, t0=18, t1=19, k0=20, k1=22, t2=23, t3=24, k2=26, k3=28)
                at.update(v1=38, v2=40, v3=45)
        else:
            at = dict(mean=0, square=0, var=1, norm=1, q=2, v0=5)
            if self.cross:
                at.update({n: 1 for n in STATS})
                at.update(ctx_scale=1, ctx_norm=2, t0=3, t1=3, t2=3, t3=3,
                          k0=4, k1=4, k2=5, k3=5, v0=6, v1=6, v2=7, v3=7)
        return [(at[n], "prep", n) for n in sorted(self.prep, key=lambda n: at[n])]


class Element:

    def __init__(self, ph, b, prev, nxt, misc):
        self.ph, self.b, self.prev, self.nxt, self.misc = ph, b, prev, nxt, misc
        pieces = []
        if ph is None:
            if nxt:
                pieces += [(0, "prep", n) for n in nxt[0].prep]
            if prev:
                pieces += [(0, "post", n) for n in ("d", "e0", "e1", "y")]
        else:
            if prev:
                at = dict(d=3, e0=5, e1=9, y=11) if ph.cross else dict(d=1, e0=3, e1=4, y=4)
                pieces += [(at[n], "post", n) for n in at]
            if nxt:
                pieces += nxt[0].prep_slots(ph)
        self.pieces = sorted(pieces, key=lambda x: x[0])
        self.uses = [(role, n) for _, role, n in self.pieces if n not in NO_BANK]
        self.slots = 1 if ph is None else ph.nt * NG

    def owner(self, role):
        return {"post": self.prev, "prep": self.nxt}[role]

    def use(self, role, name):
        return self.misc + self.uses.index((role, name))

    def here(self, slot):
        found = [(r, n) for s, r, n in self.pieces if s == slot]
        return found[:1], found[1:]


def elements(ph, misc, chained, follows):
    last = B - 1
    out = {}
    out["before"] = None if chained else Element(None, None, None, (ph, 0), misc)
    misc += 0 if chained else len(out["before"].uses)
    out["first"] = Element(ph, 0, (chained, last) if chained else None, (ph, 1), misc)
    misc += len(out["first"].uses)
    n = len(Element(ph, 1, (ph, 0), (ph, 2), 0).uses)
    out["middle"] = lambda i, m=misc: Element(ph, i, (ph, i + -1), (ph, i + 1), m + (i + -1) * n)
    misc += (B - 2) * n
    out["last"] = Element(ph, last, (ph, last - 1), (follows, 0) if follows else None, misc)
    misc += len(out["last"].uses)
    out["after"] = None if follows else Element(None, None, (ph, last), None, misc)
    misc += 0 if follows else len(out["after"].uses)
    return out, misc


class MlpPhase:

    def __init__(self, name, start):
        self.name = name
        self.mod, self.gate = ((8, 7), 9) if name == "m1" else ((14, 13), 15)
        self.c = Count(start, dict(
            mlp_mean=1, mlp_centered=1, mlp_squared=1, mlp_var=1, mlp_log=1, mlp_rstd=1, mlp_unit=1, mlp_normed=1,
            mlp_hidden=4, mlp_act=4, mlp_out=1, mlp_gated=1, stream_done=1), B // 2)

    def after(self):
        return self.c.after()


class LastPhase:

    def __init__(self, start):
        self.start = dict(start)
        norms = dict.fromkeys("""l_mean l_centered l_squared l_var l_log l_rstd l_unit l_normed l_q l_qf l_k
            l_qk""".split(), 1)
        self.c0 = Count(dict(l_centered=1), norms, B // 2)
        one = dict.fromkeys("""l_query l_shift l_shift_high l_shift_low l_rows l_rowed l_heads l_sum l_recip l_spread
            l_weighed l_ev l_evidence l_logits l_logit l_lmax l_lsub l_lexp l_lsum l_lrec l_prob""".split(), 1)
        nt = len(CROSS_TILES)
        one.update(l_max=2 * len(CHUNKS), l_maxed=2 * len(CHUNKS), l_scores=nt, l_probs=nt, l_pv=nt, l_acc=nt, l_pb=2,
                   l_pbc=2)
        self.c = Count({}, one, B)
        two = dict.fromkeys("""l_biases l_g2 l_tanh l_gate l_out l_delta l_stream""".split(), 1)
        two.update(l_hidden=7, l_silu=7, l_expert=3, l_w=3, l_routed=3)
        self.c2 = Count({}, two, B // 2)
        self.tail = dict(sum=1, spread=3, ev=5, logits=7, pb0=10, pb1=12)
        self.maxima = {4 + j: j for j in range(2 * len(CHUNKS))}

    def run(self, engine, step, experts):
        step(0, 0, False, True)
        step(1, 1, True, True)
        with engine.Fori(1, B // 2 - 1) as i:
            step(i * 2, 0, True, True)
            experts(i + -1)
            step(i * 2 + 1, 1, True, True)
        step(B - 2, 0, True, True)
        experts(B // 2 - 2)
        step(B - 1, 1, True, False)


def build(nc, xT, ctxN, ctxT, wmod, wmain, w3, outT, phases):
    f32, bf16 = mybir.dt.float32, mybir.dt.bfloat16
    ALU, ACT, AX = mybir.AluOpType, mybir.ActivationFunctionType, mybir.AxisListType
    ds = bass.ds

    start = dict(probs_full=2, pv_done=2, heads_copied=2, mlp_centered=1, mlp_gated=1)
    start["misc_full"] = 0
    names = {}
    plan = []
    for name in phases:
        before = plan[-1] if plan and isinstance(plan[-1], Phase) else None
        plan.append(Phase(name, start, before) if name in ATT else
                    MlpPhase(name, start) if name in MLP else LastPhase(start))
        if name != "l3":
            start = {**start, **plan[-1].after()}
    misc = 0
    for k, ph in enumerate(plan):
        if isinstance(ph, Phase):
            follows = plan[k + 1] if k + 1 < len(plan) and isinstance(plan[k + 1], Phase) else None
            ph.el, misc = elements(ph, misc, ph.before, follows)
        ph.misc_after = misc

    ctx = ExitStack()
    with ctx:
        def sb(name, shape, dt):
            return ctx.enter_context(nc.sbuf_tensor(name, shape, dt))

        sems = {}

        def sem(name):
            if name not in sems:
                sems[name] = ctx.enter_context(nc.semaphore(name))
            return sems[name]

        def wait(eng, name, n):
            if not (isinstance(n, int) and n <= 0):
                eng.wait_ge(sem(name), n)

        X = sb("X", [D, B * N], f32)
        W = sb("W", [128, NW], f32)
        MODT = sb("MODT", [D, NMOD * B], f32)
        KP = [sb("KP%d" % g, [128, G * S], bf16) for g in range(NG)]
        QP = [sb("QP%d" % g, [128, G * N], bf16) for g in range(NG)]
        VA = [sb("VA%d" % k, [128, len(CROSS_TILES), G, HD + 1], f32) for k in range(2)]
        VN = sb("VN", [128, len(CROSS_TILES), D], f32)
        P = [sb("P%d" % k, [128, G * N], f32) for k in range(2)]
        CN = sb("CN", [128, len(CROSS_TILES), D], f32)
        CT = sb("CT", [D, len(CROSS_TILES) * 128], f32)
        KSF = sb("KSF", [D, 3 * S + 1], bf16)
        KS = KSF[:, 0:3 * S].rearrange("p (r k) -> p r k", r=3)
        QS = sb("QS", [D, 3, N], bf16)
        REST = sb("REST", [D, N + S], f32)
        RS = [sb("RS%d" % g, [128, N], f32) for g in range(NG)]
        ON = [sb("ON%d" % g, [128, N], f32) for g in range(NG)]
        RDN = sb("RDN", [128, 2 * H], f32)
        RDX = sb("RDX", [128, 2 * NG * 128], f32)
        BPT = sb("BPT", [D, len(ATT)], f32)
        XU = sb("XU", [D, N], f32)
        XC = sb("XC", [D, 2 * N], f32)
        SQ = sb("SQ", [D, 2 * N], f32)
        LG = sb("LG", [D, 2 * N], f32)
        RSTD = sb("RSTD", [D, 2 * N], f32)
        XN = sb("XN", [D, 2 * N], f32)
        XM = sb("XM", [D, 2 * N], f32)
        ST = sb("ST", [128, len(CROSS_TILES), 6], f32)
        MV = sb("MV", [128, len(CROSS_TILES), 2], f32)
        CL = sb("CL", [128, len(CROSS_TILES)], f32)
        KVM = sb("KVM", [D, 2], f32)
        CR = sb("CR", [128, len(CROSS_TILES)], f32)
        CO = sb("CO", [128, len(CROSS_TILES)], f32)
        MX = sb("MX", [128, 2 * G, len(CHUNKS)], f32)
        NMF = sb("NMF", [128, 2 * G], f32)
        NMB = [sb("NMB%d" % k, [128, 2 * G, 2], bf16) for k in range(2)]
        XMA = sb("XMA", [D, B * N], f32)
        HM = [P[k][:, r * 2 * N:(r + 1) * 2 * N] for k in range(2) for r in range(2)]
        IDB = sb("IDB", [128, 128], bf16)

        bank = [ctx.enter_context(nc.psum_tensor("bank%d" % k, [128, 512], f32)) for k in range(8)]
        SC, OB, MB, MISC = bank[0:2], bank[2:4], bank[4:7], bank[7]

        scr_k = nc.dram_tensor("scr_k", [3 * HD, H, S], bf16, kind="Internal").ap()
        scr_ks = nc.dram_tensor("scr_ks", [3 * HD, H, N], bf16, kind="Internal").ap()
        scr_q = nc.dram_tensor("scr_q", [3, HD, H, N], bf16, kind="Internal").ap()

        def w(name, k=0, n=None):
            at, width = COLS[name]
            return W[:, at + k:at + (width if n is None else k + n)]

        def modcol(k, b):
            return MODT[:, ds(b + k * B, 1)]

        def xcols(b, n=N):
            return X[:, ds(b * N, n)]

        def wait_apart(eng, name, n):
            eng.wait_ge(sem(name), n)
            eng.sem_inc(sem("passed"), 1)

        def stream_ready(eng, ph):
            if ph is not None:
                wait(eng, "misc_free", ph.misc_after)
                wait(eng, "stream_done", ph.after().get("stream_done", 0))

        def before(ph):
            k = plan.index(ph)
            return plan[k - 1] if k else None

        WM = sb("WM", [D, NWM], f32)
        CND = sb("CND", [D, 3 * B], f32)

        W3A = KP[0][:, :].bitcast(f32)[:, 0:SPLIT3]
        W3B = KP[1][:, :].bitcast(f32)[:, 0:NW3 - SPLIT3]
        HID = [KP[2][:, :].bitcast(f32)[:, u * 2 * N:(u + 1) * 2 * N] for u in range(6)]
        T3 = KP[3][:, :].bitcast(f32)
        HID.append(T3[:, 0:2 * N])
        PB = T3[:, 2 * N:8 * N].rearrange("p (e q) -> p e q", e=E3)
        NX = T3[:, 8 * N:10 * N]
        EV = T3[:, 10 * N:12 * N]
        CTX_N = [CN, VN]
        CTX_T = [CT[:, :], KSF[:, :].bitcast(f32)]
        ACC = [SQ[:, r * N:(r + 1) * N] for r in range(2)]
        QKS = [REST[:, r * N:(r + 1) * N] for r in range(2)]
        OBS = REST[:, 2 * N:3 * N]
        QKA = W[:, COLS["a0wq"][0]:COLS["a0wq"][0] + B * N]
        ROW = [sb("ROW%d" % r, [2, N], bf16) for r in range(2)]
        ONE2 = sb("ONE2", [2, 128], bf16)
        EA = sb("EA", [D, 7 * B], f32)
        EAP = sb("EAP", [D, 7, 2], f32)
        RA = sb("RA", [D, B * E3], f32)
        HGB = sb("HGB", [D, 1], f32)
        RD = sb("RD", [128, 2], f32)
        LT = sb("LT", [128, 5, 2 * E3], f32)
        COND = WM[:, NMOD * (D + 1):NWM]

        def w3c(name, k=0, n=None):
            at, width = COLS3[name]
            src, at = (W3A, at) if at < SPLIT3 else (W3B, at - SPLIT3)
            return src[:, at + k:at + (width if n is None else k + n)]

        XCS, SQS = [XC[:, :], P[0][:, 0:2 * N]], [SQ[:, :], P[0][:, 2 * N:4 * N]]
        LGS, RSTDS = [LG[:, :], P[1][:, 0:2 * N]], [RSTD[:, :], P[1][:, 2 * N:4 * N]]
        XNS, XMS = [XN[:, :], REST[:, 0:2 * N]], [XM[:, :], REST[:, 2 * N:4 * N]]

        def mlp_tensor(pe, ph):
            at = ph.c.at
            stream_ready(pe, before(ph))
            with pe.Fori(0, B // 4) as q:
                pe.wait_ge(sem("mlp_centered"), at("mlp_centered", q * 2, 0))
                for k in range(2):
                    nc.tensor.matmul(bank[k][:, :], w("mean"), X[:, ds(q * 4 * N + k * 2 * N, 2 * N)], start=True,
                                     stop=True).then_inc(sem("mlp_mean"), 1)
                for k in range(2):
                    pe.wait_ge(sem("mlp_squared"), at("mlp_squared", q * 2, k + 1))
                    nc.tensor.matmul(bank[2 + k][:, :], w("mean"), SQS[k], start=True, stop=True).then_inc(
                        sem("mlp_var"), 1)
            with pe.Fori(0, B // 2) as i:
                pe.wait_ge(sem("mlp_normed"), at("mlp_normed", B // 2 - 1, 1))
                for c in range(4):
                    if c == 0:
                        pe.wait_ge(sem("mlp_gated"), at("mlp_gated", i, 0))
                    nc.tensor.matmul(bank[2 + c][:, :], w(ph.name + "w1", c * D, D), XMA[:, ds(i * 2 * N, 2 * N)],
                                     start=True, stop=True).then_inc(sem("mlp_hidden"), 1)
                for c in range(4):
                    pe.wait_ge(sem("mlp_act"), at("mlp_act", i, c + 1))
                    last = nc.tensor.matmul(bank[6][:, :], w(ph.name + "w2", c * D, D), HM[c], start=(c == 0),
                                            stop=(c == 3))
                last.then_inc(sem("mlp_out"), 1)

        def mlp_scalar(act, ph):
            at = ph.c.at
            with act.Fori(0, B // 4) as q:
                for k in range(2):
                    act.wait_ge(sem("mlp_centered"), at("mlp_centered", q * 2, k + 1))
                    nc.scalar.activation(SQS[k], XCS[k], ACT.Square).then_inc(sem("mlp_squared"), 1)
                for k in range(2):
                    act.wait_ge(sem("mlp_var"), at("mlp_var", q * 2, k + 1))
                    nc.scalar.activation(LGS[k], bank[2 + k][:, :], ACT.Ln, bias=w("eps6")).then_inc(
                        sem("mlp_log"), 1)
                    act.wait_ge(sem("mlp_log"), at("mlp_log", q * 2, k + 1))
                    nc.scalar.activation(RSTDS[k], LGS[k], ACT.Exp, scale=-0.5).then_inc(sem("mlp_rstd"), 1)
            nc.scalar.preload_act_table(ACT.Gelu_apprx_tanh)
            with act.Fori(0, B // 2) as i:
                for c in range(4):
                    act.wait_ge(sem("mlp_hidden"), at("mlp_hidden", i, c + 1))
                    nc.scalar.activation(HM[c], bank[2 + c][:, :], ACT.Gelu_apprx_tanh,
                                         bias=w(ph.name + "b1", c, 1)).then_inc(sem("mlp_act"), 1)
            nc.scalar.preload_act_table_set(LN_EXP)

        def mlp_vector(dve, ph):
            at = ph.c.at
            with dve.Fori(0, B // 4) as q:
                for k in range(2):
                    dve.wait_ge(sem("mlp_mean"), at("mlp_mean", q * 2, k + 1))
                    nc.vector.tensor_tensor(XCS[k], X[:, ds(q * 4 * N + k * 2 * N, 2 * N)], bank[k][:, :],
                                            ALU.subtract).then_inc(sem("mlp_centered"), 1)
                for k in range(2):
                    dve.wait_ge(sem("mlp_rstd"), at("mlp_rstd", q * 2, k + 1))
                    nc.vector.tensor_tensor(XNS[k], XCS[k], RSTDS[k], ALU.mult).then_inc(sem("mlp_unit"), 1)
                    dve.wait_ge(sem("mlp_unit"), at("mlp_unit", q * 2, k + 1))
                    for r in range(2):
                        b = q * 4 + (2 * k + r)
                        last = nc.vector.tensor_scalar(XMA[:, ds(b * N, N)], XNS[k][:, r * N:(r + 1) * N],
                                                       modcol(ph.mod[0], b), modcol(ph.mod[1], b), ALU.mult, ALU.add)
                    last.then_inc(sem("mlp_normed"), 1)
                dve.wait_ge(sem("mlp_normed"), at("mlp_normed", q * 2, 2))
            with dve.Fori(0, B // 2) as i:
                dve.wait_ge(sem("mlp_out"), at("mlp_out", i, 1))
                for r in range(2):
                    last = nc.vector.tensor_scalar(XC[:, r * N:(r + 1) * N], bank[6][:, r * N:(r + 1) * N],
                                                   w(ph.name + "b2"), modcol(ph.gate, i * 2 + r), ALU.add, ALU.mult)
                last.then_inc(sem("mlp_gated"), 1)
                dve.wait_ge(sem("mlp_gated"), at("mlp_gated", i, 1))
                nc.vector.tensor_tensor(X[:, ds(i * 2 * N, 2 * N)], X[:, ds(i * 2 * N, 2 * N)], XC[:, :],
                                        ALU.add).then_inc(sem("stream_done"), 1)
                dve.wait_ge(sem("stream_done"), at("stream_done", i, 1))

        def last_pair(i):
            return isinstance(i, int) and i == B // 2 - 1

        def last_sync(sp, ph):
            at, at2 = ph.c.at, ph.c2.at

            def load(b, r):
                sp.dma_start(CTX_T[r][:, 0:S], ctxT[ds(b, 1)].rearrange("o d s -> (o d) s")).then_inc(
                    sem("l_ctxT%d" % r), 16)
                sp.dma_start(CTX_N[r][:, 0:FULL, :], ctxN[ds(b, 1), 0:FULL * 128, :].rearrange(
                    "o (t p) d -> (o p) t d", p=128)).then_inc(sem("l_ctx%d" % r), 16)
                sp.dma_start(CTX_N[r][0:LAST, FULL, :], ctxN[ds(b, 1), FULL * 128:S, :].rearrange(
                    "o p d -> (o p) d")).then_inc(sem("l_ctx%d" % r), 16)

            def store(i):
                sp.wait_ge(sem("l_stream"), at2("l_stream", i, 1))
                sp.dma_start(outT[:, ds(i * 2 * N, 2 * N)], X[:, ds(i * 2 * N, 2 * N)]).then_inc(
                    sem("out_stored"), 16)

            c2 = [p for p in plan if isinstance(p, Phase)][-1]
            stream_ready(sp, c2)
            for r in range(2):
                load(r, r)
            for r in range(2):
                sp.wait_ge(sem("l_pv"), at("l_pv", r, len(CROSS_TILES)))
                load(2 + r, r)
            with sp.Fori(1, B // 2 - 1) as i:
                for r in range(2):
                    sp.wait_ge(sem("l_pv"), at("l_pv", i * 2 + r, len(CROSS_TILES)))
                    load(i * 2 + (2 + r), r)
                store(i + -1)
            store(B // 2 - 2)
            store(B // 2 - 1)
            sp.wait_ge(sem("out_stored"), 16 * (B // 2))

        def last_tensor(pe, ph):
            at, at2 = ph.c.at, ph.c2.at
            stream_ready(pe, before(ph))
            pe.wait_ge(sem("last_weights"), 32)
            for u in range(7):
                for_anchor = w3c("ew1", (2 * E3 + u // 2) * 2 * D + (u % 2) * D, D) if u < 6 else w3c("gw1", 2 * D, D)
                nc.tensor.matmul(bank[0][:, u * B:(u + 1) * B], for_anchor, COND, start=True, stop=True)
            for b in range(B):
                last = nc.tensor.matmul(bank[1][:, b * E3:(b + 1) * E3], COND[:, b:b + 1].to_broadcast([D, 128]),
                                        w3c("rw", 6, 3), start=True, stop=True)
            last.then_inc(sem("l_anchor"), 1)
            pe.wait_ge(sem("l_anchored"), 1)

            def norms(q):
                at0 = ph.c0.at
                pe.wait_ge(sem("l_centered"), at0("l_centered", q * 2, 0))
                for k in range(2):
                    nc.tensor.matmul(bank[k][:, :], w("mean"), X[:, ds(q * 4 * N + k * 2 * N, 2 * N)], start=True,
                                     stop=True).then_inc(sem("l_mean"), 1)
                for name, after, first in (("l_var", "l_squared", 2), ("l_q", "l_normed", 4), ("l_k", "l_qf", 6)):
                    for k in range(2):
                        lhsT, rhs = {"l_var": (w("mean"), SQS[k]), "l_k": (w3c("wkT"), XMS[k]),
                                     "l_q": (w3c("wq"), XMA[:, ds(q * 4 * N + k * 2 * N, 2 * N)])}[name]
                        pe.wait_ge(sem(after), at0(after, q * 2, k + 1))
                        nc.tensor.matmul(bank[first + k][:, :], lhsT, rhs, start=True, stop=True).then_inc(
                            sem(name), 1)

            def maximum(b, r, j):
                if j == 0:
                    pe.wait_ge(sem("l_query"), at("l_query", b, 1))
                    pe.wait_ge(sem("l_ctxT%d" % r), (b - r) * 8 + 16)
                    wait(pe, "l_rowed", at("l_rowed", b, 0))
                else:
                    wait(pe, "l_maxed", at("l_maxed", b, j - len(MB) + 1))
                qt, (c0, n) = j // len(CHUNKS), CHUNKS[j % len(CHUNKS)]
                nc.tensor.matmul(MB[j % 3][:, 0:n], QKS[r][:, qt * 128:(qt + 1) * 128], CTX_T[r][:, c0:c0 + n],
                                 start=True, stop=True).then_inc(sem("l_max"), 1)

            def rows(b, r):
                pe.wait_ge(sem("l_shift_low"), at("l_shift_low", b, 1))
                for qt in range(2):
                    last = nc.tensor.matmul(MB[2][0:2, qt * 128:(qt + 1) * 128], NMB[r][:, qt, :], IDB[:, :],
                                            start=True, stop=True)
                last.then_inc(sem("l_rows"), 1)

            def tail(b, r, t):
                if t == ph.tail["sum"]:
                    pe.wait_ge(sem("l_acc"), at("l_acc", b, len(CROSS_TILES)))
                    wait(pe, "l_pbc", at("l_pbc", b, 0))
                    for qt in range(2):
                        last = nc.tensor.matmul(MISC[:, qt:qt + 1], ACC[r][:, qt * 128:(qt + 1) * 128], w("one"),
                                                start=True, stop=True)
                    last.then_inc(sem("l_sum"), 1)
                elif t == ph.tail["spread"]:
                    pe.wait_ge(sem("l_recip"), at("l_recip", b, 1))
                    for qt in range(2):
                        last = nc.tensor.matmul(MISC[:, qt * 128:(qt + 1) * 128],
                                                RD[:, qt:qt + 1].to_broadcast([128, 128]), w("ident"), start=True,
                                                stop=True)
                    last.then_inc(sem("l_spread"), 1)
                elif t == ph.tail["ev"]:
                    pe.wait_ge(sem("l_weighed"), at("l_weighed", b, 1))
                    nc.tensor.matmul(MISC[:, 0:N], w3c("wv"), XN[:, 0:N], start=True, stop=True).then_inc(
                        sem("l_ev"), 1)
                elif t == ph.tail["logits"]:
                    pe.wait_ge(sem("l_evidence"), at("l_evidence", b, 1))
                    for qt in range(2):
                        q = slice(r * N + qt * 128, r * N + (qt + 1) * 128)
                        nc.tensor.matmul(MISC[:, qt * E3:(qt + 1) * E3], NX[:, q], w3c("rw", 0, 3), start=True,
                                         stop=False)
                        last = nc.tensor.matmul(MISC[:, qt * E3:(qt + 1) * E3], EV[:, q], w3c("rw", 3, 3), start=False,
                                                stop=True)
                    last.then_inc(sem("l_logits"), 1)
                elif t in (ph.tail["pb0"], ph.tail["pb1"]):
                    second = t == ph.tail["pb1"]
                    pe.wait_ge(sem("l_prob"), at("l_prob", b, 1))
                    if second:
                        pe.wait_ge(sem("l_pbc"), at("l_pbc", b, 1))
                    for e in ((2,) if second else (0, 1)):
                        for qt in range(2):
                            c = (e % 2) * N + qt * 128
                            last = nc.tensor.matmul(MISC[:, c:c + 128],
                                                    LT[:, 4, qt * E3 + e:qt * E3 + e + 1].to_broadcast([128, 128]),
                                                    w("ident"), start=True, stop=True)
                    last.then_inc(sem("l_pb"), 1)

            def step(b, r, prev, ahead):
                kn, kT = CTX_N[r], CTX_T[r]
                for t in range(len(CROSS_TILES) + 1):
                    if t == 0:
                        pe.wait_ge(sem("l_rowed"), at("l_rowed", b, 1))
                        pe.wait_ge(sem("l_ctx%d" % r), (b - r) * 16 + 32)
                    if t < len(CROSS_TILES):
                        kt, v = CROSS_TILES[t], r * len(CROSS_TILES) + t
                        wait(pe, "l_probs", at("l_probs", b, t - 1))
                        nc.tensor.matmul(SC[v % 2][0:kt, 0:N], kT[:, t * 128:t * 128 + kt], QKS[r], start=True,
                                         stop=False)
                        nc.tensor.matmul(SC[v % 2][0:kt, 0:N], ONE2[:, 0:kt], ROW[r][:, :], start=False,
                                         stop=True).then_inc(sem("l_scores"), 1)
                    if t:
                        kt, v = CROSS_TILES[t - 1], r * len(CROSS_TILES) + t - 1
                        if t == 1:
                            wait(pe, "l_heads", at("l_heads", b, 0))
                        pe.wait_ge(sem("l_probs"), at("l_probs", b, t))
                        nc.tensor.matmul(OB[0][:, 0:N], kn[0:kt, t - 1, :], P[v % 2][0:kt, 0:N], start=(t == 1),
                                         stop=(t == len(CROSS_TILES))).then_inc(sem("l_pv"), 1)
                    if ahead and t in ph.maxima:
                        maximum(b + 1, 1 - r, ph.maxima[t])
                    if prev:
                        tail(b - 1, 1 - r, t)
                if ahead:
                    rows(b + 1, 1 - r)

            def experts(i):
                pe.wait_ge(sem("l_heads"), at("l_heads", i * 2, 2 if last_pair(i) else 3))
                pe.wait_ge(sem("l_rowed"), at("l_rowed", i * 2, 2 if last_pair(i) else 4))
                pe.wait_ge(sem("l_pbc"), at("l_pbc", i * 2, 4))
                for u in range(7):
                    for k, src in ((0, NX), (1, EV)):
                        wt = w3c("ew1", (k * E3 + u // 2) * 2 * D + (u % 2) * D, D) if u < 6 else w3c("gw1", k * D, D)
                        last = nc.tensor.matmul(bank[u][:, :], wt, src[:, :], start=(k == 0), stop=(k == 1))
                    last.then_inc(sem("l_hidden"), 1)
                for e in range(E3):
                    pe.wait_ge(sem("l_silu"), at2("l_silu", i, 2 * e + 2))
                    for k in range(2):
                        last = nc.tensor.matmul(bank[(7, 0, 1)[e]][:, :], w3c("ew2", (2 * e + k) * D, D), HID[2 * e + k],
                                                start=(k == 0), stop=(k == 1))
                    last.then_inc(sem("l_expert"), 1)
                pe.wait_ge(sem("l_silu"), at2("l_silu", i, 7))
                nc.tensor.matmul(bank[3][:, :], w3c("gw2"), HID[6], start=True, stop=True).then_inc(sem("l_g2"), 1)
                pe.wait_ge(sem("l_routed"), at2("l_routed", i, 3))
                nc.tensor.matmul(bank[4][:, :], w3c("ow"), XN[:, :], start=True, stop=True).then_inc(sem("l_out"), 1)
                pe.wait_ge(sem("l_stream"), at2("l_stream", i, 1))

            with pe.Fori(0, B // 4) as q:
                norms(q)
            for j in range(2 * len(CHUNKS)):
                maximum(0, 0, j)
            rows(0, 0)
            ph.run(pe, step, experts)
            for t in range(len(CROSS_TILES)):
                tail(B - 1, 1, t)
            experts(B // 2 - 1)

        def last_scalar(act, ph):
            at, at2 = ph.c.at, ph.c2.at

            def one(at, b, name, after, k, *args, **kw):
                act.wait_ge(sem(after), at(after, b, k))
                nc.scalar.activation(*args, **kw).then_inc(sem(name), 1)

            def norms(q):
                at0 = ph.c0.at
                for k in range(2):
                    one(at0, q * 2, "l_squared", "l_centered", k + 1, SQS[k], XCS[k], ACT.Square)
                for k in range(2):
                    one(at0, q * 2, "l_log", "l_var", k + 1, LGS[k], bank[2 + k][:, :], ACT.Ln, bias=w("eps5"))
                    one(at0, q * 2, "l_rstd", "l_log", k + 1, RSTDS[k], LGS[k], ACT.Exp, scale=-0.5)
                for k in range(2):
                    one(at0, q * 2, "l_qf", "l_q", k + 1, XMS[k], bank[4 + k][:, :], ACT.Copy)

            def row(b, r):
                one(at, b, "l_rowed", "l_rows", 1, ROW[r][:, :], MB[2][0:2, 0:N], ACT.Copy)

            def tail(b, r, t):
                half = slice(r * N, (r + 1) * N)
                if t == ph.tail["ev"]:
                    one(at, b, "l_evidence", "l_ev", 1, EV[:, half], MISC[:, 0:N], ACT.Copy)
                elif t == ph.tail["logits"]:
                    one(at, b, "l_lexp", "l_lsub", 1, LT[:, 2, :], LT[:, 1, :], ACT.Exp)
                elif t == ph.tail["pb0"]:
                    one(at, b, "l_pbc", "l_pb", 1, PB[:, 0:2, half], MISC[:, :].rearrange("p (e q) -> p e q", e=2),
                        ACT.Copy)
                elif t == ph.tail["pb1"]:
                    one(at, b, "l_pbc", "l_pb", 2, PB[:, 2, half], MISC[:, 0:N], ACT.Copy)

            def step(b, r, prev, ahead):
                for t, kt in enumerate(CROSS_TILES):
                    v = r * len(CROSS_TILES) + t
                    wait(act, "l_pv", at("l_pv", b, t - 1))
                    wait(act, "l_acc", at("l_acc", b, t - 1))
                    one(at, b, "l_probs", "l_scores", t + 1, P[v % 2][0:kt, 0:N], SC[v % 2][0:kt, 0:N], ACT.Exp,
                        scale=float(D) ** -0.5)
                    if prev:
                        tail(b - 1, 1 - r, t)
                wait(act, "l_weighed", at("l_weighed", b, 0))
                one(at, b, "l_heads", "l_pv", len(CROSS_TILES), OBS, OB[0][:, 0:N], ACT.Copy)
                if ahead:
                    row(b + 1, 1 - r)

            def experts(i):
                nc.scalar.preload_act_table(ACT.Silu)
                act.wait_ge(sem("l_biases"), at2("l_biases", i, 1))
                for u in range(7):
                    act.wait_ge(sem("l_hidden"), at2("l_hidden", i, u + 1))
                    for r in range(2):
                        last = nc.scalar.activation(HID[u][:, r * N:(r + 1) * N], bank[u][:, r * N:(r + 1) * N],
                                                    ACT.Silu, bias=EAP[:, u, r:r + 1])
                    last.then_inc(sem("l_silu"), 1)
                act.wait_ge(sem("l_g2"), at2("l_g2", i, 1))
                nc.scalar.activation(LG[:, :], bank[3][:, :], ACT.Tanh, bias=HGB[:, :], scale=0.5).then_inc(
                    sem("l_tanh"), 1)
                nc.scalar.preload_act_table_set(LN_EXP)

            with act.Fori(0, B // 4) as q:
                norms(q)
            row(0, 0)
            ph.run(act, step, experts)
            for t in range(len(CROSS_TILES)):
                tail(B - 1, 1, t)
            experts(B // 2 - 1)

        def last_vector(dve, ph):
            at, at2 = ph.c.at, ph.c2.at
            dve.wait_ge(sem("l_anchor"), 1)
            nc.vector.tensor_tensor(EA[:, 0:6 * B].rearrange("p (u b) -> p u b", b=B),
                                    bank[0][:, 0:6 * B].rearrange("p (u b) -> p u b", b=B),
                                    w3c("eb1").unsqueeze(2).to_broadcast([D, 6, B]), ALU.add)
            nc.vector.tensor_scalar(EA[:, 6 * B:7 * B], bank[0][:, 6 * B:7 * B], w3c("gb1"), None, ALU.add)
            nc.vector.tensor_tensor(RA[:, :].rearrange("p (b e) -> p b e", e=E3),
                                    bank[1][:, 0:B * E3].rearrange("p (b e) -> p b e", e=E3),
                                    w3c("rb").unsqueeze(1).to_broadcast([D, B, E3]), ALU.add)
            nc.vector.memset(ONE2[:, :], 1.0)
            nc.vector.tensor_scalar(HGB[:, :], w3c("gb2"), 0.5, None, ALU.mult).then_inc(sem("l_anchored"), 1)
            dve.wait_ge(sem("l_anchored"), 1)

            def norms(q):
                def after(name, k):
                    dve.wait_ge(sem(name), ph.c0.at(name, q * 2, k + 1))

                for k in range(2):
                    after("l_mean", k)
                    nc.vector.tensor_tensor(XCS[k], X[:, ds(q * 4 * N + k * 2 * N, 2 * N)], bank[k][:, :],
                                            ALU.subtract).then_inc(sem("l_centered"), 1)
                for k in range(2):
                    after("l_rstd", k)
                    nc.vector.tensor_tensor(XNS[k], XCS[k], RSTDS[k], ALU.mult).then_inc(sem("l_unit"), 1)
                    after("l_unit", k)
                    nc.vector.tensor_scalar(XMA[:, ds(q * 4 * N + k * 2 * N, 2 * N)], XNS[k], w3c("gamma"),
                                            w3c("beta"), ALU.mult, ALU.add).then_inc(sem("l_normed"), 1)
                for k in range(2):
                    after("l_k", k)
                    nc.vector.tensor_scalar(QKA[:, ds(q * 4 * N + k * 2 * N, 2 * N)], bank[6 + k][:, :], 1.0, None,
                                            ALU.mult).then_inc(sem("l_qk"), 1)
                after("l_normed", 1)

            def after_b(b, name, k=1):
                dve.wait_ge(sem(name), at(name, b, k))

            def query(b, r):
                nc.vector.tensor_scalar(QKS[r], QKA[:, ds(b * N, N)], 1.0, None, ALU.mult).then_inc(sem("l_query"), 1)

            def maximum(b, r, j):
                qt, c = j // len(CHUNKS), j % len(CHUNKS)
                after_b(b, "l_max", j + 1)
                nc.vector.tensor_reduce(MX[:, qt, c:c + 1], MB[j % 3][:, 0:CHUNKS[c][1]], AX.X, ALU.max).then_inc(
                    sem("l_maxed"), 1)

            def shifts(b, r):
                after_b(b, "l_maxed", 2 * len(CHUNKS))
                nc.vector.tensor_reduce(NMF[:, 0:2], MX[:, 0:2, :], AX.X, ALU.max, negate=True).then_inc(
                    sem("l_shift"), 1)
                after_b(b, "l_shift")
                nc.vector.tensor_copy(NMB[r][:, 0:2, 0], NMF[:, 0:2]).then_inc(sem("l_shift_high"), 1)
                after_b(b, "l_shift_high")
                nc.vector.tensor_tensor(NMB[r][:, 0:2, 1], NMF[:, 0:2], NMB[r][:, 0:2, 0], ALU.subtract).then_inc(
                    sem("l_shift_low"), 1)

            def tail(b, r, t):
                def after(name, k=1):
                    after_b(b, name, k)

                if t == ph.tail["sum"]:
                    after("l_sum")
                    nc.vector.reciprocal(RD[:, :], MISC[:, 0:2]).then_inc(sem("l_recip"), 1)
                    nc.vector.tensor_scalar(NX[:, r * N:(r + 1) * N], XMA[:, ds(b * N, N)], 1.0, None, ALU.mult)
                elif t == ph.tail["spread"]:
                    after("l_heads")
                    after("l_spread")
                    nc.vector.tensor_tensor(XN[:, 0:N], OBS, MISC[:, 0:N], ALU.mult).then_inc(sem("l_weighed"), 1)
                elif t == ph.tail["logits"]:
                    after("l_logits")
                    nc.vector.tensor_tensor(LT[:, 0, :].rearrange("p (t e) -> p t e", e=E3),
                                            MISC[:, 0:2 * E3].rearrange("p (t e) -> p t e", e=E3),
                                            RA[:, ds(b * E3, E3)].unsqueeze(1).to_broadcast([128, 2, E3]),
                                            ALU.add).then_inc(sem("l_logit"), 1)
                    after("l_logit")
                    nc.vector.tensor_reduce(LT[:, 3, 0:2], LT[:, 0, :].rearrange("p (t e) -> p t e", e=E3), AX.X,
                                            ALU.max).then_inc(sem("l_lmax"), 1)
                    after("l_lmax")
                    nc.vector.tensor_tensor(LT[:, 1, :].rearrange("p (t e) -> p t e", e=E3),
                                            LT[:, 0, :].rearrange("p (t e) -> p t e", e=E3),
                                            LT[:, 3, 0:2].unsqueeze(2).to_broadcast([128, 2, E3]),
                                            ALU.subtract).then_inc(sem("l_lsub"), 1)
                elif t == ph.tail["logits"] + 1:
                    after("l_lexp")
                    nc.vector.tensor_reduce(LT[:, 3, 2:4], LT[:, 2, :].rearrange("p (t e) -> p t e", e=E3), AX.X,
                                            ALU.add).then_inc(sem("l_lsum"), 1)
                    after("l_lsum")
                    nc.vector.reciprocal(LT[:, 3, 4:6], LT[:, 3, 2:4]).then_inc(sem("l_lrec"), 1)
                    after("l_lrec")
                    nc.vector.tensor_tensor(LT[:, 4, :].rearrange("p (t e) -> p t e", e=E3),
                                            LT[:, 2, :].rearrange("p (t e) -> p t e", e=E3),
                                            LT[:, 3, 4:6].unsqueeze(2).to_broadcast([128, 2, E3]),
                                            ALU.mult).then_inc(sem("l_prob"), 1)

            def step(b, r, prev, ahead):
                if ahead:
                    if prev:
                        after_b(b - 1, "l_pv", len(CROSS_TILES))
                    query(b + 1, 1 - r)
                for t, kt in enumerate(CROSS_TILES):
                    v = r * len(CROSS_TILES) + t
                    after_b(b, "l_probs", t + 1)
                    if t == 0:
                        nc.vector.tensor_copy(ACC[r], P[v % 2][:, 0:N]).then_inc(sem("l_acc"), 1)
                    else:
                        after_b(b, "l_acc", t)
                        nc.vector.tensor_tensor(ACC[r][0:kt, :], ACC[r][0:kt, :], P[v % 2][0:kt, 0:N],
                                                ALU.add).then_inc(sem("l_acc"), 1)
                    if ahead and t in ph.maxima:
                        maximum(b + 1, 1 - r, ph.maxima[t])
                        if ph.maxima[t] == 2 * len(CHUNKS) - 1:
                            shifts(b + 1, 1 - r)
                    if prev:
                        tail(b - 1, 1 - r, t)

            def experts(i):
                nc.vector.tensor_scalar(EAP[:, :, :], EA[:, :].rearrange("p (u b) -> p u b", b=B)[:, :, ds(i * 2, 2)],
                                        1.0, None, ALU.mult).then_inc(sem("l_biases"), 1)
                for e in range(E3):
                    dve.wait_ge(sem("l_expert"), at2("l_expert", i, e + 1))
                    dst = XN if e == 0 else (XC, XM)[e - 1]
                    nc.vector.scalar_tensor_tensor(out=dst[:, :], in0=bank[(7, 0, 1)[e]][:, :], scalar=w3c("eb2", e, 1),
                                                   in1=PB[:, e, :], op0=ALU.add, op1=ALU.mult).then_inc(sem("l_w"), 1)
                dve.wait_ge(sem("l_w"), at2("l_w", i, 3))
                nc.vector.tensor_tensor(XC[:, :], XC[:, :], XM[:, :], ALU.add).then_inc(sem("l_routed"), 1)
                dve.wait_ge(sem("l_routed"), at2("l_routed", i, 1))
                nc.vector.tensor_tensor(XN[:, :], XN[:, :], XC[:, :], ALU.add).then_inc(sem("l_routed"), 2)
                dve.wait_ge(sem("l_tanh"), at2("l_tanh", i, 1))
                nc.vector.tensor_scalar(RSTD[:, :], LG[:, :], 0.5, 0.5, ALU.mult, ALU.add).then_inc(sem("l_gate"), 1)
                dve.wait_ge(sem("l_gate"), at2("l_gate", i, 1))
                dve.wait_ge(sem("l_out"), at2("l_out", i, 1))
                nc.vector.scalar_tensor_tensor(out=XC[:, :], in0=bank[4][:, :], scalar=w3c("ob"), in1=RSTD[:, :],
                                               op0=ALU.add, op1=ALU.mult).then_inc(sem("l_delta"), 1)
                dve.wait_ge(sem("l_delta"), at2("l_delta", i, 1))
                nc.vector.tensor_tensor(X[:, ds(i * 2 * N, 2 * N)], X[:, ds(i * 2 * N, 2 * N)], XC[:, :],
                                        ALU.add).then_inc(sem("l_stream"), 1)
                dve.wait_ge(sem("l_stream"), at2("l_stream", i, 1))

            with dve.Fori(0, B // 4) as q:
                norms(q)
            dve.wait_ge(sem("l_qk"), B // 2)
            query(0, 0)
            for j in range(2 * len(CHUNKS)):
                maximum(0, 0, j)
            shifts(0, 0)
            ph.run(dve, step, experts)
            for t in range(len(CROSS_TILES)):
                tail(B - 1, 1, t)
            experts(B // 2 - 1)

        block = ctx.enter_context(nc.Block())

        @block.sync
        def _(sp):
            sp.dma_start(WM[:, :], wmod).then_inc(sem("wmod_loaded"), 16)
            first = COLS["s1wq"][0]
            sp.dma_start(W[:, 0:first], wmain[:, 0:first]).then_inc(sem("weights_loaded"), 16)
            sp.dma_start(X[:, 0:2 * N], xT[:, 0:2 * N]).then_inc(sem("x_loaded"), 16)

            def prepare(el):
                ph, b = el.nxt
                at = ph.c.at
                if ph.cross:
                    wait(sp, "misc_full", el.misc)
                    if ph.raw:
                        sp.dma_start(CT[:, 0:S], ctxT[ds(b, 1)].rearrange("o d s -> (o d) s")).then_inc(
                            sem("ctx_loaded"), 16)
                    else:
                        sp.dma_start(CN[:, 0:FULL, :], ctxN[ds(b, 1), 0:FULL * 128, :].rearrange(
                            "o (p t) d -> (o p) t d", t=FULL)).then_inc(sem("ctx_loaded"), 16)
                        sp.dma_start(CN[0:LAST, FULL, :], ctxN[ds(b, 1), FULL * 128:S, :].rearrange(
                            "o p d -> (o p) d")).then_inc(sem("ctx_loaded"), 16)
                if el is plan[0].el["before"]:
                    sp.dma_start(X[:, 2 * N:B * N], xT[:, 2 * N:B * N]).then_inc(sem("rest_loaded"), 16)
                    sp.dma_start(W[:, first:NW], wmain[:, first:NW]).then_inc(sem("rest_loaded"), 16)
                for g in range(NG):
                    wait(sp, "packed_loaded%d" % g, at("packed_loaded%d" % g, b, 0))
                sp.wait_ge(sem("low_done"), at("low_done", b, 1))
                sp.dma_start(scr_q.rearrange("a d h q -> (d h) a q"), QS[:, :, :]).then_inc(sem("split_stored"), 16)
                kscr = scr_k if ph.cross else scr_ks
                for made, k0, n in ph.key_stores:
                    sp.wait_ge(sem("low_done"), at("low_done", b, made))
                    sp.dma_start(kscr[:, :, k0:k0 + n].rearrange("(r d) h k -> (d h) r k", r=3),
                                 KS[:, :, k0:k0 + n]).then_inc(sem("split_stored"), 16)
                sp.wait_ge(sem("split_stored"), at("split_stored", b, ph.c.per["split_stored"]))
                for g in range(NG):
                    if el.ph is None:
                        sp.wait_ge(sem("packs_set"), 2)
                        stream_ready(sp, before(ph))
                    else:
                        sp.wait_ge(sem("scores_full"), el.ph.c.at("scores_full", el.b, 2 * el.ph.nt * (g + 1)))
                    sp.dma_start(KP[g][0:R9, 0:G * ph.nk], kscr[:, G * g:G * g + G, :].rearrange(
                        "r h k -> r (h k)").unsqueeze(0).to_broadcast([3, 3 * HD, G * ph.nk])).then_inc(
                        sem("packed_loaded%d" % g), 16)
                    for a in range(3):
                        sp.dma_start(QP[g][24 * a:24 * a + 24, :], scr_q[a, :, G * g:G * g + G, :].rearrange(
                            "d h q -> d (h q)").unsqueeze(0).to_broadcast([3, HD, G * N])).then_inc(
                            sem("packed_loaded%d" % g), 16)

            sp.wait_ge(sem("cleared"), 1)
            for ph in plan:
                if isinstance(ph, Phase):
                    if ph.el["before"]:
                        prepare(ph.el["before"])
                    prepare(ph.el["first"])
                    with sp.Fori(1, B - 1) as i:
                        prepare(ph.el["middle"](i))
                    if ph.el["last"].nxt:
                        prepare(ph.el["last"])
                    if ph.name == "c2" and "l3" in phases:
                        stream_ready(sp, ph)
                        sp.dma_start(W3A, w3[:, 0:SPLIT3]).then_inc(sem("last_weights"), 16)
                        sp.dma_start(W3B, w3[:, SPLIT3:NW3]).then_inc(sem("last_weights"), 16)
                elif isinstance(ph, LastPhase):
                    last_sync(sp, ph)
            if not isinstance(plan[-1], LastPhase):
                stream_ready(sp, plan[-1])
                sp.dma_start(outT, X[:, :]).then_inc(sem("out_stored"), 16)
                sp.wait_ge(sem("out_stored"), 16)

        @block.tensor
        def _(pe):
            pe.wait_ge(sem("wmod_loaded"), 16)
            pe.wait_ge(sem("cond_done"), 1)
            for k in range(NMOD):
                last = nc.tensor.matmul(MISC[:, k * B:(k + 1) * B], WM[:, k * D:(k + 1) * D], CND[:, 2 * B:3 * B],
                                        start=True, stop=True)
            last.then_inc(sem("mod_full"), 1)
            pe.wait_ge(sem("weights_loaded"), 16)
            pe.wait_ge(sem("x_loaded"), 16)
            pe.wait_ge(sem("mod_done"), 1)
            pe.wait_ge(sem("cleared"), 1)

            def piece(el, role, name):
                if name in NO_BANK:
                    return
                ph, b = el.owner(role)
                at, use = ph.c.at, el.use(role, name)
                wait(pe, "misc_free", use)
                if name == "mean":
                    if ph.before and ph.before.gate is not None:
                        pe.wait_ge(sem("stream_done"), ph.before.c.at("stream_done", b, 1))
                    last = nc.tensor.matmul(MISC[:, 0:N], w("mean"), xcols(b), start=True, stop=True)
                elif name == "var":
                    pe.wait_ge(sem("squared"), at("squared", b, 1))
                    last = nc.tensor.matmul(MISC[:, 0:N], w("mean"), SQ[:, 0:N], start=True, stop=True)
                elif name == "q":
                    done = "normed" if ph.mod else "unit_done"
                    pe.wait_ge(sem(done), at(done, b, 1))
                    last = nc.tensor.matmul(MISC[:, 0:N], w(ph.name + "wq"), XM[:, 0:N], start=True, stop=True)
                    if not ph.cross:
                        last = nc.tensor.matmul(MISC[:, N:2 * N], w(ph.name + "wk"), XM[:, 0:N], start=True, stop=True)
                elif name[0] == "t":
                    j = int(name[1])
                    pe.wait_ge(sem("ctx_normed"), at("ctx_normed", b, 1))
                    for k, t in enumerate(range(4 * j, min(4 * j + 4, ph.nt))):
                        last = nc.tensor.transpose(MISC[:, k * 128:(k + 1) * 128], CN[:, t, :], w("ident"))
                elif name[0] == "k":
                    c0, n = CHUNKS[int(name[1])]
                    if ph.raw:
                        pe.wait_ge(sem("ctx_loaded"), at("ctx_loaded", b, 16))
                    last = nc.tensor.matmul(MISC[:, 0:n], w(ph.name + "wk"), CT[:, c0:c0 + n], start=True, stop=True)
                elif name[0] == "v":
                    src = CT if ph.cross else XM
                    for k, t in enumerate(range(4 * int(name[1]), min(4 * int(name[1]) + 4, ph.nt))):
                        kt = ph.tiles[t]
                        last = nc.tensor.matmul(MISC[0:kt, k * D:(k + 1) * D], src[:, t * 128:t * 128 + kt],
                                                w(ph.name + "wv"), start=True, stop=True)
                elif name == "d":
                    pe.wait_ge(sem("heads_copied"), at("heads_copied", b, NG))
                    for g in range(NG):
                        for qt in range(2):
                            c = (2 * g + qt) * G
                            last = nc.tensor.matmul(MISC[:, c:c + G], RS[g][:, qt * 128:(qt + 1) * 128], w("pick"),
                                                    start=True, stop=True)
                elif name[0] == "e":
                    pe.wait_ge(sem("inverse_ready"), at("inverse_ready", b, 1))
                    for k in range(4):
                        c = (4 * int(name[1]) + k) * 128
                        last = nc.tensor.matmul(MISC[:, k * 128:(k + 1) * 128], RDX[:, c:c + 128], w("ident"),
                                                start=True, stop=True)
                elif name == "y":
                    pe.wait_ge(sem("group_done"), at("group_done", b, NG))
                    for g in range(NG):
                        last = nc.tensor.matmul(MISC[:, 0:N], w(ph.name + "wp", g * D, D), ON[g][:, :],
                                                start=(g == 0), stop=(g == NG - 1))
                last.then_inc(sem("misc_full"), 1)

            def scores(ph, b, g, t, half):
                at, kt = ph.c.at, ph.tiles[t]
                if t == 0:
                    pe.wait_ge(sem("rows_done"), at("rows_done", b, 2 * g + half + 1))
                pe.wait_ge(sem("probs_full"), at("probs_full", b, 2 * (g * ph.nt + t) + half - 1))
                for k in range(2):
                    h = 2 * half + k
                    c0 = h * ph.nk + t * 128
                    last = nc.tensor.matmul(SC[half][0:kt, k * N:(k + 1) * N], KP[g][:, c0:c0 + kt],
                                            QP[g][:, h * N:(h + 1) * N], start=True, stop=True)
                last.then_inc(sem("scores_full"), 1)

            def maximum(ph, b, g, j):
                at = ph.c.at
                if j == 0:
                    pe.wait_ge(sem("packed_loaded%d" % g), at("packed_loaded%d" % g, b, 64))
                elif j < 3:
                    wait(pe, "rows_done", at("rows_done", b, 2 * g + j - 2))
                if j >= len(MB):
                    pe.wait_ge(sem("max_done"), at("max_done", b, g * ph.nm + j - len(MB) + 1))
                dst = MB[j % len(MB)]
                if ph.cross:
                    r, c = j // len(CHUNKS), j % len(CHUNKS)
                    h, qt, (c0, n) = r // 2, r % 2, CHUNKS[c]
                    last = nc.tensor.matmul(dst[:, 0:n], QP[g][0:MR, h * N + qt * 128:h * N + qt * 128 + 128],
                                            KP[g][0:MR, h * ph.nk + c0:h * ph.nk + c0 + n], start=True, stop=True)
                else:
                    for qt in range(2):
                        last = nc.tensor.matmul(dst[:, qt * N:(qt + 1) * N],
                                                QP[g][0:MR, j * N + qt * 128:j * N + qt * 128 + 128],
                                                KP[g][0:MR, j * ph.nk:(j + 1) * ph.nk], start=True, stop=True)
                last.then_inc(sem("max_full"), 1)

            def shift_rows(ph, b, g):
                pe.wait_ge(sem("shift_ready"), ph.c.at("shift_ready", b, g + 1))
                for half in range(2):
                    dst = MB[1 + half]
                    for r in range(4):
                        last = nc.tensor.matmul(dst[MR:MR + 2, r * 128:(r + 1) * 128], NMB[g % 2][:, 4 * half + r, :],
                                                IDB[:, :], start=True, stop=True)
                    last.then_inc(sem("rows_full"), 1)

            def head_values(ph, b, g, t):
                at, kt = ph.c.at, ph.tiles[t]
                if t == 0:
                    pe.wait_ge(sem("values_packed"), at("values_packed", b, g + 1))
                    pe.wait_ge(sem("heads_copied"), at("heads_copied", b, g - 1))
                pe.wait_ge(sem("probs_full"), at("probs_full", b, 2 * (g * ph.nt + t + 1)))
                for h in range(G):
                    last = nc.tensor.matmul(OB[g % 2][32 * h:32 * h + HD + 1, 0:N], VA[g % 2][0:kt, t, h, :],
                                            P[(g * ph.nt + t) % 2][0:kt, h * N:(h + 1) * N],
                                            start=(t == 0), stop=(t == ph.nt - 1))
                last.then_inc(sem("pv_done"), 1)

            def element(el):
                ph, b = el.ph, el.b
                last_tile = (el.prev[0], el.prev[1], NG - 1, el.prev[0].nt - 1) if el.prev else None
                for g in range(NG):
                    ahead = (ph, b, g + 1) if g + 1 < NG else (*el.nxt, 0) if el.nxt else None
                    for t in range(ph.nt):
                        js = ahead[0].maximum_at((t, ph.nt)) if ahead else []
                        third = -(-len(js) // 3)
                        among, behind = el.here(g * ph.nt + t)
                        scores(ph, b, g, t, 0)
                        for j in js[:third]:
                            maximum(*ahead, j)
                        for piece_ in among:
                            piece(el, *piece_)
                        scores(ph, b, g, t, 1)
                        for j in js[third:2 * third]:
                            maximum(*ahead, j)
                        if last_tile:
                            head_values(*last_tile)
                        last_tile = (ph, b, g, t)
                        for j in js[2 * third:]:
                            maximum(*ahead, j)
                        if ahead and t == ph.shift_tile:
                            shift_rows(*ahead)
                        for piece_ in behind:
                            piece(el, *piece_)

            for ph in plan:
                if isinstance(ph, Phase):
                    if ph.el["before"]:
                        stream_ready(pe, before(ph))
                        for piece_ in sum(ph.el["before"].here(0), []):
                            piece(ph.el["before"], *piece_)
                        pe.wait_ge(sem("packs_set"), 2)
                        for j in range(ph.nm):
                            maximum(ph, 0, 0, j)
                        shift_rows(ph, 0, 0)
                    if ph is plan[0]:
                        pe.wait_ge(sem("rest_loaded"), 32)
                        for k, a in enumerate(ATT):
                            for g in range(NG):
                                last = nc.tensor.matmul(bank[0][:, k:k + 1], w(a + "wp", g * D, D),
                                                        w(a + "bv", g, 1), start=(g == 0), stop=(g == NG - 1))
                        last.then_inc(sem("bias_full"), 1)
                        pe.wait_ge(sem("bias_done"), 1)
                    element(ph.el["first"])
                    with pe.Fori(1, B - 1) as i:
                        element(ph.el["middle"](i))
                    element(ph.el["last"])
                    if ph.el["after"]:
                        head_values(ph, B - 1, NG - 1, ph.nt - 1)
                        for piece_ in sum(ph.el["after"].here(0), []):
                            piece(ph.el["after"], *piece_)
                elif isinstance(ph, MlpPhase):
                    mlp_tensor(pe, ph)
                else:
                    last_tensor(pe, ph)

        @block.scalar
        def _(act):
            nc.scalar.preload_act_table_set(LN_EXP)
            act.wait_ge(sem("wmod_loaded"), 16)
            nc.scalar.activation(CND[:, 0:B], WM[:, NMOD * (D + 1):NWM], ACT.Exp, scale=-1.0).then_inc(
                sem("cond_exp"), 1)
            act.wait_ge(sem("weights_loaded"), 16)

            def piece(el, role, name):
                ph, b = el.owner(role)
                at = ph.c.at
                use = None if name in NO_BANK else el.use(role, name)
                if name == "square":
                    act.wait_ge(sem("misc_free"), el.use(role, "mean") + 1)
                    nc.scalar.activation(SQ[:, 0:N], XC[:, 0:N], ACT.Square).then_inc(sem("squared"), 1)
                elif name == "var":
                    act.wait_ge(sem("misc_full"), use + 1)
                    nc.scalar.activation(LG[:, 0:N], MISC[:, 0:N], ACT.Ln, bias=w(ph.eps)).then_inc(sem("misc_free"), 1)
                    act.wait_ge(sem("misc_free"), use + 1)
                    nc.scalar.activation(RSTD[:, 0:N], LG[:, 0:N], ACT.Exp, scale=-0.5).then_inc(sem("rstd_done"), 1)
                elif name == "ctx_scale":
                    act.wait_ge(sem("stats_done"), at("stats_done", b, 1))
                    nc.scalar.activation(CL[:, :], MV[:, :, 1], ACT.Ln, bias=w(ph.eps)).then_inc(sem("ctx_log"), 1)
                    act.wait_ge(sem("ctx_log"), at("ctx_log", b, 1))
                    nc.scalar.activation(CR[:, :], CL[:, :], ACT.Exp, scale=-0.5).then_inc(sem("ctx_rstd"), 1)
                elif name == "q" or name[0] == "k":
                    act.wait_ge(sem("misc_full"), use + 1)
                    if name == "q":
                        wait(act, "split_stored", at("split_stored", b, 0))
                        units = [("bq", 0, 0, N, QS[:, 0, :])]
                        if not ph.cross:
                            units.append(("bk", N, N, N, KS[:, 0, 0:N]))
                    else:
                        c0, n = CHUNKS[int(name[1])]
                        units = [("bk", 0, N + c0, n, KS[:, 0, c0:c0 + n])]
                    for bias, c, r, n, high in units:
                        nc.scalar.activation(high, MISC[:, c:c + n], ACT.Identity, bias=w(ph.name + bias))
                        last = nc.scalar.activation(REST[:, r:r + n], MISC[:, c:c + n], ACT.Identity,
                                                    bias=w(ph.name + bias))
                    last.then_inc(sem("misc_free"), 1)
                elif name[0] == "t":
                    j = int(name[1])
                    n = 128 * min(4, ph.nt - 4 * j)
                    act.wait_ge(sem("misc_full"), use + 1)
                    if ph.kvmod:
                        last = nc.scalar.activation(CT[:, 512 * j:512 * j + n], MISC[:, 0:n], ACT.Identity,
                                                    bias=KVM[:, 1:2], scale=KVM[:, 0:1])
                    else:
                        last = nc.scalar.copy(CT[:, 512 * j:512 * j + n], MISC[:, 0:n])
                    last.then_inc(sem("misc_free"), 1)
                elif name[0] == "v":
                    j = int(name[1])
                    t0, n = 4 * j, min(4, ph.nt - 4 * j)
                    kt = ph.tiles[t0]
                    act.wait_ge(sem("misc_full"), use + 1)
                    if j == 0:
                        wait(act, "values_packed", at("values_packed", b, 0))
                    nc.scalar.copy(VN[0:kt, t0:t0 + n, :],
                                   MISC[0:kt, 0:n * D].rearrange("p (t d) -> p t d", d=D)).then_inc(
                        sem("misc_free"), 1)

            def exponentials(ph, b, g, t, half):
                at, kt, v = ph.c.at, ph.tiles[t], g * ph.nt + t
                act.wait_ge(sem("scores_full"), at("scores_full", b, 2 * v + half + 1))
                if half == 0:
                    act.wait_ge(sem("pv_done"), at("pv_done", b, v - 1))
                nc.scalar.activation(P[v % 2][0:kt, half * 2 * N:(half + 1) * 2 * N], SC[half][0:kt, :], ACT.Exp,
                                     scale=SCALE).then_inc(sem("probs_full"), 1)

            def copy_heads(ph, b, g):
                at = ph.c.at
                act.wait_ge(sem("pv_done"), at("pv_done", b, (g + 1) * ph.nt))
                wait(act, "group_done", at("group_done", b, g + 1 - NG))
                nc.scalar.copy(RS[g][:, :], OB[g % 2][:, 0:N]).then_inc(sem("heads_copied"), 1)

            def copy_rows(ph, b, g):
                for half in range(2):
                    act.wait_ge(sem("rows_full"), ph.c.at("rows_full", b, 2 * g + half + 1))
                    nc.scalar.copy(QP[g][MR:MR + 2, half * 2 * N:(half + 1) * 2 * N],
                                   MB[1 + half][MR:MR + 2, :]).then_inc(sem("rows_done"), 1)

            def element(el):
                ph, b = el.ph, el.b
                for g in range(NG):
                    ahead = (ph, b, g + 1) if g + 1 < NG else (*el.nxt, 0) if el.nxt else None
                    for t in range(ph.nt):
                        among, behind = el.here(g * ph.nt + t)
                        exponentials(ph, b, g, t, 0)
                        if not ph.cross:
                            for piece_ in among:
                                piece(el, *piece_)
                        exponentials(ph, b, g, t, 1)
                        if ph.cross:
                            for piece_ in among:
                                piece(el, *piece_)
                        if t == (1 if ph.cross else 0) and g:
                            copy_heads(ph, b, g - 1)
                        elif t == (1 if ph.cross else 0) and el.prev:
                            copy_heads(*el.prev, NG - 1)
                        if ahead and t == ph.shift_tile:
                            copy_rows(*ahead)
                        for piece_ in behind:
                            piece(el, *piece_)

            for ph in plan:
                if isinstance(ph, Phase):
                    if ph.el["before"]:
                        for piece_ in sum(ph.el["before"].here(0), []):
                            piece(ph.el["before"], *piece_)
                        act.wait_ge(sem("packs_set"), 2)
                        copy_rows(ph, 0, 0)
                    element(ph.el["first"])
                    with act.Fori(1, B - 1) as i:
                        element(ph.el["middle"](i))
                    element(ph.el["last"])
                    if ph.el["after"]:
                        copy_heads(ph, B - 1, NG - 1)
                elif isinstance(ph, MlpPhase):
                    mlp_scalar(act, ph)
                else:
                    last_scalar(act, ph)

        @block.vector
        def _(dve):
            nc.vector.memset(CN[:, FULL, :], 0.0)
            for k in range(2):
                nc.vector.memset(VA[k][:, :, :, :], 1.0)
            nc.vector.memset(VN[:, FULL, :], 0.0)
            for k in range(2):
                last = nc.vector.memset(OB[k][:, :], 0.0)
            last.then_inc(sem("cleared"), 1)
            for name in ("probs_full", "pv_done", "heads_copied"):
                dve.sem_inc(sem(name), 2)
            for name in ("mlp_centered", "mlp_gated", "l_centered"):
                dve.sem_inc(sem(name), 1)
            dve.wait_ge(sem("cond_exp"), 1)
            nc.vector.tensor_scalar_add(CND[:, B:2 * B], CND[:, 0:B], 1.0).then_inc(sem("cond_step"), 1)
            dve.wait_ge(sem("cond_step"), 1)
            nc.vector.reciprocal(CND[:, 0:B], CND[:, B:2 * B]).then_inc(sem("cond_step"), 1)
            dve.wait_ge(sem("cond_step"), 2)
            nc.vector.tensor_tensor(CND[:, 2 * B:3 * B], CND[:, 0:B], WM[:, NMOD * (D + 1):NWM], ALU.mult).then_inc(
                sem("cond_done"), 1)
            for g in range(2):
                last = nc.vector.memset(KP[g][:, :], 0.0)
            last.then_inc(sem("keys_cleared"), 1)
            dve.wait_ge(sem("keys_cleared"), 1)
            for g in range(2):
                last = nc.vector.memset(KP[g][MR:MR + 2, :], 1.0)
            last.then_inc(sem("packs_set"), 1)
            dve.wait_ge(sem("weights_loaded"), 16)
            nc.vector.tensor_copy(IDB[:, :], w("ident"))
            dve.wait_ge(sem("mod_full"), 1)
            nc.vector.tensor_tensor(MODT[:, :].rearrange("p (k b) -> p k b", b=B),
                                    MISC[:, 0:NMOD * B].rearrange("p (k b) -> p k b", b=B),
                                    WM[:, NMOD * D:NMOD * (D + 1)].unsqueeze(2).to_broadcast([D, NMOD, B]),
                                    ALU.add).then_inc(sem("cond_step"), 1)
            dve.wait_ge(sem("cond_step"), 3)
            for k in MOD_SCALES:
                last = nc.vector.tensor_scalar_add(MODT[:, k * B:(k + 1) * B], MODT[:, k * B:(k + 1) * B], 1.0)
            last.then_inc(sem("mod_done"), 1)
            dve.wait_ge(sem("mod_done"), 1)
            dve.wait_ge(sem("x_loaded"), 16)

            def piece(el, role, name):
                ph, b = el.owner(role)
                at = ph.c.at
                use = None if name in NO_BANK else el.use(role, name)
                if name == "mean":
                    dve.wait_ge(sem("misc_full"), use + 1)
                    nc.vector.tensor_tensor(XC[:, 0:N], xcols(b), MISC[:, 0:N], ALU.subtract).then_inc(
                        sem("misc_free"), 1)
                elif name == "norm":
                    dve.wait_ge(sem("rstd_done"), at("rstd_done", b, 1))
                    dst = XN if ph.mod else XM
                    nc.vector.tensor_tensor(dst[:, 0:N], XC[:, 0:N], RSTD[:, 0:N], ALU.mult).then_inc(
                        sem("unit_done"), 1)
                    if ph.mod:
                        dve.wait_ge(sem("unit_done"), at("unit_done", b, 1))
                        nc.vector.tensor_scalar(XM[:, 0:N], XN[:, 0:N], modcol(ph.mod[0], b), modcol(ph.mod[1], b),
                                                ALU.mult, ALU.add).then_inc(sem("normed"), 1)
                elif name[:5] == "stats":
                    t = int(name[5:])
                    if t == 0:
                        dve.wait_ge(sem("ctx_loaded"), at("ctx_loaded", b, 32))
                    nc.vector.bn_stats(ST[:, t, :], CN[:, t, :]).then_inc(sem("stats_read"), 1)
                    wait_apart(dve, "stats_read", at("stats_read", b, t + 1))
                    last = nc.vector.bn_aggr(MV[:, t, :], ST[:, t, :])
                    if t == FULL:
                        last.then_inc(sem("stats_done"), 1)
                elif name == "ctx_norm":
                    dve.wait_ge(sem("ctx_rstd"), at("ctx_rstd", b, 1))
                    if ph.kvmod:
                        nc.vector.tensor_scalar(KVM[:, :].unsqueeze(2),
                                                MODT[:, :].rearrange("p (k b) -> p k b", b=B)[
                                                    :, ph.kvmod[0]:ph.kvmod[0] + 2, ds(b, 1)],
                                                1.0, None, ALU.mult)
                    nc.vector.scalar_tensor_tensor(out=CO[:, :], in0=MV[:, :, 0], scalar=-1.0, in1=CR[:, :],
                                                   op0=ALU.mult, op1=ALU.mult).then_inc(sem("ctx_offset"), 1)
                elif name == "d":
                    dve.wait_ge(sem("misc_full"), use + 1)
                    nc.vector.reciprocal(RDN[:, :], MISC[:, 0:2 * H]).then_inc(sem("misc_free"), 1)
                    dve.wait_ge(sem("misc_free"), use + 1)
                    nc.vector.tensor_scalar(RDX[:, :].rearrange("p (h r) -> p h r", r=32),
                                            RDN[:, :].unsqueeze(2).to_broadcast([128, 2 * H, 32]), 1.0, None,
                                            ALU.mult).then_inc(sem("inverse_ready"), 1)
                elif name[0] == "e":
                    dve.wait_ge(sem("misc_full"), use + 1)
                    for k in range(2):
                        g = 2 * int(name[1]) + k
                        last = nc.vector.tensor_tensor(ON[g][:, :], RS[g][:, :], MISC[:, k * N:(k + 1) * N], ALU.mult)
                    last.then_inc(sem("misc_free"), 1)
                    dve.wait_ge(sem("misc_free"), use + 1)
                    dve.sem_inc(sem("group_done"), 2)
                elif name == "y":
                    bias = BPT[:, ph.layer:ph.layer + 1]
                    dve.wait_ge(sem("misc_full"), use + 1)
                    if ph.gate is None:
                        nc.vector.scalar_tensor_tensor(out=xcols(b), in0=MISC[:, 0:N], scalar=bias,
                                                       in1=xcols(b), op0=ALU.add, op1=ALU.add).then_inc(
                            sem("misc_free"), 1)
                    else:
                        nc.vector.tensor_scalar(XU[:, :], MISC[:, 0:N], bias, modcol(ph.gate, b),
                                                ALU.add, ALU.mult).then_inc(sem("misc_free"), 1)
                        dve.wait_ge(sem("misc_free"), use + 1)
                        nc.vector.tensor_tensor(xcols(b), xcols(b), XU[:, :], ALU.add).then_inc(
                            sem("stream_done"), 1)

            def maximum(ph, b, g, j):
                at = ph.c.at
                dve.wait_ge(sem("max_full"), at("max_full", b, g * ph.nm + j + 1))
                src = MB[j % len(MB)]
                if ph.cross:
                    r, c = j // len(CHUNKS), j % len(CHUNKS)
                    nc.vector.tensor_reduce(MX[:, r, c:c + 1], src[:, 0:CHUNKS[c][1]], AX.X, ALU.max).then_inc(
                        sem("max_done"), 1)
                else:
                    nc.vector.tensor_reduce(MX[:, 2 * j:2 * j + 2, 0], src[:, :].rearrange("p (t k) -> p t k", t=2),
                                            AX.X, ALU.max).then_inc(sem("max_done"), 1)

            def shifts(ph, b, g):
                at = ph.c.at
                dve.wait_ge(sem("max_done"), at("max_done", b, (g + 1) * ph.nm))
                parts = MX[:, :, :] if ph.cross else MX[:, :, 0:1]
                nc.vector.tensor_reduce(NMF[:, :], parts, AX.X, ALU.max, negate=True).then_inc(sem("shift_step"), 1)
                dve.wait_ge(sem("shift_step"), at("shift_step", b, 2 * g + 1))
                nc.vector.tensor_copy(NMB[g % 2][:, :, 0], NMF[:, :]).then_inc(sem("shift_step"), 1)
                dve.wait_ge(sem("shift_step"), at("shift_step", b, 2 * g + 2))
                nc.vector.tensor_tensor(NMB[g % 2][:, :, 1], NMF[:, :], NMB[g % 2][:, :, 0], ALU.subtract).then_inc(
                    sem("shift_ready"), 1)

            def element(el):
                ph, b = el.ph, el.b
                for g in range(NG):
                    ahead = (ph, b, g + 1) if g + 1 < NG else (*el.nxt, 0) if el.nxt else None
                    for t in range(ph.nt):
                        among, behind = el.here(g * ph.nt + t)
                        mine = ahead[0].maximum_at((t, ph.nt)) if ahead else []
                        third = -(-len(mine) // 3)
                        for j in mine[:third]:
                            maximum(*ahead, j)
                        if not ph.cross:
                            for piece_ in among:
                                piece(el, *piece_)
                        for j in mine[third:]:
                            maximum(*ahead, j)
                        if mine and mine[-1] == ahead[0].nm - 1:
                            shifts(*ahead)
                        for piece_ in (among if ph.cross else []) + behind:
                            piece(el, *piece_)

            for ph in plan:
                if isinstance(ph, Phase):
                    if ph.el["before"]:
                        for piece_ in sum(ph.el["before"].here(0), []):
                            piece(ph.el["before"], *piece_)
                        for j in range(ph.nm):
                            maximum(ph, 0, 0, j)
                        shifts(ph, 0, 0)
                    if ph is plan[0]:
                        dve.wait_ge(sem("bias_full"), 1)
                        for k, a in enumerate(ATT):
                            last = nc.vector.tensor_tensor(BPT[:, k:k + 1], bank[0][:, k:k + 1], w(a + "bp"), ALU.add)
                        last.then_inc(sem("bias_done"), 1)
                        dve.wait_ge(sem("bias_done"), 1)
                    element(ph.el["first"])
                    with dve.Fori(1, B - 1) as i:
                        element(ph.el["middle"](i))
                    element(ph.el["last"])
                    if ph.el["after"]:
                        for piece_ in sum(ph.el["after"].here(0), []):
                            piece(ph.el["after"], *piece_)
                elif isinstance(ph, MlpPhase):
                    mlp_vector(dve, ph)
                else:
                    last_vector(dve, ph)

        @block.gpsimd
        def _(pool):
            for g in range(NG):
                last = nc.gpsimd.memset(QP[g][:, :], 0.0)
                if g >= 2:
                    last = nc.gpsimd.memset(KP[g][:, :], 0.0)
            last.then_inc(sem("packs_cleared"), 1)
            pool.wait_ge(sem("packs_cleared"), 1)
            for g in range(2, NG):
                last = nc.gpsimd.memset(KP[g][MR:MR + 2, :], 1.0)
            last.then_inc(sem("ones_set"), 1)
            pool.wait_ge(sem("ones_set"), 1)
            pool.sem_inc(sem("packs_set"), 1)
            pool.wait_ge(sem("cleared"), 1)

            def piece(el, role, name):
                if role != "prep":
                    return
                ph, b = el.nxt
                at = ph.c.at
                if name == "ctx_norm":
                    wait_apart(pool, "ctx_offset", at("ctx_offset", b, 1))
                    for t in range(ph.nt):
                        last = nc.gpsimd.tensor_scalar(CN[:, t, :], CN[:, t, :], CR[:, t:t + 1], CO[:, t:t + 1],
                                                       ALU.mult, ALU.add)
                    last.then_inc(sem("ctx_normed"), 1)
                elif name == "q" or name[0] == "k":
                    units = [(QS, 0, N, 0)] if name == "q" else []
                    if name == "q" and not ph.cross:
                        units.append((KS, 0, N, N))
                    if name[0] == "k":
                        c0, n = CHUNKS[int(name[1])]
                        units.append((KS, c0, n, N + c0))
                    first = 0 if name == "q" else 1 + int(name[1])
                    pool.wait_ge(sem("misc_free"), el.use(role, name) + 1)
                    for k, (dst, c, n, r) in enumerate(units):
                        rest = REST[:, r:r + n]
                        nc.gpsimd.tensor_tensor(rest, rest, dst[:, 0, c:c + n], ALU.subtract).then_inc(
                            sem("rest_done"), 1)
                        wait_apart(pool, "rest_done", at("rest_done", b, first + k + 1))
                        nc.gpsimd.tensor_copy(dst[:, 1, c:c + n], rest).then_inc(sem("mid_done"), 1)
                        pool.wait_ge(sem("mid_done"), at("mid_done", b, first + k + 1))
                        nc.gpsimd.tensor_tensor(dst[:, 2, c:c + n], rest, dst[:, 1, c:c + n],
                                                ALU.subtract).then_inc(sem("low_done"), 1)

            def pack_values(prev, ph, b, g, el):
                at = ph.c.at
                if g == 0:
                    pool.wait_ge(sem("misc_free"), el.use("prep", "v3" if ph.cross else "v0") + 1)
                if g >= 2:
                    wait_apart(pool, "pv_done", at("pv_done", b, (g - 1) * ph.nt))
                elif prev:
                    wait_apart(pool, "pv_done", prev[0].c.at("pv_done", prev[1], (g + 3) * prev[0].nt))
                else:
                    stream_ready(pool, before(ph))
                nc.gpsimd.tensor_copy(
                    VA[g % 2][:, 0:ph.nt, :, 0:HD],
                    VN[:, 0:ph.nt, G * HD * g:G * HD * (g + 1)].rearrange("p t (h d) -> p t h d", d=HD)).then_inc(
                    sem("values_packed"), 1)

            def element(el):
                ph, b = el.ph, el.b
                for g in range(NG):
                    for t in range(ph.nt):
                        for piece_ in sum(el.here(g * ph.nt + t), []):
                            piece(el, *piece_)
                        if g < NG - 1 and t == 1:
                            pack_values(el.prev, ph, b, g + 1, el)
                if el.nxt:
                    pack_values((ph, b), *el.nxt, 0, el)

            for ph in plan:
                if isinstance(ph, Phase):
                    if ph.el["before"]:
                        for piece_ in sum(ph.el["before"].here(0), []):
                            piece(ph.el["before"], *piece_)
                        pack_values(None, ph, 0, 0, ph.el["before"])
                    element(ph.el["first"])
                    with pool.Fori(1, B - 1) as i:
                        element(ph.el["middle"](i))
                    element(ph.el["last"])


def lay_out(a):
    f = np.float32

    def dh(m):
        return m.reshape(m.shape[:-1] + (H, HD)).swapaxes(-1, -2).reshape(m.shape)

    def col(v):
        return v.reshape(-1, D).T

    def row(v):
        return np.broadcast_to(v, (D, v.size))

    def strips(m):
        p = np.zeros((4, 32, NG, m.shape[1]), f)
        p[:, :HD] = m.reshape(NG, 4, HD, -1).transpose(1, 2, 0, 3)
        return p.reshape(128, -1)

    k = np.arange(128)
    main = {"mean": np.full((D, D), 1.0 / D, f), "ident": np.eye(D, dtype=f),
            "pick": (k[:, None] == 32 * np.arange(G)[None, :] + HD).astype(f),
            "eps5": np.full((D, 1), 1e-5, f), "eps6": np.full((D, 1), 1e-6, f), "one": np.ones((D, 1), f)}

    def attention(n, wq, bq, wk, bk, wv, bv, wp, bp):
        main.update({n + "wq": dh(wq), n + "wk": dh(wk), n + "wv": wv, n + "wp": strips(wp), n + "bv": strips(bv[:, None]),
                     n + "bq": col(dh(bq)), n + "bk": col(dh(bk)), n + "bp": col(bp)})

    l0, l1, l2, l3 = ({k[len(p):]: v for k, v in a.items() if k.startswith(p)}
                      for p in ("L0_xcond_", "L1_xcond_", "L2_xcond_", "L3_xcond_"))
    attention("a0", l0["Wq"], l0["bq"], l0["Wkv"][:, :D], l0["bkv"][:D], l0["Wkv"][:, D:], l0["bkv"][D:], l0["Wp"],
              l0["bp"])
    for n, wqkv, bqkv, wp, bp in (("s1", l1["qkv_w"], l1["qkv_b"], l1["sa_proj_w"], l1["sa_proj_b"]),
                                  ("s2", l2["W_qkv"], l2["b_qkv"], l2["W_proj"], l2["b_proj"])):
        attention(n, wqkv[:, :D], bqkv[:D], wqkv[:, D:2 * D], bqkv[D:2 * D], wqkv[:, 2 * D:], bqkv[2 * D:], wp, bp)
    for n, wq, bq, wkv, bkv, wp, bp in (
            ("c1", l1["q_w"], l1["q_b"], l1["kv_w"], l1["kv_b"], l1["ca_proj_w"], l1["ca_proj_b"]),
            ("c2", l2["W_qc"], l2["b_qc"], l2["W_kvc"], l2["b_kvc"], l2["W_cproj"], l2["b_cproj"])):
        attention(n, wq, bq, wkv[:, :D], bkv[:D], wkv[:, D:], bkv[D:], wp, bp)
    for n, w1, b1, w2, b2 in (("m1", l1["fc1_w"], l1["fc1_b"], l1["fc2_w"], l1["fc2_b"]),
                              ("m2", l2["W_mlp1"], l2["b_mlp1"], l2["W_mlp2"], l2["b_mlp2"])):
        main.update({n + "w1": w1, n + "w2": w2.reshape(4, D, D).transpose(1, 0, 2).reshape(D, 4 * D),
                     n + "b1": col(b1), n + "b2": col(b2)})
    thirds = (3, D)
    last = {"wq": l3["Wq"], "wkT": l3["Wk"].T, "wv": l3["Wv"],
            "rw": l3["router_W"].reshape(3, D, E3).transpose(1, 0, 2),
            "ew1": l3["e_w1"].reshape((E3,) + thirds + (2, D)).transpose(2, 1, 0, 3, 4),
            "ew2": l3["e_w2"].reshape(E3, 2, D, D).transpose(2, 0, 1, 3),
            "gw1": l3["gate_w1"].reshape(thirds + (D,)).transpose(1, 0, 2), "gw2": l3["gate_w2"],
            "ow": l3["out_w"], "gamma": col(l3["ln_gamma"]), "beta": col(l3["ln_beta"]), "rb": row(l3["router_b"]),
            "eb1": col(l3["e_b1"]), "eb2": col(l3["e_b2"]), "gb1": col(l3["gate_b1"]), "gb2": col(l3["gate_b2"]),
            "ob": col(l3["out_b"])}
    wm = [l0["Wss_q"], l0["Wss_kv"], l1["adaln_w"], l2["W_mod"]]
    bm = [l0["bss_q"], l0["bss_kv"], l1["adaln_b"], l2["b_mod"]]
    return {
        "x_t": np.ascontiguousarray(a["x"].transpose(2, 0, 1).reshape(D, B * N)),
        "ctx_n": np.ascontiguousarray(a["ctx_1024"]),
        "ctx_t": np.ascontiguousarray(a["ctx_1024"].transpose(0, 2, 1)),
        "w_mod": np.concatenate(wm + [col(b) for b in bm] + [a["cond_1024"].T], axis=1),
        "w_main": np.concatenate([main[n].reshape(D, -1) for n in COLS], axis=1),
        "w_last": np.concatenate([last[n].reshape(D, -1) for n in COLS3], axis=1),
    }


def kernel(**inputs):
    import numpy as _np
    import concourse.bacc as _bacc
    from concourse import mybir as _mybir
    from concourse.bass_utils import run_bass_kernel_spmd as _run

    nc = _bacc.Bacc("TRN2", target_bir_lowering=False, num_devices=1)
    arrays = lay_out({k: _np.asarray(v) for k, v in inputs.items()})
    aps = {n: nc.dram_tensor(n, v.shape, _mybir.dt.from_np(v.dtype), kind="ExternalInput").ap()
           for n, v in arrays.items()}
    out = nc.dram_tensor("out_t", (D, B * N), _mybir.dt.float32, kind="ExternalOutput").ap()
    build(nc, aps["x_t"], aps["ctx_n"], aps["ctx_t"], aps["w_mod"], aps["w_main"], aps["w_last"], out, PHASES)
    r = _run(nc, [arrays], core_ids=[0])
    return _np.ascontiguousarray(r.results[0]["out_t"].reshape(D, B, N).transpose(1, 2, 0))
```
